# Optimizing a Trainium2 kernel written in Bass

```python
import numpy as np
import jax
import jax.numpy as jnp

def _softmax(x, axis=-1):
    return jax.nn.softmax(x, axis=axis)

def _gelu(x):
    return jax.nn.gelu(x, approximate=True)

def _silu(x):
    return jax.nn.silu(x)

def _sigmoid(x):
    return jax.nn.sigmoid(x)

def _layernorm(x, axis=-1, eps=1e-05):
    m = jnp.mean(x, axis=axis, keepdims=True)
    v = jnp.var(x, axis=axis, keepdims=True)
    return (x - m) / jnp.sqrt(v + eps)

def _scatter_add(tgt, idx, src, axis=0):
    return tgt.at[idx].add(src)

def _segment_sum(src, seg, n):
    return jax.ops.segment_sum(src, seg, n)
kernel_name = 'mk_hybrid_d1_jaxref_r8_48e9aa'

def setup_inputs(seed: int=0):
    np.random.seed(seed)
    _w = jnp.asarray

    def _L0_attn_a_setup():
        import jax, jax.numpy as jnp
        import numpy as np
        import math
        B, T, D = (2, 256, 128)
        N_HEADS = 16
        D_HEAD = D // N_HEADS

        def _rope_tables(t, d_head, dtype=jnp.float32):
            theta = 1.0 / 10000.0 ** (jnp.arange(0, d_head, 2, dtype=jnp.float32) / d_head)
            angles = jnp.outer(jnp.arange(t, dtype=jnp.float32), theta)
            angles = jnp.concatenate([angles, angles], axis=-1)
            return (jnp.cos(angles).astype(dtype), jnp.sin(angles).astype(dtype))

        def _rotate_half(x):
            half = x.shape[-1] // 2
            return jnp.concatenate([-x[..., half:], x[..., :half]], axis=-1)

        def _apply_rope(x, cos, sin):
            return x * cos[None, None] + _rotate_half(x) * sin[None, None]
        key = jax.random.key(seed)
        k1, k2, k3, k4 = jax.random.split(key, 4)
        s_in = 1.0 / math.sqrt(D)
        return {'x': jax.random.normal(k1, (B, T, D), dtype=jnp.float32), 'w_qkv': jax.random.normal(k2, (D, 3 * D), dtype=jnp.float32) * s_in, 'w_out': jax.random.normal(k3, (D, D), dtype=jnp.float32) * s_in, 'b_out': jax.random.normal(k4, (D,), dtype=jnp.float32) * 0.01}
    _L0_attn_a_in = _L0_attn_a_setup()

    def _L0_attn_b_setup():
        import jax, jax.numpy as jnp
        import numpy as np
        EMBED_DIM = 128
        NUM_HEADS = 16
        HEAD_DIM = EMBED_DIM // NUM_HEADS
        NUM_FEATS = 32
        YAT_EPS = 0.1
        BATCH = 4
        SEQ = 512

        def _spherical_features(x, projection):
            x_norm = x / (jnp.linalg.norm(x, axis=-1, keepdims=True) + 1e-08)
            proj = jnp.einsum('bhsd,hfd->bhsf', x_norm, projection)
            return jax.nn.relu(proj) + YAT_EPS
        key = jax.random.key(seed)
        ks = jax.random.split(key, 6)
        s = 1.0 / np.sqrt(EMBED_DIM)
        return {'x': jax.random.normal(ks[0], (BATCH, SEQ, EMBED_DIM), jnp.float32), 'Wq': jax.random.normal(ks[1], (EMBED_DIM, EMBED_DIM), jnp.float32) * s, 'bq': jnp.zeros((EMBED_DIM,), jnp.float32), 'Wk': jax.random.normal(ks[2], (EMBED_DIM, EMBED_DIM), jnp.float32) * s, 'bk': jnp.zeros((EMBED_DIM,), jnp.float32), 'Wv': jax.random.normal(ks[3], (EMBED_DIM, EMBED_DIM), jnp.float32) * s, 'bv': jnp.zeros((EMBED_DIM,), jnp.float32), 'Wo': jax.random.normal(ks[4], (EMBED_DIM, EMBED_DIM), jnp.float32) * s, 'bo': jnp.zeros((EMBED_DIM,), jnp.float32), 'projection': jax.random.normal(ks[5], (NUM_HEADS, NUM_FEATS, HEAD_DIM), jnp.float32)}
    _L0_attn_b_in = _L0_attn_b_setup()

    def _L0_ffn_setup():
        import jax, jax.numpy as jnp
        import numpy as np
        DIM = 128
        DEPTH = 6
        HEADS = 16
        DIM_HEAD = 64
        WINDOW = 32
        INNER = HEADS * DIM_HEAD
        DIM_INNER = int(DIM * 4 * 2 / 3)
        QK_SCALE = 8.0

        def shift_tokens(t):
            a, s = jnp.split(t, 2, -1)
            s = jnp.pad(s, ((0, 0), (1, 0), (0, 0)))[:, :-1]
            return jnp.concatenate([a, s], -1)

        def l2norm(t):
            return t / jnp.maximum(jnp.linalg.norm(t, axis=-1, keepdims=True), 1e-12)

        def rotate_half(x):
            x1, x2 = jnp.split(x, 2, -1)
            return jnp.concatenate([-x2, x1], -1)

        def rotary_tables(n):
            half = jnp.arange(0, DIM_HEAD, 2, dtype=jnp.float32)
            inv_freq = 1.0 / 10000.0 ** (half / DIM_HEAD)
            t = jnp.arange(n, dtype=jnp.float32)
            freqs = t[:, None] * inv_freq[None, :]
            freqs = jnp.concatenate([freqs, freqs], -1)
            base_scale = (half + 0.4 * DIM_HEAD) / (1.4 * DIM_HEAD)
            power = (t - n // 2) / (WINDOW // 2)
            scale = base_scale[None, :] ** power[:, None]
            scale = jnp.concatenate([scale, scale], -1)
            return (freqs, scale)

        def local_attention(q, k, v):
            b, h, n, d = q.shape
            w = WINDOW
            nw = n // w
            bq = q.reshape(b, h, nw, w, d)
            bk = k.reshape(b, h, nw, w, d)
            bv = v.reshape(b, h, nw, w, d)

            def look(t):
                p = jnp.pad(t, ((0, 0), (0, 0), (1, 0), (0, 0), (0, 0)))
                return jnp.concatenate([p[:, :, :nw], p[:, :, 1:]], axis=3)
            bk2, bv2 = (look(bk), look(bv))
            seq = jnp.arange(n).reshape(nw, w)
            seq_p = jnp.pad(seq, ((1, 0), (0, 0)), constant_values=-1)
            jt = jnp.concatenate([seq_p[:nw], seq_p[1:]], axis=1)
            it = seq[:, :, None]
            jb = jt[:, None, :]
            mask = (it < jb) | (it > jb + w) | (jb == -1)
            sim = jnp.einsum('bhwie,bhwje->bhwij', bq, bk2) * QK_SCALE
            sim = jnp.where(mask, -jnp.finfo(sim.dtype).max, sim)
            attn = jax.nn.softmax(sim, -1)
            out = jnp.einsum('bhwij,bhwje->bhwie', attn, bv2)
            return out.reshape(b, h, n, d)

        def attn_layer(x, Wqkv, qs, ksc, Wo):
            b, n, _ = x.shape
            qkv = x @ Wqkv
            q, k, v = jnp.split(qkv, 3, -1)
            sh = lambda t: t.reshape(b, n, HEADS, DIM_HEAD).transpose(0, 2, 1, 3)
            q, k, v = (sh(q), sh(k), sh(v))
            q = l2norm(q) * qs
            k = l2norm(k) * ksc
            freqs, scale = rotary_tables(n)
            cos, sin = (jnp.cos(freqs), jnp.sin(freqs))
            q = q * cos * scale + rotate_half(q) * sin * scale
            inv = 1.0 / scale
            k = k * cos * inv + rotate_half(k) * sin * inv
            out = local_attention(q, k, v)
            out = out.transpose(0, 2, 1, 3).reshape(b, n, INNER)
            return out @ Wo

        def ffn_layer(x, g, bln, W1, b1, W2, b2):
            mu = x.mean(-1, keepdims=True)
            var = ((x - mu) ** 2).mean(-1, keepdims=True)
            xn = (x - mu) / jnp.sqrt(var + 1e-05) * g + bln
            hg = xn @ W1 + b1
            a, gate = jnp.split(hg, 2, -1)
            return a * jax.nn.gelu(gate, approximate=False) @ W2 + b2
        key = jax.random.key(seed)
        ks = jax.random.split(key, 8)
        B, N = (2, 256)
        init = lambda k, shape: jax.random.normal(k, shape, jnp.float32) * 0.02
        return {'x': jax.random.normal(ks[0], (B, N, DIM), jnp.float32), 'Wqkv': init(ks[1], (DEPTH, DIM, 3 * INNER)), 'q_scale': jnp.ones((DEPTH, DIM_HEAD), jnp.float32), 'k_scale': jnp.ones((DEPTH, DIM_HEAD), jnp.float32), 'Wo': init(ks[2], (DEPTH, INNER, DIM)), 'ln_g': jnp.ones((DEPTH, DIM), jnp.float32), 'ln_b': jnp.zeros((DEPTH, DIM), jnp.float32), 'W1': init(ks[3], (DEPTH, DIM, 2 * DIM_INNER)), 'b1': jnp.zeros((DEPTH, 2 * DIM_INNER), jnp.float32), 'W2': init(ks[4], (DEPTH, DIM_INNER, DIM)), 'b2': jnp.zeros((DEPTH, DIM), jnp.float32)}
    _L0_ffn_in = _L0_ffn_setup()
    _d = {'L0_attn_a_x': _L0_attn_a_in['x'], 'L0_attn_a_w_qkv': _L0_attn_a_in['w_qkv'], 'L0_attn_a_w_out': _L0_attn_a_in['w_out'], 'L0_attn_a_b_out': _L0_attn_a_in['b_out'], 'L0_attn_b_Wq': _L0_attn_b_in['Wq'], 'L0_attn_b_bq': _L0_attn_b_in['bq'], 'L0_attn_b_Wk': _L0_attn_b_in['Wk'], 'L0_attn_b_bk': _L0_attn_b_in['bk'], 'L0_attn_b_Wv': _L0_attn_b_in['Wv'], 'L0_attn_b_bv': _L0_attn_b_in['bv'], 'L0_attn_b_Wo': _L0_attn_b_in['Wo'], 'L0_attn_b_bo': _L0_attn_b_in['bo'], 'L0_attn_b_projection': _L0_attn_b_in['projection'], 'L0_ffn_Wqkv': _L0_ffn_in['Wqkv'], 'L0_ffn_q_scale': _L0_ffn_in['q_scale'], 'L0_ffn_k_scale': _L0_ffn_in['k_scale'], 'L0_ffn_Wo': _L0_ffn_in['Wo'], 'L0_ffn_ln_g': _L0_ffn_in['ln_g'], 'L0_ffn_ln_b': _L0_ffn_in['ln_b'], 'L0_ffn_W1': _L0_ffn_in['W1'], 'L0_ffn_b1': _L0_ffn_in['b1'], 'L0_ffn_W2': _L0_ffn_in['W2'], 'L0_ffn_b2': _L0_ffn_in['b2']}
    _x0 = _d['L0_attn_a_x']
    _d['L0_attn_a_x'] = jax.random.normal(jax.random.fold_in(jax.random.key(seed), 1), (1, 2048, 128), dtype=_x0.dtype)
    del _x0
    return _d

def reference(L0_attn_a_x, L0_attn_a_w_qkv, L0_attn_a_w_out, L0_attn_a_b_out, L0_attn_b_Wq, L0_attn_b_bq, L0_attn_b_Wk, L0_attn_b_bk, L0_attn_b_Wv, L0_attn_b_bv, L0_attn_b_Wo, L0_attn_b_bo, L0_attn_b_projection, L0_ffn_Wqkv, L0_ffn_q_scale, L0_ffn_k_scale, L0_ffn_Wo, L0_ffn_ln_g, L0_ffn_ln_b, L0_ffn_W1, L0_ffn_b1, L0_ffn_W2, L0_ffn_b2):

    def _L0_attn_a_ref(x, w_qkv, w_out, b_out):
        import jax, jax.numpy as jnp
        import numpy as np
        import math
        B, T, D = (2, 256, 128)
        N_HEADS = 16
        D_HEAD = D // N_HEADS

        def _rope_tables(t, d_head, dtype=jnp.float32):
            theta = 1.0 / 10000.0 ** (jnp.arange(0, d_head, 2, dtype=jnp.float32) / d_head)
            angles = jnp.outer(jnp.arange(t, dtype=jnp.float32), theta)
            angles = jnp.concatenate([angles, angles], axis=-1)
            return (jnp.cos(angles).astype(dtype), jnp.sin(angles).astype(dtype))

        def _rotate_half(x):
            half = x.shape[-1] // 2
            return jnp.concatenate([-x[..., half:], x[..., :half]], axis=-1)

        def _apply_rope(x, cos, sin):
            return x * cos[None, None] + _rotate_half(x) * sin[None, None]
        b, t, d = x.shape
        qkv = x @ w_qkv
        qkv = qkv.reshape(b, t, 3, N_HEADS, D_HEAD)
        q = jnp.transpose(qkv[:, :, 0], (0, 2, 1, 3))
        k = jnp.transpose(qkv[:, :, 1], (0, 2, 1, 3))
        v = jnp.transpose(qkv[:, :, 2], (0, 2, 1, 3))
        cos, sin = _rope_tables(t, D_HEAD, x.dtype)
        q = _apply_rope(q, cos, sin)
        k = _apply_rope(k, cos, sin)
        scores = jnp.einsum('bhqd,bhkd->bhqk', q, k) / math.sqrt(D_HEAD)
        probs = jax.nn.softmax(scores, axis=-1)
        out = jnp.einsum('bhqk,bhkd->bhqd', probs, v)
        out = jnp.transpose(out, (0, 2, 1, 3)).reshape(b, t, d)
        return out @ w_out + b_out

    def _L0_attn_b_ref(x, Wq, bq, Wk, bk, Wv, bv, Wo, bo, projection):
        import jax, jax.numpy as jnp
        import numpy as np
        EMBED_DIM = 128
        NUM_HEADS = 16
        HEAD_DIM = EMBED_DIM // NUM_HEADS
        NUM_FEATS = 32
        YAT_EPS = 0.1
        BATCH = 4
        SEQ = 512

        def _spherical_features(x, projection):
            x_norm = x / (jnp.linalg.norm(x, axis=-1, keepdims=True) + 1e-08)
            proj = jnp.einsum('bhsd,hfd->bhsf', x_norm, projection)
            return jax.nn.relu(proj) + YAT_EPS
        b, s, _ = x.shape

        def heads(t):
            return jnp.transpose(t.reshape(b, s, NUM_HEADS, HEAD_DIM), (0, 2, 1, 3))
        Q = heads(x @ Wq + bq)
        K = heads(x @ Wk + bk)
        V = heads(x @ Wv + bv)
        Qp = _spherical_features(Q, projection)
        Kp = _spherical_features(K, projection)
        KV = jnp.einsum('bhsf,bhsd->bhfd', Kp, V)
        QKV = jnp.einsum('bhsf,bhfd->bhsd', Qp, KV)
        K_sum = jnp.sum(Kp, axis=2)
        normalizer = jnp.einsum('bhsf,bhf->bhs', Qp, K_sum)[..., None]
        normalizer = jnp.maximum(normalizer, 1e-06)
        out = QKV / normalizer
        out = jnp.transpose(out, (0, 2, 1, 3)).reshape(b, s, EMBED_DIM)
        return out @ Wo + bo

    def _L0_ffn_ref(x, Wqkv, q_scale, k_scale, Wo, ln_g, ln_b, W1, b1, W2, b2):
        import jax, jax.numpy as jnp
        import numpy as np
        DIM = 128
        DEPTH = 6
        HEADS = 16
        DIM_HEAD = 64
        WINDOW = 32
        INNER = HEADS * DIM_HEAD
        DIM_INNER = int(DIM * 4 * 2 / 3)
        QK_SCALE = 8.0

        def shift_tokens(t):
            a, s = jnp.split(t, 2, -1)
            s = jnp.pad(s, ((0, 0), (1, 0), (0, 0)))[:, :-1]
            return jnp.concatenate([a, s], -1)

        def l2norm(t):
            return t / jnp.maximum(jnp.linalg.norm(t, axis=-1, keepdims=True), 1e-12)

        def rotate_half(x):
            x1, x2 = jnp.split(x, 2, -1)
            return jnp.concatenate([-x2, x1], -1)

        def rotary_tables(n):
            half = jnp.arange(0, DIM_HEAD, 2, dtype=jnp.float32)
            inv_freq = 1.0 / 10000.0 ** (half / DIM_HEAD)
            t = jnp.arange(n, dtype=jnp.float32)
            freqs = t[:, None] * inv_freq[None, :]
            freqs = jnp.concatenate([freqs, freqs], -1)
            base_scale = (half + 0.4 * DIM_HEAD) / (1.4 * DIM_HEAD)
            power = (t - n // 2) / (WINDOW // 2)
            scale = base_scale[None, :] ** power[:, None]
            scale = jnp.concatenate([scale, scale], -1)
            return (freqs, scale)

        def local_attention(q, k, v):
            b, h, n, d = q.shape
            w = WINDOW
            nw = n // w
            bq = q.reshape(b, h, nw, w, d)
            bk = k.reshape(b, h, nw, w, d)
            bv = v.reshape(b, h, nw, w, d)

            def look(t):
                p = jnp.pad(t, ((0, 0), (0, 0), (1, 0), (0, 0), (0, 0)))
                return jnp.concatenate([p[:, :, :nw], p[:, :, 1:]], axis=3)
            bk2, bv2 = (look(bk), look(bv))
            seq = jnp.arange(n).reshape(nw, w)
            seq_p = jnp.pad(seq, ((1, 0), (0, 0)), constant_values=-1)
            jt = jnp.concatenate([seq_p[:nw], seq_p[1:]], axis=1)
            it = seq[:, :, None]
            jb = jt[:, None, :]
            mask = (it < jb) | (it > jb + w) | (jb == -1)
            sim = jnp.einsum('bhwie,bhwje->bhwij', bq, bk2) * QK_SCALE
            sim = jnp.where(mask, -jnp.finfo(sim.dtype).max, sim)
            attn = jax.nn.softmax(sim, -1)
            out = jnp.einsum('bhwij,bhwje->bhwie', attn, bv2)
            return out.reshape(b, h, n, d)

        def attn_layer(x, Wqkv, qs, ksc, Wo):
            b, n, _ = x.shape
            qkv = x @ Wqkv
            q, k, v = jnp.split(qkv, 3, -1)
            sh = lambda t: t.reshape(b, n, HEADS, DIM_HEAD).transpose(0, 2, 1, 3)
            q, k, v = (sh(q), sh(k), sh(v))
            q = l2norm(q) * qs
            k = l2norm(k) * ksc
            freqs, scale = rotary_tables(n)
            cos, sin = (jnp.cos(freqs), jnp.sin(freqs))
            q = q * cos * scale + rotate_half(q) * sin * scale
            inv = 1.0 / scale
            k = k * cos * inv + rotate_half(k) * sin * inv
            out = local_attention(q, k, v)
            out = out.transpose(0, 2, 1, 3).reshape(b, n, INNER)
            return out @ Wo

        def ffn_layer(x, g, bln, W1, b1, W2, b2):
            mu = x.mean(-1, keepdims=True)
            var = ((x - mu) ** 2).mean(-1, keepdims=True)
            xn = (x - mu) / jnp.sqrt(var + 1e-05) * g + bln
            hg = xn @ W1 + b1
            a, gate = jnp.split(hg, 2, -1)
            return a * jax.nn.gelu(gate, approximate=False) @ W2 + b2
        for i in range(DEPTH):
            x = attn_layer(shift_tokens(x), Wqkv[i], q_scale[i], k_scale[i], Wo[i]) + x
            x = ffn_layer(shift_tokens(x), ln_g[i], ln_b[i], W1[i], b1[i], W2[i], b2[i]) + x
        return x
    x = L0_attn_a_x
    x = x + _L0_attn_a_ref(_layernorm(x, axis=-1), L0_attn_a_w_qkv, L0_attn_a_w_out, L0_attn_a_b_out)
    x = x + _L0_ffn_ref(_layernorm(x, axis=-1), L0_ffn_Wqkv, L0_ffn_q_scale, L0_ffn_k_scale, L0_ffn_Wo, L0_ffn_ln_g, L0_ffn_ln_b, L0_ffn_W1, L0_ffn_b1, L0_ffn_W2, L0_ffn_b2)
    x = x + _L0_attn_b_ref(_layernorm(x, axis=-1), L0_attn_b_Wq, L0_attn_b_bq, L0_attn_b_Wk, L0_attn_b_bk, L0_attn_b_Wv, L0_attn_b_bv, L0_attn_b_Wo, L0_attn_b_bo, L0_attn_b_projection)
    x = x + _L0_ffn_ref(_layernorm(x, axis=-1), L0_ffn_Wqkv, L0_ffn_q_scale, L0_ffn_k_scale, L0_ffn_Wo, L0_ffn_ln_g, L0_ffn_ln_b, L0_ffn_W1, L0_ffn_b1, L0_ffn_W2, L0_ffn_b2)
    return x

_drawn_inputs = setup_inputs


def setup_inputs(seed=0):
    import zlib

    import numpy as np

    out = dict(_drawn_inputs(seed))
    spreads = {'L0_attn_b_bq': (0.0, 0.8),
     'L0_attn_b_bk': (0.0, 0.8),
     'L0_attn_b_bv': (0.0, 0.1),
     'L0_attn_b_bo': (0.0, 0.1),
     'L0_ffn_q_scale': (1.0, 0.6),
     'L0_ffn_k_scale': (1.0, 0.6),
     'L0_ffn_ln_g': (1.0, 0.6),
     'L0_ffn_ln_b': (0.0, 0.8),
     'L0_ffn_b1': (0.0, 0.577),
     'L0_ffn_b2': (0.0, 0.1)}
    factors = {'L0_attn_a_b_out': 4.998,
     'L0_attn_b_Wq': 3.452,
     'L0_attn_b_Wk': 2.984,
     'L0_attn_b_projection': 5.202}
    for name, (base, spread) in spreads.items():
        noise = np.random.default_rng([zlib.crc32(name.encode()), seed]).standard_normal(out[name].shape)
        drawn = base * np.exp(spread * noise) if base else spread * noise
        out[name] = jnp.asarray(drawn.astype(out[name].dtype))
    for name, factor in factors.items():
        out[name] = (out[name] * factor).astype(out[name].dtype)
    return out
```

```python
from contextlib import ExitStack, contextmanager

import numpy as np

import concourse.bass as bass
from concourse import mybir

F32 = mybir.dt.float32
BF16 = mybir.dt.bfloat16
ALU = mybir.AluOpType
ACT = mybir.ActivationFunctionType
AX = mybir.AxisListType

P = 128
D = 128
N = 2048
NT = N // P
DEPTH = 6
HEADS = 16
DH = 64
INNER = HEADS * DH
WINDOW = 32
BLK = 64
KEYS = BLK + WINDOW
PAIRS = HEADS // 2
HID = int(D * 4 * 2 / 3)
HCH = [(0, 128), (128, 128), (256, HID - 256)]
GT = 4
NG = NT // GT
MASKED = -1e30
AD = D // HEADS
HQ = 4
FEATS = P // HQ
FEAT_EPS = 0.1
VW = 32


def host_tables():
    f = np.float32
    half = np.arange(0, DH, 2, dtype=f)
    inv_freq = (f(1.0) / np.power(f(10000.0), half / f(DH))).astype(f)
    t = np.arange(N, dtype=f)
    freqs = (t[:, None] * inv_freq[None, :]).astype(f)
    freqs = np.concatenate([freqs, freqs], -1)
    base = ((half + f(0.4 * DH)) / f(1.4 * DH)).astype(f)
    power = ((t - f(N // 2)) / f(WINDOW // 2)).astype(f)
    scale = np.power(base[None, :], power[:, None]).astype(f)
    scale = np.concatenate([scale, scale], -1)
    inv = (f(1.0) / scale).astype(f)
    cos, sin = np.cos(freqs), np.sin(freqs)
    sign = np.where(np.arange(DH) < DH // 2, f(-1), f(1))
    qk_scale = f(8.0)
    rope = np.stack([cos * scale * qk_scale, sign * sin * scale * qk_scale, cos * inv, sign * sin * inv])
    rope = rope.astype(f).reshape(4, NT, P, DH).transpose(2, 0, 1, 3)
    q = np.arange(P) % BLK
    c = np.arange(KEYS)
    seen = (c[None, :] >= q[:, None]) & (c[None, :] <= q[:, None] + WINDOW)
    rest = np.where(seen, f(0), f(MASKED))
    first = np.where(seen & (c[None, :] >= WINDOW), f(0), f(MASKED))
    mask = np.stack([np.stack([first if i == 0 else rest, rest], 1) for i in range(NT // 2)], 1)
    theta = (f(1.0) / np.power(f(10000.0), np.arange(0, AD, 2, dtype=f) / f(AD))).astype(f)
    angles = (t[:, None] * theta[None, :]).astype(f)
    angles = np.concatenate([angles, angles], -1)
    cos, sin = np.cos(angles), np.sin(angles)
    sign = np.where(np.arange(AD) < AD // 2, f(-1), f(1))
    down = f(1.0) / np.sqrt(f(AD))
    rope_a = np.stack([cos * down, sign * sin * down, cos, sign * sin]).astype(f).reshape(4, NT, P, AD).transpose(2, 0, 1, 3)
    fold = np.zeros((P, VW), f)
    for n in range(P):
        fold[n, n % VW] = 1
    own_head = np.zeros((P, HQ * AD + HQ), f)
    for n in range(P):
        h = n // FEATS
        own_head[n, h * AD:h * AD + AD] = 1
        own_head[n, HQ * AD + h] = 1
    return {
        "own_head": own_head,
        "rope_a": np.ascontiguousarray(rope_a.reshape(P, -1)),
        "fold": fold,
        "zero_row": np.zeros((1, D), f),
        "rope": np.ascontiguousarray(rope.reshape(P, -1)),
        "mask": np.ascontiguousarray(mask.astype(f).reshape(P, -1)),
        "ident": np.eye(P, dtype=f),
    }


@contextmanager
def clearing(nc, sems):
    with nc.Block() as block:
        yield block
    with nc.Block() as after:
        @after.sync
        def _(sp):
            for s in sems:
                sp.sem_clear(s)


def softmax_attention(nc, tag, x_in, w_qkv, w_out, b_out, consts, x_out, xf, xa):
    with ExitStack() as ctx:
        sems = []

        def sb(name, shape, dt=F32):
            return ctx.enter_context(nc.sbuf_tensor(f"{tag}_{name}", shape, dt))

        def sem(name):
            sems.append(ctx.enter_context(nc.semaphore(f"{tag}_{name}")))
            return sems[-1]

        banks = [ctx.enter_context(nc.psum_tensor(f"{tag}_bank{i}", [P, 512], F32)) for i in range(8)]
        ps_max = banks[0:2]
        ps_s = banks[2:6]
        ps_o = banks[6]
        ps_t = banks[7]

        GQ = GT * P
        wqkv = sb("wqkv", [P, 3 * D])
        wout = sb("wout", [P, D])
        bout = sb("bout", [P, D])
        ident = sb("ident", [P, P])
        ident_bf = sb("ident_bf", [P, P], BF16)
        rope = sb("rope", [P, 4, NT, AD])
        fold = sb("fold", [P, VW])
        minus_half = sb("minus_half", [P, GT])
        xg = sb("xg", [P, GT, D])
        st6 = sb("st6", [P, GT, 6])
        mv = sb("mv", [P, GT, 2])
        var = sb("var", [P, GT])
        rstd = sb("rstd", [P, GT])
        xn = sb("xn", [P, GT, D])
        xnT = sb("xnT", [P, GT, P])
        qk = sb("qk", [P, 2, GT, D])
        t1 = sb("t1", [P, 2, GT, D])
        t2 = sb("t2", [P, 2, GT, D])
        rest = sb("rest", [P, 2, 2, GT, D])
        parts = sb("parts", [P, 2, 3, NT, D], BF16)
        v_all = sb("v_all", [P, NT, D])
        stack = sb("stack", [P, 2, 2, NT, P], BF16)
        stackT = sb("stackT", [P, 2, 2, N], BF16)
        v_head = sb("v_head", [P, 2, NT, VW])
        maxima = sb("maxima", [P, NT, 4])
        neg = sb("neg", [P, 3, NT])
        pex = sb("pex", [P, 2, 2, GQ])
        osum = sb("osum", [P, GT, GQ])
        rec = sb("rec", [P, NT])
        ao = sb("ao", [P, NT, D])
        aoT = sb("aoT", [P, GT, P])
        y = sb("y", [P, GT, D])

        ld_c, ld_x, st_o, st_0, zeroed = sem("ld_c"), sem("ld_x"), sem("st_o"), sem("st_0"), sem("zeroed")
        dv_st, dv_mv, pl_var, pl_rstd, dv_xn = sem("dv_st"), sem("dv_mv"), sem("pl_var"), sem("pl_rstd"), sem("dv_xn")
        pe_xT, act_xT, pe_qkv, act_qk, act_v = sem("pe_xT"), sem("act_xT"), sem("pe_qkv"), sem("act_qk"), sem("act_v")
        dv_t2, pl_t1, pl_qr = sem("dv_t2"), sem("pl_t1"), sem("pl_qr")
        dv_part, dv_rest = sem("dv_part"), sem("dv_rest")
        pl_stack, pl_vh = sem("pl_stack"), sem("pl_vh")
        pe_tr, act_tr = sem("pe_tr"), sem("act_tr")
        pe_max, dv_max, dv_neg, dv_negp = sem("pe_max"), sem("dv_max"), sem("dv_neg"), sem("dv_negp")
        pe_s, act_ex, pe_pv, dv_os, pe_f, dv_rec, dv_ao = (sem("pe_s"), sem("act_ex"), sem("pe_pv"), sem("dv_os"),
                                                           sem("pe_f"), sem("dv_rec"), sem("dv_ao"))
        pe_aT, act_aT, pe_y, pl_xb, dv_y = sem("pe_aT"), sem("act_aT"), sem("pe_y"), sem("pl_xb"), sem("dv_y")

        FINAL = NG
        own_dve = sem("own_dve")
        own_pe = sem("own_pe")
        own_pool = sem("own_pool")
        block = ctx.enter_context(clearing(nc, sems))

        def grouped(dram, first):
            return dram[bass.ds(first, GQ), :].rearrange("(s p) d -> p s d", p=P)

        @block.sync
        def _(sp):
            sp.dma_start(ident[:], consts["ident"]).then_inc(ld_c, 16)
            sp.dma_start(rope[:], consts["rope_a"].rearrange("p (k t d) -> p k t d", k=4, t=NT)).then_inc(ld_c, 16)
            sp.dma_start(fold[:], consts["fold"]).then_inc(ld_c, 16)
            sp.dma_start(wqkv[:], w_qkv).then_inc(ld_c, 16)
            sp.dma_start(wout[:], w_out).then_inc(ld_c, 16)
            sp.dma_start(bout[:], b_out.rearrange("(o d) -> o d", o=1).broadcast_to([P, D])).then_inc(ld_c, 16)
            sp.dma_start(xf[0:1, :], consts["zero_row"]).then_inc(st_0, 16)
            sp.dma_start(xa[0:1, :], consts["zero_row"]).then_inc(st_0, 16)
            sp.dma_start(xg[:], grouped(x_in, 0)).then_inc(ld_x, 16)
            with sp.Fori(1, NG) as g:
                sp.wait_ge(dv_xn, g)
                sp.dma_start(xg[:], grouped(x_in, g * GQ)).then_inc(ld_x, 16)
            sp.wait_ge(dv_xn, NG)
            sp.dma_start(xg[:], grouped(x_in, 0)).then_inc(ld_x, 16)
            for g in range(NG):
                sp.wait_ge(dv_y, g + 1)
                sp.dma_start(grouped(x_out, g * GQ), y[:]).then_inc(st_o, 16)
                sp.wait_ge(dv_xn, FINAL + g + 1)
                sp.dma_start(grouped(xf, g * GQ + 1), xn[:]).then_inc(st_o, 16)
                if g + 1 < NG:
                    sp.dma_start(xg[:], grouped(x_in, (g + 1) * GQ)).then_inc(ld_x, 16)
                sp.wait_ge(st_o, 32 * g + 32)
            sp.wait_ge(st_0, 32)

        @block.gpsimd
        def _(pool):
            pool.memset(minus_half[:], -0.5).then_inc(zeroed, 1)
            pool.memset(stack[:], 0.0).then_inc(zeroed, 1)
            pool.memset(v_head[:], 0.0).then_inc(zeroed, 1)
            pool.wait_ge(zeroed, 3)
            pool.memset(stack[:, :, 1, :, 72:75], 1.0).then_inc(zeroed, 1)
            pool.memset(v_head[:, :, :, AD:AD + 1], 1.0).then_inc(zeroed, 1)
            pool.wait_ge(zeroed, 5)

            def inverse_std(k):
                pool.wait_ge(dv_mv, k + 1).then_inc(own_pool, 1)
                pool.tensor_scalar(var[:], mv[:, :, 1], 1e-5, None, ALU.add).then_inc(pl_var, 1)
                pool.wait_ge(pl_var, k + 1)
                pool.tensor_tensor(rstd[:], var[:], minus_half[:], ALU.pow).then_inc(pl_rstd, 1)

            with pool.Fori(0, NG) as g:
                inverse_std(g)
                pool.wait_ge(ld_c, 96)
                pool.wait_ge(act_qk, g + 1)
                heads = lambda a: a.rearrange("p s (h d) -> p s h d", d=AD)
                for kind in range(2):
                    tab = rope[:, 2 * kind, bass.ds(g * GT, GT), :].unsqueeze(2).broadcast_to([P, GT, HEADS, AD])
                    pool.tensor_tensor(heads(t1[:, kind, :, :]), heads(qk[:, kind, :, :]), tab, ALU.mult).then_inc(pl_t1, 1)
                for kind in range(2):
                    pool.wait_ge(pl_t1, 2 * g + kind + 1)
                    pool.wait_ge(dv_t2, 4 * g + 2 * kind + 2)
                    pool.tensor_tensor(t1[:, kind, :, :], t1[:, kind, :, :], t2[:, kind, :, :], ALU.add).then_inc(pl_qr, 1)
                pool.wait_ge(dv_part, 3 * g + 3)

            def stacks(h, p, first):
                if not first:
                    pool.wait_ge(pe_tr, 6 * h - 6).then_inc(own_pool, 1)
                    pool.wait_ge(pe_pv, 32 * h - 30).then_inc(own_pool, 1)
                one = lambda a: a[:, :, bass.ds(h * AD, AD)] if not isinstance(h, int) else a[:, :, h * AD:h * AD + AD]
                pool.memset(stack[:, p, 0, :, 72:75], 0.0)
                for i in range(3):
                    pool.tensor_copy(stack[:, p, 0, :, 24 * i:24 * i + 24].rearrange("p t (j d) -> p t j d", j=3),
                                     one(parts[:, 0, i, :, :]).unsqueeze(2).broadcast_to([P, NT, 3, AD]))
                    last = pool.tensor_copy(stack[:, p, 1, :, 0:72].rearrange("p t (i j d) -> p t i j d", i=3, j=3)[:, :, :, i, :],
                                            one(parts[:, 1, i, :, :]).unsqueeze(2).broadcast_to([P, NT, 3, AD]))
                last.then_inc(pl_stack, 1)
                pool.tensor_copy(v_head[:, p, :, 0:AD], one(v_all)).then_inc(pl_vh, 1)

            pool.wait_ge(act_v, NG)
            stacks(0, 0, True)
            stacks(1, 1, True)
            with pool.Fori(1, HEADS // 2) as i:
                for p in range(2):
                    stacks(2 * i + p, p, False)
            for g in range(NG):
                pool.wait_ge(ld_x, 16 * (NG + g + 1))
                pool.tensor_tensor(xg[:], xg[:], bout[:].unsqueeze(1).broadcast_to([P, GT, D]), ALU.add).then_inc(pl_xb, 1)
                inverse_std(FINAL + g)

        @block.scalar
        def _(act):
            act.sem_inc(act_ex, 2)
            with act.Fori(0, NG) as g:
                act.wait_ge(pe_xT, g + 1)
                act.copy(xnT[:], ps_t[:].rearrange("p (s q) -> p s q", s=GT)).then_inc(act_xT, 1)
                act.wait_ge(pe_qkv, g + 1)
                for s in range(GT):
                    last = act.copy(qk[:, :, s, :], banks[s][:, 0:2 * D].rearrange("p (k d) -> p k d", k=2))
                last.then_inc(act_qk, 1)
                for s in range(GT):
                    last = act.copy(v_all[:, bass.ds(g * GT + s, 1), :], banks[s][:, 2 * D:3 * D].unsqueeze(1))
                last.then_inc(act_v, 1)
                act.wait_ge(pl_qr, 2 * g + 2)

            act.wait_ge(ld_c, 96)
            act.copy(ident_bf[:], ident[:]).then_inc(zeroed, 1)

            def put_T(h, p, kind, half, n):
                act.wait_ge(pe_tr, 6 * h + n + 1)
                act.copy(stackT[:, p, kind, 1024 * half:1024 * half + 1024], ps_t[:].bitcast(BF16)).then_inc(act_tr, 1)

            def first_T(h, p):
                for n, (kind, half) in enumerate(((1, 0), (1, 1), (0, 0), (0, 1))):
                    put_T(h, p, kind, half, n)

            def second_T(h, p):
                for half in range(2):
                    put_T(h, p, 0, half, 4 + half)

            def exps(h, p):
                with act.Fori(0, NG) as g:
                    for r in range(8):
                        n = h * 32 + g * 8 + r
                        act.wait_ge(pe_s, n + 1)
                        act.wait_ge(pe_pv, n + 1)
                        b = r % 2
                        for e in range(2):
                            last = act.activation(pex[:, b, e, :], ps_s[2 * b + e][:], ACT.Exp)
                        last.then_inc(act_ex, 1)

            first_T(0, 0)
            second_T(0, 0)
            with act.Fori(0, HEADS // 2 - 1) as i:
                for p in range(2):
                    first_T(2 * i + p + 1, 1 - p)
                    exps(2 * i + p, p)
                    second_T(2 * i + p + 1, 1 - p)
            first_T(HEADS - 1, 1)
            exps(HEADS - 2, 0)
            second_T(HEADS - 1, 1)
            exps(HEADS - 1, 1)
            for g in range(NG):
                act.wait_ge(pe_aT, g + 1)
                act.copy(aoT[:], ps_t[:].rearrange("p (s q) -> p s q", s=GT)).then_inc(act_aT, 1)

        @block.vector
        def _(dve):
            dve.sem_inc(dv_max, 2)
            dve.sem_inc(dv_os, 4)
            dve.sem_inc(dv_ao, 1)

            def norm_stats(k, src):
                for s in range(GT):
                    last = dve.bn_stats(st6[:, s, :], src[:, s, :])
                last.then_inc(dv_st, 1)
                dve.wait_ge(dv_st, k + 1).then_inc(own_dve, 1)
                for s in range(GT):
                    last = dve.bn_aggr(mv[:, s, :], st6[:, s, :])
                last.then_inc(dv_mv, 1)

            def normalise(k, src):
                dve.wait_ge(pl_rstd, k + 1)
                for s in range(GT):
                    last = dve.tensor_scalar(xn[:, s, :], src[:, s, :], mv[:, s, 0:1], rstd[:, s:s + 1], ALU.subtract, ALU.mult)
                last.then_inc(dv_xn, 1)

            with dve.Fori(0, NG) as g:
                dve.wait_ge(ld_x, 16 * g + 16)
                norm_stats(g, xg)
                normalise(g, xg)
                dve.wait_ge(ld_c, 96)
                dve.wait_ge(act_qk, g + 1)
                heads = lambda a: a.rearrange("p s (h d) -> p s h d", d=AD)
                for kind in range(2):
                    for a in range(2):
                        tab = rope[:, 2 * kind + 1, bass.ds(g * GT, GT), AD // 2 * a:AD // 2 * a + AD // 2]
                        dve.tensor_tensor(heads(t2[:, kind, :, :])[:, :, :, AD // 2 * a:AD // 2 * a + AD // 2],
                                          heads(qk[:, kind, :, :])[:, :, :, AD // 2 * (1 - a):AD // 2 * (1 - a) + AD // 2],
                                          tab.unsqueeze(2).broadcast_to([P, GT, HEADS, AD // 2]), ALU.mult).then_inc(dv_t2, 1)
                dve.wait_ge(pl_qr, 2 * g + 2)
                src = t1
                for i in range(3):
                    at = parts[:, :, i, bass.ds(g * GT, GT), :]
                    dve.tensor_copy(at, src[:] if i == 0 else rest[:, i - 1, :, :, :]).then_inc(dv_part, 1)
                    if i < 2:
                        dve.wait_ge(dv_part, 3 * g + i + 1)
                        dve.tensor_tensor(rest[:, i, :, :, :], src[:] if i == 0 else rest[:, i - 1, :, :, :], at,
                                          ALU.subtract).then_inc(dv_rest, 1)
                        dve.wait_ge(dv_rest, 2 * g + i + 1)

            def maxima_of(h, g):
                for e in range(16):
                    m = h * 64 + g * 16 + e
                    dve.wait_ge(pe_max, m + 1)
                    dve.tensor_reduce(maxima[:, bass.ds(g * GT + e // 4, 1), e % 4:e % 4 + 1], ps_max[e % 2][:], AX.X,
                                      ALU.max).then_inc(dv_max, 1)

            def negate(h, p):
                dve.wait_ge(dv_max, 64 * h + 66)
                dve.tensor_reduce(neg[:, 0, :], maxima[:], AX.X, ALU.max, negate=True).then_inc(dv_neg, 1)
                for i in range(3):
                    dve.wait_ge(dv_neg, 3 * h + i + 1)
                    at = stack[:, p, 0, :, 72 + i]
                    dve.tensor_copy(at, neg[:, i, :]).then_inc(dv_negp, 1)
                    if i < 2:
                        dve.wait_ge(dv_negp, 3 * h + i + 1)
                        dve.tensor_tensor(neg[:, i + 1, :], neg[:, i, :], at, ALU.subtract).then_inc(dv_neg, 1)

            def sums(h, g):
                dve.wait_ge(pe_pv, 32 * h + 8 * g + 10)
                dve.tensor_copy(osum[:, bass.ds(g, 1), :], ps_o[:].unsqueeze(1)).then_inc(dv_os, 1)

            def outputs(h):
                dve.wait_ge(pe_f, h + 1)
                both = ps_t[:, 0:NT * VW].rearrange("p (t c) -> p t c", t=NT)
                dve.reciprocal(rec[:], both[:, :, AD]).then_inc(dv_rec, 1)
                dve.wait_ge(dv_rec, h + 1)
                at = ao[:, :, bass.ds(h * AD, AD)] if not isinstance(h, int) else ao[:, :, h * AD:h * AD + AD]
                dve.tensor_tensor(at, both[:, :, 0:AD], rec[:].unsqueeze(2).broadcast_to([P, NT, AD]), ALU.mult).then_inc(dv_ao, 1)

            def head(h, p, more):
                with dve.Fori(0, NG) as g:
                    if more:
                        maxima_of(h + 1, g)
                    sums(h, g)
                if more:
                    negate(h + 1, 1 - p)
                outputs(h)

            with dve.Fori(0, NG) as g:
                maxima_of(0, g)
            negate(0, 0)
            with dve.Fori(0, HEADS // 2 - 1) as i:
                for p in range(2):
                    head(2 * i + p, p, True)
            head(HEADS - 2, 0, True)
            head(HEADS - 1, 1, False)
            for g in range(NG):
                dve.wait_ge(pe_y, g + 1)
                dve.wait_ge(pl_xb, g + 1)
                if g:
                    dve.wait_ge(st_o, 32 * g)
                dve.tensor_tensor(y[:], banks[0][:].rearrange("p (s d) -> p s d", s=GT), xg[:], ALU.add).then_inc(dv_y, 1)
                dve.wait_ge(dv_y, g + 1)
                norm_stats(FINAL + g, y)
                normalise(FINAL + g, y)

        @block.tensor
        def _(pe):
            pe.sem_inc(pe_pv, 2)
            pe.wait_ge(ld_c, 96)
            with pe.Fori(0, NG) as g:
                pe.wait_ge(dv_xn, g + 1)
                for s in range(GT):
                    last = pe.transpose(ps_t[:, P * s:P * s + P], xn[:, s, :], ident[:])
                last.then_inc(pe_xT, 1)
                pe.wait_ge(act_xT, g + 1)
                for s in range(GT):
                    last = pe.matmul(banks[s][:, 0:3 * D], xnT[:, s, :], wqkv[:], start=True, stop=True)
                last.then_inc(pe_qkv, 1)
                pe.wait_ge(act_v, g + 1)

            def transposes(h, p, kind, half):
                for t in range(8):
                    last = pe.transpose(ps_t[:].bitcast(BF16)[:, P * t:P * t + P], stack[:, p, kind, 8 * half + t, :], ident_bf[:])
                last.then_inc(pe_tr, 1)

            def first_T(h, p):
                pe.wait_ge(pl_stack, h + 1)
                for n, (kind, half) in enumerate(((1, 0), (1, 1), (0, 0), (0, 1))):
                    if n:
                        pe.wait_ge(act_tr, 6 * h + n)
                    elif not (isinstance(h, int) and h == 0):
                        pe.wait_ge(act_tr, 6 * h)
                    transposes(h, p, kind, half)

            def second_T(h, p):
                pe.wait_ge(dv_negp, 3 * h + 3)
                for half in range(2):
                    pe.wait_ge(act_tr, 6 * h + 4 + half)
                    transposes(h, p, 0, half)

            def scores_for_max(h, p, g, e):
                m = h * 64 + g * 16 + e
                pe.wait_ge(dv_max, m + 1)
                pe.matmul(ps_max[e % 2][:], stackT[:, p, 0, bass.ds((g * GT + e // 4) * P, P)],
                          stackT[:, p, 1, GQ * (e % 4):GQ * (e % 4) + GQ], start=True, stop=True).then_inc(pe_max, 1)

            def scores(h, p, g, r):
                n = h * 32 + g * 8 + r
                pe.wait_ge(act_ex, n + 1)
                for e in range(2):
                    kt = 2 * r + e
                    last = pe.matmul(ps_s[2 * (r % 2) + e][:], stackT[:, p, 1, P * kt:P * kt + P],
                                     stackT[:, p, 0, bass.ds(g * GQ, GQ)], start=True, stop=True)
                last.then_inc(pe_s, 1)

            def values(h, p, g, r):
                n = h * 32 + g * 8 + r
                pe.wait_ge(act_ex, n + 3)
                if r == 0:
                    pe.wait_ge(dv_os, 4 * h + g + 4)
                for e in range(2):
                    kt = 2 * r + e
                    c = 32 * (kt % 4)
                    last = pe.matmul(ps_o[c:c + VW, :], v_head[:, p, kt, :], pex[:, r % 2, e, :], start=(kt < 4), stop=(kt >= 12),
                                     tile_position=(0, c))
                last.then_inc(pe_pv, 1)

            def head(h, p, more):
                pe.wait_ge(act_tr, 6 * h + 6).then_inc(own_pe, 1)
                pe.wait_ge(pl_vh, h + 1).then_inc(own_pe, 1)
                with pe.Fori(0, NG) as g:
                    for r in range(8):
                        scores(h, p, g, r)
                        if r == 7:
                            values(h, p, g, 6)
                        if more:
                            for e in range(2):
                                scores_for_max(h + 1, 1 - p, g, 2 * r + e)
                        if 1 <= r < 7:
                            values(h, p, g, r - 1)
                    values(h, p, g, 7)
                if more:
                    second_T(h + 1, 1 - p)
                    pe.wait_ge(act_tr, 6 * h + 12)
                pe.wait_ge(dv_os, 4 * h + 8)
                for t in range(NT):
                    last = pe.matmul(ps_t[:, VW * t:VW * t + VW], osum[:, t // GT, P * (t % GT):P * (t % GT) + P], fold[:],
                                     start=True, stop=True)
                last.then_inc(pe_f, 1)

            pe.wait_ge(zeroed, 6)
            first_T(0, 0)
            pe.wait_ge(act_tr, 4)
            with pe.Fori(0, NG) as g:
                for e in range(16):
                    scores_for_max(0, 0, g, e)
            second_T(0, 0)
            with pe.Fori(0, HEADS // 2 - 1) as i:
                for p in range(2):
                    h = 2 * i + p
                    pe.wait_ge(dv_ao, h + 1)
                    first_T(h + 1, 1 - p)
                    pe.wait_ge(act_tr, 6 * h + 10).then_inc(own_pe, 1)
                    head(h, p, True)
            pe.wait_ge(dv_ao, HEADS - 1)
            first_T(HEADS - 1, 1)
            pe.wait_ge(act_tr, 6 * HEADS - 2)
            head(HEADS - 2, 0, True)
            pe.wait_ge(dv_ao, HEADS)
            head(HEADS - 1, 1, False)
            pe.wait_ge(dv_ao, HEADS + 1)
            for g in range(NG):
                for s in range(GT):
                    last = pe.transpose(ps_t[:, P * s:P * s + P], ao[:, g * GT + s, :], ident[:])
                last.then_inc(pe_aT, 1)
                pe.wait_ge(act_aT, g + 1)
                if g:
                    pe.wait_ge(dv_y, g)
                for s in range(GT):
                    last = pe.matmul(banks[0][:, P * s:P * s + P], aoT[:, s, :], wout[:], start=True, stop=True)
                last.then_inc(pe_y, 1)


def local_stack(nc, tag, w, consts, xf, xa):
    with ExitStack() as ctx:
        sems = []

        def sb(name, shape, dt=F32):
            return ctx.enter_context(nc.sbuf_tensor(f"{tag}_{name}", shape, dt))

        def sem(name):
            sems.append(ctx.enter_context(nc.semaphore(f"{tag}_{name}")))
            return sems[-1]

        banks = [ctx.enter_context(nc.psum_tensor(f"{tag}_bank{i}", [P, 512], F32)) for i in range(8)]
        ps_qkv = banks[0:2]
        ps_s = banks[2:4]
        ps_t = banks[4:6]
        ps_v = banks[6]
        ps_x = banks[7]

        wqkv = sb("wqkv", [P, 3 * INNER])
        wo = sb("wo", [P, PAIRS, D])
        w1 = sb("w1", [P, 2 * HID])
        w2 = sb("w2", [P, 3, D])
        ln_g = sb("ln_g", [P, 1])
        ln_b = sb("ln_b", [P, 1])
        b1 = sb("b1", [P, 6])
        b2 = sb("b2", [P, D])
        qk_scales = sb("qk_scales", [P, 2, DH])
        rope0 = sb("rope0", [P, 4, NT, DH])
        rope = sb("rope", [P, 4, NT, DH])
        mask = sb("mask", [P, NT // 2, 2 * KEYS])
        ident = sb("ident", [P, P])

        x = sb("x", [P, 2, D])
        xs = sb("xs", [P, 2, D])
        xT = sb("xT", [P, P])
        sq = sb("sq", [P, 2, 512])
        ss = sb("ss", [P, 2, 8])
        sg = sb("sg", [P, 2, 8])
        rn = sb("rn", [P, 2, 8])
        minus_half = sb("minus_half", [P, 8])
        var = sb("var", [P, GT])
        qh = sb("qh", [P, 2, 512])
        t1 = sb("t1", [P, 2, 512])
        t2 = sb("t2", [P, 2, 512])
        qr = sb("qr", [P, 4, 512])
        qbd = sb("qbd", [P, PAIRS, 2, 2 * BLK])
        kT = sb("kT", [P, PAIRS, WINDOW + P])
        vt = sb("vt", [P, 2, INNER])
        vw = sb("vw", [P, 2, 2, INNER])
        s_sb = sb("s_sb", [P, 2, 4, KEYS])
        mx = sb("mx", [P, 2, 4])
        ex = sb("ex", [P, 2, 4, KEYS])
        sm = sb("sm", [P, 2, 4])
        rd = sb("rd", [P, 2, 4])
        pn = sb("pn", [P, 4, 4, KEYS])
        pT = sb("pT", [P, 2, 4, P])
        aT = sb("aT", [P, PAIRS, P])
        fx = sb("fx", [P, 2, GT, D])
        fxs = sb("fxs", [P, 2, GT, D])
        st6 = sb("st6", [P, GT, 6])
        mv = sb("mv", [P, GT, 2])
        rstd = sb("rstd", [P, GT])
        xn = sb("xn", [P, GT, D])
        xnT = sb("xnT", [P, GT * P])
        gl = sb("gl", [P, 3, GT * P])
        ag = sb("ag", [P, 3, GT * P])

        ld_const = sem("ld_const")
        ld_wa, ld_wf = sem("ld_wa"), sem("ld_wf")
        ld_x = [sem("ld_x0"), sem("ld_x1")]
        ld_vw = [sem("ld_vw0"), sem("ld_vw1")]
        ld_f = [sem("ld_f0"), sem("ld_f1")]
        st_a, st_f = sem("st_a"), sem("st_f")
        zeroed = sem("zeroed")
        pe_xT, pe_qkv, pe_qkT, pe_S = sem("pe_xT"), sem("pe_qkv"), sem("pe_qkT"), sem("pe_S")
        pe_PT, pe_PV, pe_Wo = sem("pe_PT"), sem("pe_PV"), sem("pe_Wo")
        act_xT, act_sq, act_v, act_qk = sem("act_xT"), sem("act_sq"), sem("act_v"), sem("act_qk")
        act_exp, act_PT, act_PV, act_kprev = sem("act_exp"), sem("act_PT"), sem("act_PV"), sem("act_kprev")
        dv_ssq, dv_qh, dv_t2 = sem("dv_ssq"), sem("dv_qh"), sem("dv_t2")
        dv_mask, dv_max, dv_sub, dv_sum, dv_rd = sem("dv_mask"), sem("dv_max"), sem("dv_sub"), sem("dv_sum"), sem("dv_rd")
        dv_y, dv_kzero = sem("dv_y"), sem("dv_kzero")
        pl_sg, pl_var = sem("pl_sg"), sem("pl_var")
        pl_rn, pl_rstd = sem("pl_rn"), sem("pl_rstd")
        pl_t1, pl_qr, pl_pn, pl_rope = sem("pl_t1"), sem("pl_qr"), sem("pl_pn"), sem("pl_rope")
        pe_fT, pe_h, pe_out = sem("pe_fT"), sem("pe_h"), sem("pe_out")
        act_fT, act_gelu = sem("act_fT"), sem("act_gelu")
        dv_st, dv_mv, dv_xn, dv_ag, dv_fy = (sem("dv_st"), sem("dv_mv"), sem("dv_xn"),
                                                      sem("dv_ag"), sem("dv_fy"))
        pl_b2 = sem("pl_b2")

        QK = [0, 2, 1, 3]
        KIND = [0, 1, 0, 1]
        HALF = [0, 0, 1, 1]
        ffn_bank = lambda n: [banks[0], banks[1], banks[2], banks[3], banks[5], banks[6]][n]

        def attn_weights(sp, layer):
            sp.dma_start(wqkv[:], w["Wqkv"][bass.ds(layer, 1), :, :].rearrange("l d n -> (l d) n")).then_inc(ld_wa, 16)
            sp.dma_start(wo[:], w["Wo"][bass.ds(layer, 1), :, :].rearrange("l (j p) n -> p (l j) n", p=P)).then_inc(ld_wa, 16)
            for n, name in enumerate(("q_scale", "k_scale")):
                sp.dma_start(qk_scales[:, n, :], w[name][bass.ds(layer, 1), :].broadcast_to([P, DH])).then_inc(ld_wa, 16)

        def ffn_weights(sp, layer):
            sp.dma_start(w1[:], w["W1"][bass.ds(layer, 1), :, :].rearrange("l d n -> (l d) n")).then_inc(ld_wf, 16)
            col = lambda a: a.rearrange("l (n o) -> (l n) o", o=1)
            for c, (f0, m) in enumerate(HCH):
                sp.dma_start(w2[0:m, c, :], w["W2"][bass.ds(layer, 1), f0:f0 + m, :].rearrange("l f n -> (l f) n")).then_inc(ld_wf, 16)
                sp.dma_start(b1[0:m, c:c + 1], col(w["b1"][bass.ds(layer, 1), f0:f0 + m])).then_inc(ld_wf, 16)
                sp.dma_start(b1[0:m, 3 + c:4 + c], col(w["b1"][bass.ds(layer, 1), HID + f0:HID + f0 + m])).then_inc(ld_wf, 16)
            sp.dma_start(ln_g[:], col(w["ln_g"][bass.ds(layer, 1), :])).then_inc(ld_wf, 16)
            sp.dma_start(ln_b[:], col(w["ln_b"][bass.ds(layer, 1), :])).then_inc(ld_wf, 16)
            sp.dma_start(b2[:], w["b2"][bass.ds(layer, 1), :].broadcast_to([P, D])).then_inc(ld_wf, 16)

        WA, WF = 4 * 16, 13 * 16

        own_dve = sem("own_dve")
        own_pe = sem("own_pe")
        own_pool = sem("own_pool")
        own_sp = sem("own_sp")
        block = ctx.enter_context(clearing(nc, sems))

        def rows(dram, first, n):
            return dram[bass.ds(first, n), :]

        @block.sync
        def _(sp):
            sp.sem_inc(st_f, 64)
            sp.sem_inc(ld_vw[1], 48)
            sp.dma_start(ident[:], consts["ident"]).then_inc(ld_const, 16)
            sp.dma_start(rope0[:], consts["rope"].rearrange("p (k t d) -> p k t d", k=4, t=NT)).then_inc(ld_const, 16)
            sp.dma_start(mask[:], consts["mask"].rearrange("p (i c) -> p i c", i=NT // 2)).then_inc(ld_const, 16)
            attn_weights(sp, 0)
            ffn_weights(sp, 0)
            sp.wait_ge(zeroed, 6)

            def load_x(L, t, p):
                sp.wait_ge(st_f, 64 * L + 16 * (t // 4 if isinstance(t, int) else t >> 2) + 16)
                sp.dma_start(x[:, p, :], rows(xf, t * P + 1, P)).then_inc(ld_x[p], 16)
                sp.dma_start(xs[:, p, 0:64], rows(xf, t * P + 1, P)[:, 0:64]).then_inc(ld_x[p], 16)
                sp.dma_start(xs[:, p, 64:128], rows(xf, t * P, P)[:, 64:128]).then_inc(ld_x[p], 16)

            def copy_v(L, t, p):
                k = L * NT + t
                sp.wait_ge(act_v, 2 * k + 4)
                sp.wait_ge(pe_PV, 4 * k + 4)
                sp.dma_start(vw[0:32, p, 0, :], vt[96:128, 1 - p, :]).then_inc(ld_vw[p], 16)
                sp.dma_start(vw[32:96, p, 0, :], vt[0:64, p, :]).then_inc(ld_vw[p], 16)
                sp.dma_start(vw[0:96, p, 1, :], vt[32:128, p, :]).then_inc(ld_vw[p], 16)

            def store_y(L, t, p):
                k = L * NT + t
                sp.wait_ge(dv_y, k + 3)
                sp.dma_start(rows(xa, t * P + 1, P), x[:, p, :]).then_inc(st_a, 16)
                sp.wait_ge(st_a, 16 * (k + 1)).then_inc(own_sp, 1)

            def load_f(L, g, p):
                sp.wait_ge(st_a, 16 * (L * NT + GT * g + GT))
                sp.wait_ge(st_f, 16 * (L * NG + g) + 48)
                r = lambda first: rows(xa, first, GT * P).rearrange("(s p) d -> p s d", p=P)
                sp.dma_start(fx[:, p, :, :], r(g * GT * P + 1)).then_inc(ld_f[p], 16)
                sp.dma_start(fxs[:, p, :, 0:64], r(g * GT * P + 1)[:, :, 0:64]).then_inc(ld_f[p], 16)
                sp.dma_start(fxs[:, p, :, 64:128], r(g * GT * P)[:, :, 64:128]).then_inc(ld_f[p], 16)

            def store_f(L, g, p):
                k = L * NG + g
                sp.wait_ge(dv_fy, k + 2)
                sp.dma_start(rows(xf, g * GT * P + 1, GT * P).rearrange("(s p) d -> p s d", p=P), fx[:, p, :, :]).then_inc(st_f, 16)
                sp.wait_ge(st_f, 16 * k + 80).then_inc(own_sp, 1)

            with sp.Fori(0, DEPTH) as L:
                load_x(L, 0, 0)
                load_x(L, 1, 1)
                copy_v(L, 0, 0)
                with sp.Fori(0, NT // 2 - 1) as i:
                    for p in range(2):
                        copy_v(L, 2 * i + p + 1, 1 - p)
                        store_y(L, 2 * i + p, p)
                        load_x(L, 2 * i + p + 2, p)
                copy_v(L, NT - 1, 1)
                store_y(L, NT - 2, 0)
                store_y(L, NT - 1, 1)
                load_f(L, 0, 0)
                load_f(L, 1, 1)
                attn_weights(sp, (L + 1) % DEPTH)
                for g in range(NG):
                    store_f(L, g, g % 2)
                    if g + 2 < NG:
                        load_f(L, g + 2, g % 2)
                ffn_weights(sp, (L + 1) % DEPTH)
            sp.wait_ge(ld_wa, WA * (DEPTH + 1))
            sp.wait_ge(ld_wf, WF * (DEPTH + 1))

        @block.gpsimd
        def _(pool):
            pool.sem_inc(pl_t1, 2)
            pool.sem_inc(pl_qr, 2)
            pool.sem_inc(pl_pn, 2)
            pool.memset(minus_half[:], -0.5).then_inc(zeroed, 1)
            for buf in (qbd, kT, vt, vw, pT):
                pool.memset(buf[:], 0.0).then_inc(zeroed, 1)

            def fold_rope(n):
                pool.wait_ge(ld_wa, WA * (n + 1))
                for kind in range(2):
                    whole = qk_scales[:, kind, :].unsqueeze(1).broadcast_to([P, NT, DH])
                    halves = qk_scales[:, kind, :].rearrange("p (a b) -> p a b", a=2)[:, ::-1, :]
                    pool.tensor_tensor(rope[:, 2 * kind, :, :], rope0[:, 2 * kind, :, :], whole, ALU.mult).then_inc(pl_rope, 1)
                    for a in range(2):
                        sl = slice(a * 32, a * 32 + 32)
                        pool.tensor_tensor(rope[:, 2 * kind + 1, :, sl], rope0[:, 2 * kind + 1, :, sl],
                                           halves[:, a, :].unsqueeze(1).broadcast_to([P, NT, 32]),
                                           ALU.mult).then_inc(pl_rope, 1)

            def inverse_norms(k, c):
                pool.wait_ge(dv_ssq, 4 * k + c + 3).then_inc(own_pool, 1)
                if c >= 2:
                    pool.wait_ge(dv_qh, 4 * k + c - 1).then_inc(own_pool, 1)
                pool.tensor_scalar(sg[:, c % 2, :], ss[:, c % 2, :], 1e-24, None, ALU.max).then_inc(pl_sg, 1)
                pool.wait_ge(pl_sg, 4 * k + c + 1)
                pool.tensor_tensor(rn[:, c % 2, :], sg[:, c % 2, :], minus_half[:], ALU.pow).then_inc(pl_rn, 1)

            def rotate(L, t, p):
                k = L * NT + t
                inverse_norms(k, 0)
                for c in range(4):
                    b = c % 2
                    if c < 3:
                        inverse_norms(k, c + 1)
                    pool.wait_ge(dv_qh, 4 * k + c + 1).then_inc(own_pool, 1)
                    pool.wait_ge(pl_qr, 4 * k + c + 1).then_inc(own_pool, 1)
                    tab = rope[:, 2 * KIND[c], t if isinstance(t, int) else bass.ds(t, 1), :]
                    tab = tab.unsqueeze(1) if isinstance(t, int) else tab
                    pool.tensor_tensor(t1[:, b, :].rearrange("p (h d) -> p h d", h=8),
                                       qh[:, b, :].rearrange("p (h d) -> p h d", h=8),
                                       tab.broadcast_to([P, 8, DH]), ALU.mult).then_inc(pl_t1, 1)
                    pool.wait_ge(pl_t1, 4 * k + c + 3)
                    pool.wait_ge(dv_t2, 4 * k + c + 3)
                    pool.wait_ge(pe_qkT, 4 * k + c + 1)
                    pool.tensor_tensor(qr[:, c, :], t1[:, b, :], t2[:, b, :], ALU.add).then_inc(pl_qr, 1)

            def normalise(L, t, p):
                k = L * NT + t
                for g in range(4):
                    b = g % 2
                    pool.wait_ge(dv_rd, 4 * k + g + 1)
                    pool.wait_ge(pe_PT, 4 * k + g + 1)
                    pool.tensor_tensor(pn[:, g, :, :], ex[:, b, :, :],
                                       rd[:, b, :].unsqueeze(2).broadcast_to([P, 4, KEYS]), ALU.mult).then_inc(pl_pn, 1)

            pool.wait_ge(zeroed, 6)
            pool.wait_ge(ld_const, 48)
            fold_rope(0)
            with pool.Fori(0, DEPTH) as L:
                pool.wait_ge(pl_rope, 6 * (L + 1))
                rotate(L, 0, 0)
                with pool.Fori(0, NT // 2 - 1) as i:
                    for p in range(2):
                        normalise(L, 2 * i + p, p)
                        rotate(L, 2 * i + p + 1, 1 - p)
                normalise(L, NT - 2, 0)
                rotate(L, NT - 1, 1)
                normalise(L, NT - 1, 1)
                pool.wait_ge(dv_t2, 4 * NT * (L + 1) + 2)
                fold_rope(L + 1)
                pool.wait_ge(ld_wf, WF * (L + 1)).then_inc(own_pool, 1)
                with pool.Fori(0, NG // 2) as i:
                    for p in range(2):
                        kp = L * (NG // 2) + i
                        k = L * NG + 2 * i + p
                        pool.wait_ge(dv_mv, k + 1).then_inc(own_pool, 1)
                        pool.tensor_scalar(var[:], mv[:, :, 1], 1e-5, None, ALU.add).then_inc(pl_var, 1)
                        pool.wait_ge(pl_var, k + 1)
                        pool.tensor_tensor(rstd[:], var[:], minus_half[:, 0:GT], ALU.pow).then_inc(pl_rstd, 1)
                        pool.wait_ge(ld_f[p], 48 * (kp + 1))
                        pool.tensor_tensor(fx[:, p, :, :], fx[:, p, :, :],
                                           b2[:].unsqueeze(1).broadcast_to([P, GT, D]), ALU.add).then_inc(pl_b2, 1)

        @block.scalar
        def _(act):
            act.sem_inc(act_PT, 4)
            act.sem_inc(act_v, 2)
            act.sem_inc(act_PV, 4)
            act.sem_inc(act_exp, 2)
            act.sem_inc(act_gelu, 3)
            act.sem_inc(act_fT, 1)

            def put_qk(L, t, p):
                k = L * NT + t
                for c in range(4):
                    half = HALF[c]
                    pairs = slice(4 * half, 4 * half + 4)
                    ps = ps_t[c % 2]
                    act.wait_ge(pe_qkT, 4 * k + c + 5)
                    if KIND[c] == 0:
                        for h in range(2):
                            r = slice(64 * h, 64 * h + 64)
                            last = act.copy(qbd[r, pairs, :, 64 * h:64 * h + 64],
                                            ps[r, :].rearrange("p (j b q) -> p j b q", j=4, b=2))
                        last.then_inc(act_qk, 1)
                    else:
                        act.copy(kT[:, pairs, 0:WINDOW], kT[:, pairs, P:P + WINDOW]).then_inc(act_kprev, 1)
                        act.wait_ge(act_kprev, 2 * k + half + 1)
                        act.copy(kT[:, pairs, WINDOW:], ps[:, :].rearrange("p (j q) -> p j q", j=4)).then_inc(act_qk, 1)

            def put_xT(L, t, p):
                act.wait_ge(pe_xT, L * NT + t + 1)
                act.copy(xT[:], ps_x[:, 0:P]).then_inc(act_xT, 1)

            def square(L, t, c):
                k = L * NT + t
                act.wait_ge(pe_qkv, 6 * k + c + 1)
                act.wait_ge(dv_ssq, 4 * k + c + 1)
                act.activation(sq[:, c % 2, :], ps_qkv[c % 2][:], ACT.Square).then_inc(act_sq, 1)

            def put_v(L, t, p, c):
                k = L * NT + t
                kp = L * (NT // 2) + (t // 2 if isinstance(t, int) else t >> 1)
                act.wait_ge(pe_qkv, 6 * k + 4 + c + 1)
                act.wait_ge(ld_vw[1 - p], 48 * (kp + 1))
                act.copy(vt[:, p, 512 * c:512 * c + 512], ps_qkv[c][:]).then_inc(act_v, 1)

            def exps(L, t, g):
                k = L * NT + t
                act.wait_ge(dv_sub, 4 * k + g + 1)
                act.wait_ge(pl_pn, 4 * k + g + 1)
                act.activation(ex[:, g % 2, :, :], s_sb[:, g % 2, :, :], ACT.Exp).then_inc(act_exp, 1)

            def put_pT(L, t, g):
                k = L * NT + t
                act.wait_ge(pe_PT, 4 * k + g + 5)
                act.wait_ge(pe_PV, 4 * k + g + 7)
                act.copy(pT[0:KEYS, g % 2, :, :], ps_t[g % 2][0:KEYS, :].rearrange("p (u q) -> p u q", u=4)).then_inc(act_PT, 1)

            def put_aT(L, t, g):
                k = L * NT + t
                act.wait_ge(pe_PV, 4 * k + g + 9)
                for h in range(2):
                    r = slice(64 * h, 64 * h + 64)
                    last = act.copy(aT[r, 2 * g:2 * g + 2, :].rearrange("p j (b q) -> p (j b) q", b=2),
                                    ps_v[r, :].rearrange("p (u q) -> p u q", u=4)[:, :, 64 * h:64 * h + 64])
                last.then_inc(act_PV, 1)

            def start_tile(L, t, p):
                put_xT(L, t, p)
                for c in range(4):
                    square(L, t, c)
                for c in range(2):
                    put_v(L, t, p, c)

            def tile(L, t, p, more):
                put_qk(L, t, p)
                if more:
                    put_xT(L, t + 1, 1 - p)
                for g in range(4):
                    exps(L, t, g)
                    if more and g < 2:
                        square(L, t + 1, g)
                if more:
                    for c in range(2, 4):
                        square(L, t + 1, c)
                    for c in range(2):
                        put_v(L, t + 1, 1 - p, c)
                for g in range(5):
                    if g < 4:
                        put_pT(L, t, g)
                    if g >= 1:
                        put_aT(L, t, g - 1)

            act.wait_ge(zeroed, 6)
            with act.Fori(0, DEPTH) as L:
                start_tile(L, 0, 0)
                act.wait_ge(dv_kzero, L + 1)
                with act.Fori(0, NT // 2 - 1) as i:
                    for p in range(2):
                        tile(L, 2 * i + p, p, True)
                tile(L, NT - 2, 0, True)
                tile(L, NT - 1, 1, False)
                act.wait_ge(ld_wf, WF * (L + 1))
                with act.Fori(0, NG // 2) as i:
                    for p in range(2):
                        k = L * NG + 2 * i + p
                        act.wait_ge(pe_fT, k + 2)
                        act.wait_ge(pe_h, 6 * k + 6)
                        act.activation(xnT[:], ps_t[0][:], ACT.Identity, bias=ln_b[:], scale=ln_g[:]).then_inc(act_fT, 1)
                        for c, (_, m) in enumerate(HCH):
                            act.wait_ge(pe_h, 6 * k + 2 * c + 7)
                            act.wait_ge(dv_ag, 3 * k + c + 1)
                            act.activation(gl[0:m, c, :], ffn_bank(2 * c)[0:m, :], ACT.Gelu,
                                           bias=b1[0:m, 3 + c:4 + c]).then_inc(act_gelu, 1)

        @block.vector
        def _(dve):
            dve.sem_inc(dv_mask, 4)
            dve.sem_inc(dv_y, 2)
            dve.sem_inc(dv_ssq, 2)
            dve.sem_inc(dv_t2, 2)
            dve.sem_inc(dv_ag, 3)
            dve.sem_inc(dv_fy, 1)
            dve.sem_inc(dv_kzero, 1)

            def norms(L, t, c):
                k = L * NT + t
                b = c % 2
                heads = lambda a: a.rearrange("p (h d) -> p h d", h=8)
                dve.wait_ge(act_sq, 4 * k + c + 1)
                if c >= 2:
                    dve.wait_ge(pl_rn, 4 * k + c - 1)
                dve.tensor_reduce(ss[:, b, :], heads(sq[:, b, :]), AX.X, ALU.add).then_inc(dv_ssq, 1)

            def rotate(L, t, c):
                k = L * NT + t
                b = c % 2
                heads = lambda a: a.rearrange("p (h d) -> p h d", h=8)
                dve.wait_ge(pl_rn, 4 * k + c + 1)
                dve.wait_ge(pl_t1, 4 * k + c + 1)
                dve.wait_ge(dv_t2, 4 * k + c + 1)
                dve.tensor_tensor(heads(qh[:, b, :]), heads(ps_qkv[b][:]), rn[:, b, :].unsqueeze(2).broadcast_to([P, 8, DH]),
                                  ALU.mult).then_inc(dv_qh, 1)
                dve.wait_ge(dv_qh, 4 * k + c + 1)
                dve.wait_ge(pl_qr, 4 * k + c + 1)
                tab = rope[:, 2 * KIND[c] + 1, t if isinstance(t, int) else bass.ds(t, 1), :]
                tab = tab.unsqueeze(1) if isinstance(t, int) else tab
                split = lambda a: a.rearrange("p (h a b) -> p h a b", h=8, a=2)
                dve.tensor_tensor(split(t2[:, b, :]), split(qh[:, b, :])[:, :, ::-1, :],
                                  tab.broadcast_to([P, 8, DH]).rearrange("p h (a b) -> p h a b", a=2),
                                  ALU.mult).then_inc(dv_t2, 1)

            def rotate_all(L, t):
                norms(L, t, 0)
                for c in range(4):
                    if c < 3:
                        norms(L, t, c + 1)
                    rotate(L, t, c)

            def softmax(L, t, g, mask_at):
                k = L * NT + t
                b = g % 2
                dve.wait_ge(pe_S, 4 * k + g + 1)
                dve.wait_ge(act_exp, 4 * k + g + 1)
                blocks = lambda a: a.rearrange("p (j c) -> p j c", j=2)
                dve.tensor_tensor(blocks(s_sb[:, b, :, :].rearrange("p u c -> p (u c)")), blocks(ps_s[b][:, 0:4 * KEYS]),
                                  mask[:, mask_at, :].broadcast_to([P, 2, 2 * KEYS]), ALU.add).then_inc(dv_mask, 1)
                dve.wait_ge(dv_mask, 4 * k + g + 5)
                dve.tensor_reduce(mx[:, b, :], s_sb[:, b, :, :], AX.X, ALU.max).then_inc(dv_max, 1)
                dve.wait_ge(dv_max, 4 * k + g + 1)
                dve.tensor_tensor(s_sb[:, b, :, :], s_sb[:, b, :, :], mx[:, b, :].unsqueeze(2).broadcast_to([P, 4, KEYS]),
                                  ALU.subtract).then_inc(dv_sub, 1)

            def sums(L, t, g):
                k = L * NT + t
                b = g % 2
                dve.wait_ge(act_exp, 4 * k + g + 3)
                dve.tensor_reduce(sm[:, b, :], ex[:, b, :, :], AX.X, ALU.add).then_inc(dv_sum, 1)
                dve.wait_ge(dv_sum, 4 * k + g + 1)
                dve.wait_ge(pl_pn, 4 * k + g + 1)
                dve.reciprocal(rd[:, b, :], sm[:, b, :]).then_inc(dv_rd, 1)

            def add_x(L, t, p):
                k = L * NT + t
                dve.wait_ge(pe_Wo, k + 1)
                dve.tensor_tensor(x[:, p, :], ps_x[:, P:2 * P], x[:, p, :], ALU.add).then_inc(dv_y, 1)

            def tile(L, t, p, mask_at, more):
                for g in range(5):
                    if g < 4:
                        softmax(L, t, g, mask_at)
                    if g >= 1:
                        sums(L, t, g - 1)
                if more:
                    rotate_all(L, t + 1)
                add_x(L, t, p)

            dve.wait_ge(ld_const, 48)
            with dve.Fori(0, DEPTH) as L:
                dve.wait_ge(pl_rope, 6 * (L + 1))
                rotate_all(L, 0)
                with dve.Fori(0, NT // 2 - 1) as i:
                    for p in range(2):
                        tile(L, 2 * i + p, p, bass.ds(i, 1) if p == 0 else slice(1, 2), True)
                tile(L, NT - 2, 0, slice(1, 2), True)
                tile(L, NT - 1, 1, slice(1, 2), False)
                dve.wait_ge(pe_S, 4 * NT * (L + 1))
                dve.memset(kT[:, :, P:P + WINDOW], 0.0).then_inc(dv_kzero, 1)
                dve.wait_ge(ld_wf, WF * (L + 1)).then_inc(own_dve, 1)
                with dve.Fori(0, NG // 2) as i:
                    for p in range(2):
                        k = L * NG + 2 * i + p
                        kp = L * (NG // 2) + i
                        dve.wait_ge(ld_f[p], 48 * (kp + 1))
                        for s in range(GT):
                            last = dve.bn_stats(st6[:, s, :], fxs[:, p, s, :])
                        last.then_inc(dv_st, 1)
                        dve.wait_ge(dv_st, k + 1).then_inc(own_dve, 1)
                        for s in range(GT):
                            last = dve.bn_aggr(mv[:, s, :], st6[:, s, :])
                        last.then_inc(dv_mv, 1)
                        dve.wait_ge(pl_rstd, k + 1)
                        dve.wait_ge(pe_fT, k + 1)
                        for s in range(GT):
                            last = dve.tensor_scalar(xn[:, s, :], fxs[:, p, s, :], mv[:, s, 0:1], rstd[:, s:s + 1],
                                                     ALU.subtract, ALU.mult)
                        last.then_inc(dv_xn, 1)
                        for c, (_, m) in enumerate(HCH):
                            dve.wait_ge(act_gelu, 3 * k + c + 4)
                            dve.wait_ge(pe_h, 6 * k + 2 * c + 8)
                            dve.wait_ge(pe_out, k + 1)
                            dve.scalar_tensor_tensor(out=ag[0:m, c, :], in0=ffn_bank(2 * c + 1)[0:m, :], scalar=b1[0:m, c:c + 1],
                                                     in1=gl[0:m, c, :], op0=ALU.add, op1=ALU.mult).then_inc(dv_ag, 1)
                        dve.wait_ge(pe_out, k + 2)
                        dve.wait_ge(pl_b2, k + 1)
                        dve.tensor_tensor(fx[:, p, :, :], ps_x[:].rearrange("p (s d) -> p s d", s=GT), fx[:, p, :, :],
                                          ALU.add).then_inc(dv_fy, 1)

        @block.tensor
        def _(pe):
            pe.sem_inc(pe_PV, 8)
            pe.sem_inc(pe_PT, 4)
            pe.sem_inc(pe_qkT, 4)
            pe.sem_inc(pe_fT, 1)
            pe.sem_inc(pe_out, 1)
            pe.sem_inc(pe_h, 6)

            def project(L, t, p):
                k = L * NT + t
                kp = L * (NT // 2) + (t // 2 if isinstance(t, int) else t >> 1)
                pe.wait_ge(ld_x[p], 48 * (kp + 1))
                pe.wait_ge(dv_y, k + 1)
                pe.transpose(ps_x[:, 0:P], xs[:, p, :], ident[:]).then_inc(pe_xT, 1)
                pe.wait_ge(act_xT, k + 1)
                for c in range(6):
                    if c < 2:
                        pe.wait_ge(act_v, 2 * k + c + 1)
                    else:
                        pe.wait_ge(dv_qh, 4 * k + c - 1)
                    at = 512 * ((QK + [4, 5])[c])
                    pe.matmul(ps_qkv[c % 2][:], xT[:], wqkv[:, at:at + 512], start=True, stop=True).then_inc(pe_qkv, 1)

            def scores(L, t, p):
                k = L * NT + t
                for c in range(4):
                    pe.wait_ge(pl_qr, 4 * k + c + 3)
                    if c < 2:
                        pe.wait_ge(act_PT, 4 * k + c + 3)
                    else:
                        pe.wait_ge(act_qk, 4 * k + c - 1)
                    for j in range(4):
                        last = pe.transpose(ps_t[c % 2][:, P * j:P * j + P], qr[:, c, P * j:P * j + P], ident[:])
                    last.then_inc(pe_qkT, 1)
                for g in range(4):
                    pe.wait_ge(act_qk, 4 * k + (2 if g < 2 else 4))
                    pe.wait_ge(dv_mask, 4 * k + g + 3)
                    for u in range(4):
                        j, b = 2 * g + u // 2, u % 2
                        last = pe.matmul(ps_s[g % 2][:, KEYS * u:KEYS * u + KEYS], qbd[:, j, b, :],
                                         kT[:, j, BLK * b:BLK * b + KEYS], start=True, stop=True)
                    last.then_inc(pe_S, 1)

            def values(L, t, p, more):
                k = L * NT + t
                kp = L * (NT // 2) + (t // 2 if isinstance(t, int) else t >> 1)
                for g in range(5):
                    if g < 4:
                        pe.wait_ge(pl_pn, 4 * k + g + 3)
                        if g < 2:
                            pe.wait_ge(act_qk, 4 * k + g + 3)
                        else:
                            pe.wait_ge(act_PT, 4 * k + g + 3)
                        for u in range(4):
                            last = pe.transpose(ps_t[g % 2][0:KEYS, P * u:P * u + P], pn[:, g, u, :], ident[:])
                        last.then_inc(pe_PT, 1)
                    if g == 1:
                        pe.wait_ge(ld_vw[p], 48 * (kp + 1) + 48 * p)
                    if g >= 1:
                        f = g - 1
                        pe.wait_ge(act_PT, 4 * k + f + 5)
                        pe.wait_ge(act_PV, 4 * k + f + 4)
                        for u in range(4):
                            j, b = 2 * f + u // 2, u % 2
                            last = pe.matmul(ps_v[:, P * u:P * u + P], vw[:, p, b, P * j:P * j + P], pT[:, f % 2, u, :],
                                             start=True, stop=True)
                        last.then_inc(pe_PV, 1)
                pe.wait_ge(act_PV, 4 * k + 8)
                pe.wait_ge(act_xT, k + (2 if more else 1))
                for j in range(PAIRS):
                    last = pe.matmul(ps_x[:, P:2 * P], aT[:, j, :], wo[:, j, :], start=(j == 0), stop=(j == PAIRS - 1))
                last.then_inc(pe_Wo, 1)

            pe.wait_ge(ld_const, 48)
            pe.wait_ge(zeroed, 6)
            with pe.Fori(0, DEPTH) as L:
                pe.wait_ge(dv_fy, NG * L + 1)
                pe.wait_ge(ld_wa, WA * (L + 1))
                project(L, 0, 0)
                with pe.Fori(0, NT // 2 - 1) as i:
                    for p in range(2):
                        scores(L, 2 * i + p, p)
                        project(L, 2 * i + p + 1, 1 - p)
                        values(L, 2 * i + p, p, True)
                scores(L, NT - 2, 0)
                project(L, NT - 1, 1)
                values(L, NT - 2, 0, True)
                scores(L, NT - 1, 1)
                values(L, NT - 1, 1, False)
                pe.wait_ge(dv_y, NT * (L + 1) + 2).then_inc(own_pe, 1)
                pe.wait_ge(ld_wf, WF * (L + 1)).then_inc(own_pe, 1)
                with pe.Fori(0, NG // 2) as i:
                    for p in range(2):
                        k = L * NG + 2 * i + p
                        pe.wait_ge(dv_xn, k + 1)
                        pe.wait_ge(act_fT, k + 1)
                        for s in range(GT):
                            last = pe.transpose(ps_t[0][:, P * s:P * s + P], xn[:, s, :], ident[:])
                        last.then_inc(pe_fT, 1)
                        pe.wait_ge(act_fT, k + 2)
                        for c, (f0, m) in enumerate(HCH):
                            pe.wait_ge(act_gelu, 3 * k + c + 1)
                            pe.matmul(ffn_bank(2 * c)[0:m, :], w1[:, HID + f0:HID + f0 + m], xnT[:], start=True, stop=True).then_inc(pe_h, 1)
                            pe.wait_ge(dv_ag, 3 * k + c + 1)
                            pe.matmul(ffn_bank(2 * c + 1)[0:m, :], w1[:, f0:f0 + m], xnT[:], start=True, stop=True).then_inc(pe_h, 1)
                        pe.wait_ge(dv_ag, 3 * k + 6)
                        pe.wait_ge(dv_fy, k + 1)
                        for s in range(GT):
                            for c, (_, m) in enumerate(HCH):
                                last = pe.matmul(ps_x[:, P * s:P * s + P], ag[0:m, c, P * s:P * s + P], w2[0:m, c, :],
                                                 start=(c == 0), stop=(c == 2))
                        last.then_inc(pe_out, 1)


def linear_attention(nc, tag, x_in, w, consts, x_out, xf):
    with ExitStack() as ctx:
        sems = []

        def sb(name, shape, dt=F32):
            return ctx.enter_context(nc.sbuf_tensor(f"{tag}_{name}", shape, dt))

        def sem(name):
            sems.append(ctx.enter_context(nc.semaphore(f"{tag}_{name}")))
            return sems[-1]

        banks = [ctx.enter_context(nc.psum_tensor(f"{tag}_bank{i}", [P, 512], F32)) for i in range(8)]
        ps_t = banks[4]
        ps_qk = banks[5:7]
        ps_kv = banks[7]

        GQ = GT * P
        HG = HEADS // HQ
        wqkv = sb("wqkv", [P, 3, D])
        wout = sb("wout", [P, D])
        bqkv = sb("bqkv", [P, 3, D])
        bout = sb("bout", [P, D])
        ident = sb("ident", [P, P])
        own_head = sb("own_head", [P, HQ * AD + HQ])
        proj_rows = sb("proj_rows", [P, HG, D])
        proj = sb("proj", [P, HEADS * FEATS])
        half = sb("half", [P, GT * 2 * HEADS])
        minus_half = sb("minus_half", [P, GT])
        xg = sb("xg", [P, GT, D])
        yg = sb("yg", [P, GT, D])
        x2 = sb("x2", [P, NT, D])
        st6 = sb("st6", [P, GT, 6])
        mv = sb("mv", [P, GT, 2])
        var = sb("var", [P, GT])
        rstd = sb("rstd", [P, GT])
        xn = sb("xn", [P, GT, D])
        xnT = sb("xnT", [P, GT, P])
        qk = sb("qk", [P, GT, 2, D])
        sq = sb("sq", [P, GT, 2, D])
        ss = sb("ss", [P, GT * 2 * HEADS])
        norm = sb("norm", [P, GT * 2 * HEADS])
        rn = sb("rn", [P, GT * 2 * HEADS])
        qkn = sb("qkn", [P, GT, 2, D])
        qkT = sb("qkT", [P, 2, GQ])
        v_one = sb("v_one", [P, GT, HG, HQ * AD + 1])
        kp = sb("kp", [P, GT, HEADS * FEATS])
        qp = sb("qp", [P, HG, N])
        kv = sb("kv", [P, HG, HQ * AD + 1])
        kvd = sb("kvd", [P, HG, HQ * AD + HQ])
        nrm = sb("nrm", [P, GT, HEADS])
        rec = sb("rec", [P, GT, HEADS])
        ao = sb("ao", [P, GT, D])
        aoT = sb("aoT", [P, GT, P])
        y = sb("y", [P, GT, D])

        ld_c, ld_p, ld_x, st_o, zeroed = sem("ld_c"), sem("ld_p"), sem("ld_x"), sem("st_o"), sem("zeroed")
        pe_proj, act_proj = sem("pe_proj"), sem("act_proj")
        dv_x2, dv_st, dv_mv, pl_var, pl_rstd, dv_xn, pl_xb = (sem("dv_x2"), sem("dv_st"), sem("dv_mv"), sem("pl_var"),
                                                              sem("pl_rstd"), sem("dv_xn"), sem("pl_xb"))
        pe_xT, act_xT, pe_qkv, dv_qk, dv_v = sem("pe_xT"), sem("act_xT"), sem("pe_qkv"), sem("dv_qk"), sem("dv_v")
        pl_sq, dv_ss, pl_root, pl_norm, dv_rn, dv_qkn = (sem("pl_sq"), sem("dv_ss"), sem("pl_root"), sem("pl_norm"),
                                                         sem("dv_rn"), sem("dv_qkn"))
        pe_qkT, act_qkT, pe_kp, dv_kp, pe_kv, dv_kv = (sem("pe_qkT"), sem("act_qkT"), sem("pe_kp"), sem("dv_kp"),
                                                       sem("pe_kv"), sem("dv_kv"))
        pe_qp, dv_qp, dv_kvd = sem("pe_qp"), sem("dv_qp"), sem("dv_kvd")
        pe_o, dv_nrm, dv_rec, dv_ao, pe_aT, act_aT, pe_y, dv_y = (sem("pe_o"), sem("dv_nrm"), sem("dv_rec"), sem("dv_ao"),
                                                                  sem("pe_aT"), sem("act_aT"), sem("pe_y"), sem("dv_y"))
        own_dve = sem("own_dve")
        own_pool = sem("own_pool")
        FINAL = NG
        LC = 16 * 10
        block = ctx.enter_context(clearing(nc, sems))

        def grouped(dram, first):
            return dram[bass.ds(first, GQ), :].rearrange("(s p) d -> p s d", p=P)

        @block.sync
        def _(sp):
            sp.dma_start(xg[:], grouped(x_in, 0)).then_inc(ld_x, 16)
            sp.dma_start(yg[:], grouped(xf, 1)).then_inc(ld_x, 16)
            sp.dma_start(ident[:], consts["ident"]).then_inc(ld_c, 16)
            for i, n in enumerate("qkv"):
                sp.dma_start(wqkv[:, i, :], w["W" + n]).then_inc(ld_c, 16)
                sp.dma_start(bqkv[:, i, :], w["b" + n].rearrange("(o d) -> o d", o=1).broadcast_to([P, D])).then_inc(ld_c, 16)
            sp.dma_start(own_head[:], consts["own_head"]).then_inc(ld_c, 16)
            sp.dma_start(wout[:], w["Wo"]).then_inc(ld_c, 16)
            sp.dma_start(bout[:], w["bo"].rearrange("(o d) -> o d", o=1).broadcast_to([P, D])).then_inc(ld_c, 16)
            with sp.Fori(1, NG) as g:
                sp.wait_ge(dv_xn, g)
                sp.wait_ge(pl_xb, g)
                sp.dma_start(xg[:], grouped(x_in, g * GQ)).then_inc(ld_x, 16)
                sp.dma_start(yg[:], grouped(xf, g * GQ + 1)).then_inc(ld_x, 16)
            for g in range(NG):
                sp.wait_ge(dv_y, g + 1)
                sp.dma_start(grouped(x_out, g * GQ), y[:]).then_inc(st_o, 16)
                sp.wait_ge(dv_xn, FINAL + g + 1)
                sp.dma_start(grouped(xf, g * GQ + 1), xn[:]).then_inc(st_o, 16)
            sp.wait_ge(st_o, 32 * NG)

        @block.gpsimd
        def _(pool):
            pool.memset(proj_rows[:], 0.0).then_inc(zeroed, 1)
            pool.memset(half[:], 0.5).then_inc(zeroed, 1)
            pool.memset(minus_half[:], -0.5).then_inc(zeroed, 1)
            pool.memset(v_one[:, :, :, HQ * AD:HQ * AD + 1], 1.0).then_inc(zeroed, 1)
            pool.wait_ge(zeroed, 4)

            def inverse_std(k):
                pool.wait_ge(dv_mv, k + 1).then_inc(own_pool, 1)
                pool.tensor_scalar(var[:], mv[:, :, 1], 1e-5, None, ALU.add).then_inc(pl_var, 1)
                pool.wait_ge(pl_var, k + 1)
                pool.tensor_tensor(rstd[:], var[:], minus_half[:], ALU.pow).then_inc(pl_rstd, 1)

            pool.wait_ge(ld_c, LC)
            with pool.Fori(0, NG) as g:
                inverse_std(g)
                pool.tensor_tensor(x2[:, bass.ds(g * GT, GT), :], xg[:], bout[:].unsqueeze(1).broadcast_to([P, GT, D]),
                                   ALU.add).then_inc(pl_xb, 1)
                pool.wait_ge(dv_qk, g + 1)
                pool.tensor_tensor(sq[:], qk[:], qk[:], ALU.mult).then_inc(pl_sq, 1)
                pool.wait_ge(dv_ss, g + 1)
                pool.tensor_tensor(norm[:], ss[:], half[:], ALU.pow).then_inc(pl_root, 1)
                pool.wait_ge(pl_root, g + 1).then_inc(own_pool, 1)
                pool.tensor_scalar(norm[:], norm[:], 1e-8, None, ALU.add).then_inc(pl_norm, 1)
            for g in range(NG):
                inverse_std(FINAL + g)

        @block.scalar
        def _(act):
            act.wait_ge(zeroed, 4)
            for h in range(HEADS):
                r = FEATS * (h % HQ)
                act.dma_start(proj_rows[r:r + FEATS, h // HQ, AD * h:AD * h + AD],
                              w["projection"][h:h + 1, :, :].rearrange("o f d -> (o f) d")).then_inc(ld_p, 16)
            act.wait_ge(pe_proj, 1)
            act.copy(proj[:], ps_t[:]).then_inc(act_proj, 1)
            with act.Fori(0, NG) as g:
                act.wait_ge(pe_xT, g + 1)
                act.copy(xnT[:], ps_t[:].rearrange("p (s q) -> p s q", s=GT)).then_inc(act_xT, 1)
                act.wait_ge(pe_qkT, g + 1)
                for i in (1, 0):
                    last = act.copy(qkT[:, i, :], ps_qk[i][:])
                last.then_inc(act_qkT, 1)
            for g in range(NG):
                act.wait_ge(pe_aT, g + 1)
                act.copy(aoT[:], ps_t[:].rearrange("p (s q) -> p s q", s=GT)).then_inc(act_aT, 1)

        @block.vector
        def _(dve):
            def norm_stats(k, src):
                for s in range(GT):
                    last = dve.bn_stats(st6[:, s, :], src[:, s, :])
                last.then_inc(dv_st, 1)
                dve.wait_ge(dv_st, k + 1).then_inc(own_dve, 1)
                for s in range(GT):
                    last = dve.bn_aggr(mv[:, s, :], st6[:, s, :])
                last.then_inc(dv_mv, 1)

            def normalise(k, src):
                dve.wait_ge(pl_rstd, k + 1)
                for s in range(GT):
                    last = dve.tensor_scalar(xn[:, s, :], src[:, s, :], mv[:, s, 0:1], rstd[:, s:s + 1], ALU.subtract, ALU.mult)
                last.then_inc(dv_xn, 1)

            dve.memset(kv[:], 0.0).then_inc(dv_kv, 1)
            with dve.Fori(0, NG) as g:
                dve.wait_ge(ld_x, 32 * g + 32)
                dve.tensor_tensor(xg[:], xg[:], yg[:], ALU.add).then_inc(dv_x2, 1)
                dve.wait_ge(dv_x2, g + 1)
                norm_stats(g, xg)
                normalise(g, xg)
                dve.wait_ge(ld_c, LC)
                dve.wait_ge(pe_qkv, g + 1)
                for s in range(GT):
                    last = dve.tensor_tensor(qk[:, s, :, :], banks[s][:, 0:2 * D].rearrange("p (k d) -> p k d", k=2),
                                             bqkv[:, 0:2, :], ALU.add)
                last.then_inc(dv_qk, 1)
                dve.wait_ge(zeroed, 4)
                for s in range(GT):
                    last = dve.tensor_tensor(v_one[:, s, :, 0:HQ * AD], banks[s][:, 2 * D:3 * D].rearrange("p (g d) -> p g d", g=HG),
                                             bqkv[:, 2, :].rearrange("p (g d) -> p g d", g=HG), ALU.add)
                last.then_inc(dv_v, 1)
                by_head = lambda a: a.rearrange("p s k (h d) -> p (s k h) d", d=AD)
                dve.wait_ge(pl_sq, g + 1)
                dve.tensor_reduce(ss[:], by_head(sq[:]), AX.X, ALU.add).then_inc(dv_ss, 1)
                dve.wait_ge(pl_norm, g + 1)
                dve.reciprocal(rn[:], norm[:]).then_inc(dv_rn, 1)
                dve.wait_ge(dv_rn, g + 1)
                dve.tensor_tensor(by_head(qkn[:]), by_head(qk[:]), rn[:].unsqueeze(2).broadcast_to([P, GT * 2 * HEADS, AD]),
                                  ALU.mult).then_inc(dv_qkn, 1)
                for s in range(GT):
                    dve.wait_ge(pe_kp, GT * g + s + 1)
                    dve.tensor_scalar(kp[:, s, :], banks[s][:], 0.0, FEAT_EPS, ALU.max, ALU.add).then_inc(dv_kp, 1)
                for i in range(HG):
                    dve.wait_ge(pe_qp, HG * g + i + 1)
                    dve.tensor_scalar(qp[:, i, bass.ds(g * GQ, GQ)], banks[i][:], 0.0, FEAT_EPS, ALU.max, ALU.add).then_inc(dv_qp, 1)
                dve.wait_ge(pe_kv, g + 1)
                dve.wait_ge(dv_kv, g + 1)
                dve.tensor_tensor(kv[:], kv[:], ps_kv[:, 0:HG * (HQ * AD + 1)].rearrange("p (g c) -> p g c", g=HG),
                                  ALU.add).then_inc(dv_kv, 1)
            C = HQ * AD
            dve.wait_ge(dv_kv, NG + 1)
            dve.tensor_tensor(kvd[:, :, 0:C], kv[:, :, 0:C], own_head[:, 0:C].unsqueeze(1).broadcast_to([P, HG, C]),
                              ALU.mult).then_inc(dv_kvd, 1)
            dve.tensor_tensor(kvd[:, :, C:C + HQ], kv[:, :, C:C + 1].broadcast_to([P, HG, HQ]),
                              own_head[:, C:C + HQ].unsqueeze(1).broadcast_to([P, HG, HQ]), ALU.mult).then_inc(dv_kvd, 1)
            for g in range(NG):
                for s in range(GT):
                    dve.wait_ge(pe_o, GT * g + s + 1)
                    o = banks[s][:, 0:HG * (C + HQ)].rearrange("p (g c) -> p g c", g=HG)
                    by_group = lambda a: a.rearrange("p (g h) -> p g h", g=HG)
                    dve.tensor_scalar(by_group(nrm[:, s, :]), o[:, :, C:C + HQ], 1e-6, None, ALU.max).then_inc(dv_nrm, 1)
                dve.wait_ge(dv_nrm, GT * g + GT)
                dve.reciprocal(rec[:], nrm[:]).then_inc(dv_rec, 1)
                dve.wait_ge(dv_rec, g + 1)
                if g:
                    dve.wait_ge(pe_aT, g)
                for s in range(GT):
                    o = banks[s][:, 0:HG * (C + HQ)].rearrange("p (g c) -> p g c", g=HG)
                    last = dve.tensor_tensor(ao[:, s, :].rearrange("p (g h d) -> p g h d", g=HG, h=HQ),
                                             o[:, :, 0:C].rearrange("p g (h d) -> p g h d", h=HQ),
                                             by_group(rec[:, s, :]).unsqueeze(3).broadcast_to([P, HG, HQ, AD]), ALU.mult)
                last.then_inc(dv_ao, 1)
                dve.wait_ge(pe_y, g + 1)
                dve.wait_ge(pl_xb, NG)
                if g:
                    dve.wait_ge(st_o, 32 * g)
                dve.tensor_tensor(y[:], ps_kv[:].rearrange("p (s d) -> p s d", s=GT), x2[:, g * GT:g * GT + GT, :],
                                  ALU.add).then_inc(dv_y, 1)
                dve.wait_ge(dv_y, g + 1)
                norm_stats(FINAL + g, y)
                normalise(FINAL + g, y)

        @block.tensor
        def _(pe):
            pe.wait_ge(ld_c, LC)
            pe.wait_ge(ld_p, 16 * HEADS)
            for i in range(HG):
                last = pe.transpose(ps_t[:, P * i:P * i + P], proj_rows[:, i, :], ident[:])
            last.then_inc(pe_proj, 1)
            pe.wait_ge(act_proj, 1)
            with pe.Fori(0, NG) as g:
                pe.wait_ge(dv_xn, g + 1)
                for s in range(GT):
                    last = pe.transpose(ps_t[:, P * s:P * s + P], xn[:, s, :], ident[:])
                last.then_inc(pe_xT, 1)
                pe.wait_ge(act_xT, g + 1)
                for s in range(GT):
                    last = pe.matmul(banks[s][:, 0:3 * D], xnT[:, s, :], wqkv[:].rearrange("p k d -> p (k d)"), start=True, stop=True)
                last.then_inc(pe_qkv, 1)
                pe.wait_ge(dv_qkn, g + 1)
                for i in (1, 0):
                    for s in range(GT):
                        last = pe.transpose(ps_qk[i][:, P * s:P * s + P], qkn[:, s, i, :], ident[:])
                last.then_inc(pe_qkT, 1)
                pe.wait_ge(act_qkT, g + 1)
                pe.wait_ge(dv_v, g + 1)
                for s in range(GT):
                    pe.matmul(banks[s][:], qkT[:, 1, P * s:P * s + P], proj[:], start=True, stop=True).then_inc(pe_kp, 1)
                for i in range(HG):
                    pe.wait_ge(dv_kp, GT * g + i + 1)
                    pe.matmul(banks[i][:], proj[:, P * i:P * i + P], qkT[:, 0, :], start=True, stop=True).then_inc(pe_qp, 1)
                pe.wait_ge(dv_kv, g + 1)
                for i in range(HG):
                    for s in range(GT):
                        last = pe.matmul(ps_kv[:, (HQ * AD + 1) * i:(HQ * AD + 1) * (i + 1)], kp[:, s, P * i:P * i + P],
                                         v_one[:, s, i, :], start=(s == 0), stop=(s == GT - 1))
                last.then_inc(pe_kv, 1)
                pe.wait_ge(dv_qp, HG * g + HG)
            pe.wait_ge(dv_kvd, 2)
            for g in range(NG):
                if g:
                    pe.wait_ge(dv_ao, g)
                for s in range(GT):
                    for i in range(HG):
                        c = HQ * AD + HQ
                        last = pe.matmul(banks[s][:, c * i:c * i + c], qp[:, i, P * (g * GT + s):P * (g * GT + s) + P], kvd[:, i, :],
                                         start=True, stop=True)
                    last.then_inc(pe_o, 1)
                pe.wait_ge(dv_ao, g + 1)
                for s in range(GT):
                    last = pe.transpose(ps_t[:, P * s:P * s + P], ao[:, s, :], ident[:])
                last.then_inc(pe_aT, 1)
                pe.wait_ge(act_aT, g + 1)
                if g:
                    pe.wait_ge(dv_y, g)
                for s in range(GT):
                    last = pe.matmul(ps_kv[:, P * s:P * s + P], aoT[:, s, :], wout[:], start=True, stop=True)
                last.then_inc(pe_y, 1)


def add_stack(nc, tag, x_in, xf, out):
    with ExitStack() as ctx:
        xg = ctx.enter_context(nc.sbuf_tensor(f"{tag}_xg", [P, NT, D], F32))
        yg = ctx.enter_context(nc.sbuf_tensor(f"{tag}_yg", [P, NT, D], F32))
        ld = [ctx.enter_context(nc.semaphore(f"{tag}_ld{g}")) for g in range(NG)]
        added = ctx.enter_context(nc.semaphore(f"{tag}_added"))
        stored = ctx.enter_context(nc.semaphore(f"{tag}_stored"))
        block = ctx.enter_context(nc.Block())

        def grouped(dram, first):
            return dram[first:first + GT * P, :].rearrange("(s p) d -> p s d", p=P)

        @block.sync
        def _(sp):
            for g in range(NG):
                sp.dma_start(xg[:, g * GT:g * GT + GT, :], grouped(x_in, g * GT * P)).then_inc(ld[g], 16)
                sp.dma_start(yg[:, g * GT:g * GT + GT, :], grouped(xf, g * GT * P + 1)).then_inc(ld[g], 16)
            for g in range(NG):
                sp.wait_ge(added, g + 1)
                sp.dma_start(grouped(out, g * GT * P), xg[:, g * GT:g * GT + GT, :]).then_inc(stored, 16)
            sp.wait_ge(stored, 16 * NG)

        @block.vector
        def _(dve):
            for g in range(NG):
                s = slice(g * GT, g * GT + GT)
                dve.wait_ge(ld[g], 32)
                dve.tensor_tensor(xg[:, s, :], xg[:, s, :], yg[:, s, :], ALU.add).then_inc(added, 1)


def block_program(nc, x, a, b, f, consts, out):
    x1 = nc.dram_tensor("x1", [N, D], F32, kind="Internal").ap()
    x3 = nc.dram_tensor("x3", [N, D], F32, kind="Internal").ap()
    xf = nc.dram_tensor("xf", [N + 1, D], F32, kind="Internal").ap()
    xa = nc.dram_tensor("xa", [N + 1, D], F32, kind="Internal").ap()
    softmax_attention(nc, "a", x, a["w_qkv"], a["w_out"], a["b_out"], consts, x1, xf, xa)
    local_stack(nc, "f", f, consts, xf, xa)
    linear_attention(nc, "b", x1, b, consts, x3, xf)
    local_stack(nc, "g", f, consts, xf, xa)
    add_stack(nc, "r", x3, xf, out)


A_NAMES = ["w_qkv", "w_out", "b_out"]
B_NAMES = ["Wq", "bq", "Wk", "bk", "Wv", "bv", "Wo", "bo", "projection"]
F_NAMES = ["Wqkv", "q_scale", "k_scale", "Wo", "ln_g", "ln_b", "W1", "b1", "W2", "b2"]


def kernel(**inputs):
    import concourse.bacc as bacc
    from concourse.bass_utils import run_bass_kernel_spmd

    nc = bacc.Bacc("TRN2", target_bir_lowering=False, num_devices=1)
    arrays = {}

    def load(name, a):
        arrays[name] = np.ascontiguousarray(a)
        return nc.dram_tensor(name, arrays[name].shape, F32, kind="ExternalInput").ap()

    x = load("in_x_dram", np.asarray(inputs["L0_attn_a_x"]).reshape(N, D))
    a = {n: load(f"in_a_{n}_dram", inputs[f"L0_attn_a_{n}"]) for n in A_NAMES}
    b = {n: load(f"in_b_{n}_dram", inputs[f"L0_attn_b_{n}"]) for n in B_NAMES}
    f = {n: load(f"in_f_{n}_dram", inputs[f"L0_ffn_{n}"]) for n in F_NAMES}
    consts = {n: load(f"const_{n}_dram", t) for n, t in host_tables().items()}
    out = nc.dram_tensor("out_0_dram", (N, D), F32, kind="ExternalOutput").ap()
    block_program(nc, x, a, b, f, consts, out)
    r = run_bass_kernel_spmd(nc, [arrays], core_ids=[0])
    return r.results[0]["out_0_dram"].reshape(1, N, D)
```

```python
from contextlib import ExitStack, contextmanager

import numpy as np

import concourse.bass as bass
from concourse import mybir

F32 = mybir.dt.float32
BF16 = mybir.dt.bfloat16
ALU = mybir.AluOpType
ACT = mybir.ActivationFunctionType
AX = mybir.AxisListType

P = 128
D = 128
N = 2048
NT = N // P
DEPTH = 6
HEADS = 16
DH = 64
INNER = HEADS * DH
WINDOW = 32
BLK = 64
KEYS = BLK + WINDOW
PAIRS = HEADS // 2
HID = int(D * 4 * 2 / 3)
HCH = [(0, 128), (128, 128), (256, HID - 256)]
FT = 2
FQ = FT * P
NF = NT // FT
GT = 4
NG = NT // GT
MASKED = -1e30
AD = D // HEADS
HQ = 4
FEATS = P // HQ
FEAT_EPS = 0.1
VW = 32


def host_tables():
    f = np.float32
    half = np.arange(0, DH, 2, dtype=f)
    inv_freq = (f(1.0) / np.power(f(10000.0), half / f(DH))).astype(f)
    t = np.arange(N, dtype=f)
    freqs = (t[:, None] * inv_freq[None, :]).astype(f)
    freqs = np.concatenate([freqs, freqs], -1)
    base = ((half + f(0.4 * DH)) / f(1.4 * DH)).astype(f)
    power = ((t - f(N // 2)) / f(WINDOW // 2)).astype(f)
    scale = np.power(base[None, :], power[:, None]).astype(f)
    scale = np.concatenate([scale, scale], -1)
    inv = (f(1.0) / scale).astype(f)
    cos, sin = np.cos(freqs), np.sin(freqs)
    sign = np.where(np.arange(DH) < DH // 2, f(-1), f(1))
    qk_scale = f(8.0)
    rope = np.stack([cos * scale * qk_scale, sign * sin * scale * qk_scale, cos * inv, sign * sin * inv])
    rope = rope.astype(f).reshape(4, NT, P, DH).transpose(2, 0, 1, 3)
    q = np.arange(P) % BLK
    c = np.arange(KEYS)
    seen = (c[None, :] >= q[:, None]) & (c[None, :] <= q[:, None] + WINDOW)
    rest = np.where(seen, f(0), f(MASKED))
    first = np.where(seen & (c[None, :] >= WINDOW), f(0), f(MASKED))
    mask = np.stack([np.stack([start, rest, start, rest], 1) for start in (first, rest)], 1)
    theta = (f(1.0) / np.power(f(10000.0), np.arange(0, AD, 2, dtype=f) / f(AD))).astype(f)
    angles = (t[:, None] * theta[None, :]).astype(f)
    angles = np.concatenate([angles, angles], -1)
    cos, sin = np.cos(angles), np.sin(angles)
    sign = np.where(np.arange(AD) < AD // 2, f(-1), f(1))
    down = f(1.0) / np.sqrt(f(AD))
    rope_a = np.stack([cos * down, sign * sin * down, cos, sign * sin]).astype(f).reshape(4, NT, P, AD).transpose(2, 0, 1, 3)
    fold = np.zeros((P, VW), f)
    for n in range(P):
        fold[n, n % VW] = 1
    own_head = np.zeros((P, HQ * AD + HQ), f)
    for n in range(P):
        h = n // FEATS
        own_head[n, h * AD:h * AD + AD] = 1
        own_head[n, HQ * AD + h] = 1
    return {
        "own_head": own_head,
        "rope_a": np.ascontiguousarray(rope_a.reshape(P, -1)),
        "fold": fold,
        "zero_row": np.zeros((1, D), f),
        "rope": np.ascontiguousarray(rope.reshape(P, -1)),
        "mask": np.ascontiguousarray(mask.astype(f).reshape(P, -1)),
        "ident": np.eye(P, dtype=f),
    }


@contextmanager
def clearing(nc, sems):
    with nc.Block() as block:
        yield block
    with nc.Block() as after:
        @after.sync
        def _(sp):
            for s in sems:
                sp.sem_clear(s)


def softmax_attention(nc, tag, x_in, w_qkv, w_out, b_out, consts, x_out, xf, xa):
    with ExitStack() as ctx:
        sems = []

        def sb(name, shape, dt=F32):
            return ctx.enter_context(nc.sbuf_tensor(f"{tag}_{name}", shape, dt))

        def sem(name):
            sems.append(ctx.enter_context(nc.semaphore(f"{tag}_{name}")))
            return sems[-1]

        banks = [ctx.enter_context(nc.psum_tensor(f"{tag}_bank{i}", [P, 512], F32)) for i in range(8)]
        ps_max = banks[0:2]
        ps_s = banks[2:6]
        ps_o = banks[6]
        ps_t = banks[7]

        GQ = GT * P
        wqkv = sb("wqkv", [P, 3 * D])
        wout = sb("wout", [P, D])
        bout = sb("bout", [P, D])
        ident = sb("ident", [P, P])
        ident_bf = sb("ident_bf", [P, P], BF16)
        rope = sb("rope", [P, 4, NT, AD])
        fold = sb("fold", [P, VW])
        minus_half = sb("minus_half", [P, GT])
        xg = sb("xg", [P, GT, D])
        st6 = sb("st6", [P, GT, 6])
        mv = sb("mv", [P, GT, 2])
        var = sb("var", [P, GT])
        rstd = sb("rstd", [P, GT])
        xn = sb("xn", [P, GT, D])
        xnT = sb("xnT", [P, GT, P])
        qk = sb("qk", [P, 2, GT, D])
        t1 = sb("t1", [P, 2, GT, D])
        t2 = sb("t2", [P, 2, GT, D])
        rest = sb("rest", [P, 2, 2, GT, D])
        parts = sb("parts", [P, 2, 3, NT, D], BF16)
        v_all = sb("v_all", [P, NT, D])
        stack = sb("stack", [P, 2, 2, NT, P], BF16)
        stackT = sb("stackT", [P, 2, 2, N], BF16)
        v_head = sb("v_head", [P, 2, NT, VW])
        maxima = sb("maxima", [P, NT, 4])
        neg = sb("neg", [P, 3, NT])
        pex = sb("pex", [P, 2, 2, GQ])
        osum = sb("osum", [P, GT, GQ])
        rec = sb("rec", [P, NT])
        ao = sb("ao", [P, NT, D])
        aoT = sb("aoT", [P, GT, P])
        y = sb("y", [P, GT, D])

        ld_c, ld_x, st_o, st_0, zeroed = sem("ld_c"), sem("ld_x"), sem("st_o"), sem("st_0"), sem("zeroed")
        dv_st, dv_mv, pl_var, pl_rstd, dv_xn = sem("dv_st"), sem("dv_mv"), sem("pl_var"), sem("pl_rstd"), sem("dv_xn")
        pe_xT, act_xT, pe_qkv, act_qk, act_v = sem("pe_xT"), sem("act_xT"), sem("pe_qkv"), sem("act_qk"), sem("act_v")
        dv_t2, pl_t1, pl_qr = sem("dv_t2"), sem("pl_t1"), sem("pl_qr")
        dv_part, dv_rest = sem("dv_part"), sem("dv_rest")
        pl_stack, pl_vh = sem("pl_stack"), sem("pl_vh")
        pe_tr, act_tr = sem("pe_tr"), sem("act_tr")
        pe_max, dv_max, dv_neg, dv_negp = sem("pe_max"), sem("dv_max"), sem("dv_neg"), sem("dv_negp")
        pe_s, act_ex, pe_pv, dv_os, pe_f, dv_rec, dv_ao = (sem("pe_s"), sem("act_ex"), sem("pe_pv"), sem("dv_os"),
                                                           sem("pe_f"), sem("dv_rec"), sem("dv_ao"))
        pe_aT, act_aT, pe_y, pl_xb, dv_y = sem("pe_aT"), sem("act_aT"), sem("pe_y"), sem("pl_xb"), sem("dv_y")

        FINAL = NG
        own_dve = sem("own_dve")
        own_pe = sem("own_pe")
        own_pool = sem("own_pool")
        block = ctx.enter_context(clearing(nc, sems))

        def grouped(dram, first):
            return dram[bass.ds(first, GQ), :].rearrange("(s p) d -> p s d", p=P)

        @block.sync
        def _(sp):
            sp.dma_start(ident[:], consts["ident"]).then_inc(ld_c, 16)
            sp.dma_start(rope[:], consts["rope_a"].rearrange("p (k t d) -> p k t d", k=4, t=NT)).then_inc(ld_c, 16)
            sp.dma_start(fold[:], consts["fold"]).then_inc(ld_c, 16)
            sp.dma_start(wqkv[:], w_qkv).then_inc(ld_c, 16)
            sp.dma_start(wout[:], w_out).then_inc(ld_c, 16)
            sp.dma_start(bout[:], b_out.rearrange("(o d) -> o d", o=1).broadcast_to([P, D])).then_inc(ld_c, 16)
            sp.dma_start(xf[0:1, :], consts["zero_row"]).then_inc(st_0, 16)
            sp.dma_start(xa[0:1, :], consts["zero_row"]).then_inc(st_0, 16)
            sp.dma_start(xg[:], grouped(x_in, 0)).then_inc(ld_x, 16)
            with sp.Fori(1, NG) as g:
                sp.wait_ge(dv_xn, g)
                sp.dma_start(xg[:], grouped(x_in, g * GQ)).then_inc(ld_x, 16)
            sp.wait_ge(dv_xn, NG)
            sp.dma_start(xg[:], grouped(x_in, 0)).then_inc(ld_x, 16)
            for g in range(NG):
                sp.wait_ge(dv_y, g + 1)
                sp.dma_start(grouped(x_out, g * GQ), y[:]).then_inc(st_o, 16)
                sp.wait_ge(dv_xn, FINAL + g + 1)
                sp.dma_start(grouped(xf, g * GQ + 1), xn[:]).then_inc(st_o, 16)
                if g + 1 < NG:
                    sp.dma_start(xg[:], grouped(x_in, (g + 1) * GQ)).then_inc(ld_x, 16)
                sp.wait_ge(st_o, 32 * g + 32)
            sp.wait_ge(st_0, 32)

        @block.gpsimd
        def _(pool):
            pool.memset(minus_half[:], -0.5).then_inc(zeroed, 1)
            pool.memset(stack[:], 0.0).then_inc(zeroed, 1)
            pool.memset(v_head[:], 0.0).then_inc(zeroed, 1)
            pool.wait_ge(zeroed, 3)
            pool.memset(stack[:, :, 1, :, 72:75], 1.0).then_inc(zeroed, 1)
            pool.memset(v_head[:, :, :, AD:AD + 1], 1.0).then_inc(zeroed, 1)
            pool.wait_ge(zeroed, 5)

            def inverse_std(k):
                pool.wait_ge(dv_mv, k + 1).then_inc(own_pool, 1)
                pool.tensor_scalar(var[:], mv[:, :, 1], 1e-5, None, ALU.add).then_inc(pl_var, 1)
                pool.wait_ge(pl_var, k + 1)
                pool.tensor_tensor(rstd[:], var[:], minus_half[:], ALU.pow).then_inc(pl_rstd, 1)

            with pool.Fori(0, NG) as g:
                inverse_std(g)
                pool.wait_ge(ld_c, 96)
                pool.wait_ge(act_qk, g + 1)
                heads = lambda a: a.rearrange("p s (h d) -> p s h d", d=AD)
                for kind in range(2):
                    tab = rope[:, 2 * kind, bass.ds(g * GT, GT), :].unsqueeze(2).broadcast_to([P, GT, HEADS, AD])
                    pool.tensor_tensor(heads(t1[:, kind, :, :]), heads(qk[:, kind, :, :]), tab, ALU.mult).then_inc(pl_t1, 1)
                for kind in range(2):
                    pool.wait_ge(pl_t1, 2 * g + kind + 1)
                    pool.wait_ge(dv_t2, 4 * g + 2 * kind + 2)
                    pool.tensor_tensor(t1[:, kind, :, :], t1[:, kind, :, :], t2[:, kind, :, :], ALU.add).then_inc(pl_qr, 1)
                pool.wait_ge(dv_part, 3 * g + 3)

            def stacks(h, p, first):
                if not first:
                    pool.wait_ge(pe_tr, 6 * h - 6).then_inc(own_pool, 1)
                    pool.wait_ge(pe_pv, 32 * h - 30).then_inc(own_pool, 1)
                one = lambda a: a[:, :, bass.ds(h * AD, AD)] if not isinstance(h, int) else a[:, :, h * AD:h * AD + AD]
                pool.memset(stack[:, p, 0, :, 72:75], 0.0)
                for i in range(3):
                    pool.tensor_copy(stack[:, p, 0, :, 24 * i:24 * i + 24].rearrange("p t (j d) -> p t j d", j=3),
                                     one(parts[:, 0, i, :, :]).unsqueeze(2).broadcast_to([P, NT, 3, AD]))
                    last = pool.tensor_copy(stack[:, p, 1, :, 0:72].rearrange("p t (i j d) -> p t i j d", i=3, j=3)[:, :, :, i, :],
                                            one(parts[:, 1, i, :, :]).unsqueeze(2).broadcast_to([P, NT, 3, AD]))
                last.then_inc(pl_stack, 1)
                pool.tensor_copy(v_head[:, p, :, 0:AD], one(v_all)).then_inc(pl_vh, 1)

            pool.wait_ge(act_v, NG)
            stacks(0, 0, True)
            stacks(1, 1, True)
            with pool.Fori(1, HEADS // 2) as i:
                for p in range(2):
                    stacks(2 * i + p, p, False)
            for g in range(NG):
                pool.wait_ge(ld_x, 16 * (NG + g + 1))
                pool.tensor_tensor(xg[:], xg[:], bout[:].unsqueeze(1).broadcast_to([P, GT, D]), ALU.add).then_inc(pl_xb, 1)
                inverse_std(FINAL + g)

        @block.scalar
        def _(act):
            act.sem_inc(act_ex, 2)
            with act.Fori(0, NG) as g:
                act.wait_ge(pe_xT, g + 1)
                act.copy(xnT[:], ps_t[:].rearrange("p (s q) -> p s q", s=GT)).then_inc(act_xT, 1)
                act.wait_ge(pe_qkv, g + 1)
                for s in range(GT):
                    last = act.copy(qk[:, :, s, :], banks[s][:, 0:2 * D].rearrange("p (k d) -> p k d", k=2))
                last.then_inc(act_qk, 1)
                for s in range(GT):
                    last = act.copy(v_all[:, bass.ds(g * GT + s, 1), :], banks[s][:, 2 * D:3 * D].unsqueeze(1))
                last.then_inc(act_v, 1)
                act.wait_ge(pl_qr, 2 * g + 2)

            act.wait_ge(ld_c, 96)
            act.copy(ident_bf[:], ident[:]).then_inc(zeroed, 1)

            def put_T(h, p, kind, half, n):
                act.wait_ge(pe_tr, 6 * h + n + 1)
                act.copy(stackT[:, p, kind, 1024 * half:1024 * half + 1024], ps_t[:].bitcast(BF16)).then_inc(act_tr, 1)

            def first_T(h, p):
                for n, (kind, half) in enumerate(((1, 0), (1, 1), (0, 0), (0, 1))):
                    put_T(h, p, kind, half, n)

            def second_T(h, p):
                for half in range(2):
                    put_T(h, p, 0, half, 4 + half)

            def exps(h, p):
                with act.Fori(0, NG) as g:
                    for r in range(8):
                        n = h * 32 + g * 8 + r
                        act.wait_ge(pe_s, n + 1)
                        act.wait_ge(pe_pv, n + 1)
                        b = r % 2
                        for e in range(2):
                            last = act.activation(pex[:, b, e, :], ps_s[2 * b + e][:], ACT.Exp)
                        last.then_inc(act_ex, 1)

            first_T(0, 0)
            second_T(0, 0)
            with act.Fori(0, HEADS // 2 - 1) as i:
                for p in range(2):
                    first_T(2 * i + p + 1, 1 - p)
                    exps(2 * i + p, p)
                    second_T(2 * i + p + 1, 1 - p)
            first_T(HEADS - 1, 1)
            exps(HEADS - 2, 0)
            second_T(HEADS - 1, 1)
            exps(HEADS - 1, 1)
            for g in range(NG):
                act.wait_ge(pe_aT, g + 1)
                act.copy(aoT[:], ps_t[:].rearrange("p (s q) -> p s q", s=GT)).then_inc(act_aT, 1)

        @block.vector
        def _(dve):
            dve.sem_inc(dv_max, 2)
            dve.sem_inc(dv_os, 4)
            dve.sem_inc(dv_ao, 1)

            def norm_stats(k, src):
                for s in range(GT):
                    last = dve.bn_stats(st6[:, s, :], src[:, s, :])
                last.then_inc(dv_st, 1)
                dve.wait_ge(dv_st, k + 1).then_inc(own_dve, 1)
                for s in range(GT):
                    last = dve.bn_aggr(mv[:, s, :], st6[:, s, :])
                last.then_inc(dv_mv, 1)

            def normalise(k, src):
                dve.wait_ge(pl_rstd, k + 1)
                for s in range(GT):
                    last = dve.tensor_scalar(xn[:, s, :], src[:, s, :], mv[:, s, 0:1], rstd[:, s:s + 1], ALU.subtract, ALU.mult)
                last.then_inc(dv_xn, 1)

            with dve.Fori(0, NG) as g:
                dve.wait_ge(ld_x, 16 * g + 16)
                norm_stats(g, xg)
                normalise(g, xg)
                dve.wait_ge(ld_c, 96)
                dve.wait_ge(act_qk, g + 1)
                heads = lambda a: a.rearrange("p s (h d) -> p s h d", d=AD)
                for kind in range(2):
                    for a in range(2):
                        tab = rope[:, 2 * kind + 1, bass.ds(g * GT, GT), AD // 2 * a:AD // 2 * a + AD // 2]
                        dve.tensor_tensor(heads(t2[:, kind, :, :])[:, :, :, AD // 2 * a:AD // 2 * a + AD // 2],
                                          heads(qk[:, kind, :, :])[:, :, :, AD // 2 * (1 - a):AD // 2 * (1 - a) + AD // 2],
                                          tab.unsqueeze(2).broadcast_to([P, GT, HEADS, AD // 2]), ALU.mult).then_inc(dv_t2, 1)
                dve.wait_ge(pl_qr, 2 * g + 2)
                src = t1
                for i in range(3):
                    at = parts[:, :, i, bass.ds(g * GT, GT), :]
                    dve.tensor_copy(at, src[:] if i == 0 else rest[:, i - 1, :, :, :]).then_inc(dv_part, 1)
                    if i < 2:
                        dve.wait_ge(dv_part, 3 * g + i + 1)
                        dve.tensor_tensor(rest[:, i, :, :, :], src[:] if i == 0 else rest[:, i - 1, :, :, :], at,
                                          ALU.subtract).then_inc(dv_rest, 1)
                        dve.wait_ge(dv_rest, 2 * g + i + 1)

            def maxima_of(h, g):
                for e in range(16):
                    m = h * 64 + g * 16 + e
                    dve.wait_ge(pe_max, m + 1)
                    dve.tensor_reduce(maxima[:, bass.ds(g * GT + e // 4, 1), e % 4:e % 4 + 1], ps_max[e % 2][:], AX.X,
                                      ALU.max).then_inc(dv_max, 1)

            def negate(h, p):
                dve.wait_ge(dv_max, 64 * h + 66)
                dve.tensor_reduce(neg[:, 0, :], maxima[:], AX.X, ALU.max, negate=True).then_inc(dv_neg, 1)
                for i in range(3):
                    dve.wait_ge(dv_neg, 3 * h + i + 1)
                    at = stack[:, p, 0, :, 72 + i]
                    dve.tensor_copy(at, neg[:, i, :]).then_inc(dv_negp, 1)
                    if i < 2:
                        dve.wait_ge(dv_negp, 3 * h + i + 1)
                        dve.tensor_tensor(neg[:, i + 1, :], neg[:, i, :], at, ALU.subtract).then_inc(dv_neg, 1)

            def sums(h, g):
                dve.wait_ge(pe_pv, 32 * h + 8 * g + 10)
                dve.tensor_copy(osum[:, bass.ds(g, 1), :], ps_o[:].unsqueeze(1)).then_inc(dv_os, 1)

            def outputs(h):
                dve.wait_ge(pe_f, h + 1)
                both = ps_t[:, 0:NT * VW].rearrange("p (t c) -> p t c", t=NT)
                dve.reciprocal(rec[:], both[:, :, AD]).then_inc(dv_rec, 1)
                dve.wait_ge(dv_rec, h + 1)
                at = ao[:, :, bass.ds(h * AD, AD)] if not isinstance(h, int) else ao[:, :, h * AD:h * AD + AD]
                dve.tensor_tensor(at, both[:, :, 0:AD], rec[:].unsqueeze(2).broadcast_to([P, NT, AD]), ALU.mult).then_inc(dv_ao, 1)

            def head(h, p, more):
                with dve.Fori(0, NG) as g:
                    if more:
                        maxima_of(h + 1, g)
                    sums(h, g)
                if more:
                    negate(h + 1, 1 - p)
                outputs(h)

            with dve.Fori(0, NG) as g:
                maxima_of(0, g)
            negate(0, 0)
            with dve.Fori(0, HEADS // 2 - 1) as i:
                for p in range(2):
                    head(2 * i + p, p, True)
            head(HEADS - 2, 0, True)
            head(HEADS - 1, 1, False)
            for g in range(NG):
                dve.wait_ge(pe_y, g + 1)
                dve.wait_ge(pl_xb, g + 1)
                if g:
                    dve.wait_ge(st_o, 32 * g)
                dve.tensor_tensor(y[:], banks[0][:].rearrange("p (s d) -> p s d", s=GT), xg[:], ALU.add).then_inc(dv_y, 1)
                dve.wait_ge(dv_y, g + 1)
                norm_stats(FINAL + g, y)
                normalise(FINAL + g, y)

        @block.tensor
        def _(pe):
            pe.sem_inc(pe_pv, 2)
            pe.wait_ge(ld_c, 96)
            with pe.Fori(0, NG) as g:
                pe.wait_ge(dv_xn, g + 1)
                for s in range(GT):
                    last = pe.transpose(ps_t[:, P * s:P * s + P], xn[:, s, :], ident[:])
                last.then_inc(pe_xT, 1)
                pe.wait_ge(act_xT, g + 1)
                for s in range(GT):
                    last = pe.matmul(banks[s][:, 0:3 * D], xnT[:, s, :], wqkv[:], start=True, stop=True)
                last.then_inc(pe_qkv, 1)
                pe.wait_ge(act_v, g + 1)

            def transposes(h, p, kind, half):
                for t in range(8):
                    last = pe.transpose(ps_t[:].bitcast(BF16)[:, P * t:P * t + P], stack[:, p, kind, 8 * half + t, :], ident_bf[:])
                last.then_inc(pe_tr, 1)

            def first_T(h, p):
                pe.wait_ge(pl_stack, h + 1)
                for n, (kind, half) in enumerate(((1, 0), (1, 1), (0, 0), (0, 1))):
                    if n:
                        pe.wait_ge(act_tr, 6 * h + n)
                    elif not (isinstance(h, int) and h == 0):
                        pe.wait_ge(act_tr, 6 * h)
                    transposes(h, p, kind, half)

            def second_T(h, p):
                pe.wait_ge(dv_negp, 3 * h + 3)
                for half in range(2):
                    pe.wait_ge(act_tr, 6 * h + 4 + half)
                    transposes(h, p, 0, half)

            def scores_for_max(h, p, g, e):
                m = h * 64 + g * 16 + e
                pe.wait_ge(dv_max, m + 1)
                pe.matmul(ps_max[e % 2][:], stackT[:, p, 0, bass.ds((g * GT + e // 4) * P, P)],
                          stackT[:, p, 1, GQ * (e % 4):GQ * (e % 4) + GQ], start=True, stop=True).then_inc(pe_max, 1)

            def scores(h, p, g, r):
                n = h * 32 + g * 8 + r
                pe.wait_ge(act_ex, n + 1)
                for e in range(2):
                    kt = 2 * r + e
                    last = pe.matmul(ps_s[2 * (r % 2) + e][:], stackT[:, p, 1, P * kt:P * kt + P],
                                     stackT[:, p, 0, bass.ds(g * GQ, GQ)], start=True, stop=True)
                last.then_inc(pe_s, 1)

            def values(h, p, g, r):
                n = h * 32 + g * 8 + r
                pe.wait_ge(act_ex, n + 3)
                if r == 0:
                    pe.wait_ge(dv_os, 4 * h + g + 4)
                for e in range(2):
                    kt = 2 * r + e
                    c = 32 * (kt % 4)
                    last = pe.matmul(ps_o[c:c + VW, :], v_head[:, p, kt, :], pex[:, r % 2, e, :], start=(kt < 4), stop=(kt >= 12),
                                     tile_position=(0, c))
                last.then_inc(pe_pv, 1)

            def head(h, p, more):
                pe.wait_ge(act_tr, 6 * h + 6).then_inc(own_pe, 1)
                pe.wait_ge(pl_vh, h + 1).then_inc(own_pe, 1)
                with pe.Fori(0, NG) as g:
                    for r in range(8):
                        scores(h, p, g, r)
                        if r == 7:
                            values(h, p, g, 6)
                        if more:
                            for e in range(2):
                                scores_for_max(h + 1, 1 - p, g, 2 * r + e)
                        if 1 <= r < 7:
                            values(h, p, g, r - 1)
                    values(h, p, g, 7)
                if more:
                    second_T(h + 1, 1 - p)
                    pe.wait_ge(act_tr, 6 * h + 12)
                pe.wait_ge(dv_os, 4 * h + 8)
                for t in range(NT):
                    last = pe.matmul(ps_t[:, VW * t:VW * t + VW], osum[:, t // GT, P * (t % GT):P * (t % GT) + P], fold[:],
                                     start=True, stop=True)
                last.then_inc(pe_f, 1)

            pe.wait_ge(zeroed, 6)
            first_T(0, 0)
            pe.wait_ge(act_tr, 4)
            with pe.Fori(0, NG) as g:
                for e in range(16):
                    scores_for_max(0, 0, g, e)
            second_T(0, 0)
            with pe.Fori(0, HEADS // 2 - 1) as i:
                for p in range(2):
                    h = 2 * i + p
                    pe.wait_ge(dv_ao, h + 1)
                    first_T(h + 1, 1 - p)
                    pe.wait_ge(act_tr, 6 * h + 10).then_inc(own_pe, 1)
                    head(h, p, True)
            pe.wait_ge(dv_ao, HEADS - 1)
            first_T(HEADS - 1, 1)
            pe.wait_ge(act_tr, 6 * HEADS - 2)
            head(HEADS - 2, 0, True)
            pe.wait_ge(dv_ao, HEADS)
            head(HEADS - 1, 1, False)
            pe.wait_ge(dv_ao, HEADS + 1)
            for g in range(NG):
                for s in range(GT):
                    last = pe.transpose(ps_t[:, P * s:P * s + P], ao[:, g * GT + s, :], ident[:])
                last.then_inc(pe_aT, 1)
                pe.wait_ge(act_aT, g + 1)
                if g:
                    pe.wait_ge(dv_y, g)
                for s in range(GT):
                    last = pe.matmul(banks[0][:, P * s:P * s + P], aoT[:, s, :], wout[:], start=True, stop=True)
                last.then_inc(pe_y, 1)


def local_stack(nc, tag, w, consts, xf, xa):
    with ExitStack() as ctx:
        sems, per_layer, ahead = [], {}, {}

        def sb(name, shape, dt=F32):
            return ctx.enter_context(nc.sbuf_tensor(f"{tag}_{name}", shape, dt))

        def sem(name, each=0, start=0):
            s = ctx.enter_context(nc.semaphore(f"{tag}_{name}"))
            sems.append(s)
            per_layer[s.num], ahead[s.num] = each, start
            return s

        def upto(s, L, n, by=1):
            return L * per_layer[s.num] + (n * by + (by + ahead[s.num]))

        banks = [ctx.enter_context(nc.psum_tensor(f"{tag}_bank{i}", [P, 512], F32)) for i in range(8)]
        ps_qk = banks[0:2]
        ps_v = banks[2]
        ps_qkT = banks[3]
        ps_pT = banks[4]
        ps_s = banks[5]
        ps_o = banks[6]
        ps_x = banks[7]
        ps_h = [[banks[0], banks[1], banks[7]], [banks[3], banks[4], banks[5]]]
        ps_fT = banks[2]
        ps_f = banks[6]

        wqkv = sb("wqkv", [P, 3 * INNER])
        wo = sb("wo", [P, PAIRS, D])
        w1 = sb("w1", [P, 2 * HID])
        w2 = sb("w2", [P, 3, D])
        ln_g = sb("ln_g", [P, 1])
        ln_b = sb("ln_b", [P, 1])
        b1 = sb("b1", [P, 6])
        b2 = sb("b2", [P, D])
        qk_scales = sb("qk_scales", [P, 2, DH])
        rope0 = sb("rope0", [P, 4, NT, DH])
        rope = sb("rope", [P, 4, NT, DH])
        mask = sb("mask", [P, 2, 4 * KEYS])
        mask_bf = sb("mask_bf", [P, 2, 4 * KEYS], BF16)
        ident = sb("ident", [P, P])
        ident_bf = sb("ident_bf", [P, P], BF16)
        minus_half = sb("minus_half", [P, 8])

        xs = sb("xs", [P, 2, D])
        xT = sb("xT", [P, 2, P])
        sq = sb("sq", [P, 2, 512])
        ss = sb("ss", [P, 2, 8])
        sg = sb("sg", [P, 2, 8])
        rn = sb("rn", [P, 2, 8])
        qh = sb("qh", [P, 2, 512])
        t1 = sb("t1", [P, 2, 512])
        t2 = sb("t2", [P, 2, 512])
        qr = sb("qr", [P, 2, 512])
        qbd = sb("qbd", [P, PAIRS, 2, 2 * BLK])
        kT = sb("kT", [P, PAIRS, WINDOW + P])
        vt = sb("vt", [P, 2, INNER])
        vw = sb("vw", [P, 2, 2, INNER])
        nmx = sb("nmx", [P, 2, 4])
        ex = sb("ex", [P, 2, 4, KEYS])
        sm = sb("sm", [P, 2, 4])
        rd = sb("rd", [P, 2, 4])
        pn = sb("pn", [P, 2, 4, KEYS])
        pT = sb("pT", [P, 2, 4, P])
        aT = sb("aT", [P, 2, PAIRS, P])
        xr = sb("xr", [P, 2, D])
        fx = sb("fx", [P, 2, FT, D])
        fxs = sb("fxs", [P, 2, FT, D])
        fy = sb("fy", [P, 2, FT, D])
        st6 = sb("st6", [P, 2, FT, 6])
        mv = sb("mv", [P, 2, FT, 2])
        var = sb("var", [P, 2, FT])
        rstd = sb("rstd", [P, 2, FT])
        xn = sb("xn", [P, 2, FT, D])
        xnT = sb("xnT", [P, 2, FQ])
        gl = sb("gl", [P, 2, 3, FQ])
        ag = sb("ag", [P, 2, 3, FQ])

        STEPS = 4 * NT
        ld_const, zeroed, act_const = sem("ld_const"), sem("zeroed"), sem("act_const")
        ld_wqkv, ld_wo, ld_wf = sem("ld_wqkv", 48), sem("ld_wo", 16), sem("ld_wf", 13 * 16)
        ld_x = [sem(f"ld_x{p}", 32 * NT // 2) for p in range(2)]
        ld_r = [sem(f"ld_r{p}", 16 * NT // 2) for p in range(2)]
        ld_vw = [sem(f"ld_vw{p}", 48 * NT // 2, 48) for p in range(2)]
        ld_f = [sem(f"ld_f{p}", 16 * NF // 2) for p in range(2)]
        ld_fs = [sem(f"ld_fs{p}", 32 * NF // 2) for p in range(2)]
        st_a, st_f = sem("st_a", 16 * NT, 32), sem("st_f", 16 * NF, 16 * NF)
        pe_xT, act_xT, pe_Wo, dv_y = sem("pe_xT", NT, 2), sem("act_xT", NT), sem("pe_Wo", NT, 2), sem("dv_y", NT, 4)
        pe_v, act_v = sem("pe_v", 2 * NT, 3), sem("act_v", 2 * NT, 1)
        pe_qkv, act_sq, dv_ssq = sem("pe_qkv", STEPS), sem("act_sq", STEPS), sem("dv_ssq", STEPS, 2)
        pl_sg, pl_rn, dv_qh, dv_t2, pl_qr = (sem("pl_sg", STEPS), sem("pl_rn", STEPS, 2), sem("dv_qh", STEPS, 2),
                                             sem("dv_t2", STEPS), sem("pl_qr", STEPS, 2))
        pe_qkT, act_kprev, act_qk = sem("pe_qkT", STEPS, 2), sem("act_kprev", STEPS // 2), sem("act_qk", STEPS, 1)
        pe_s, dv_max, act_exp = sem("pe_s", STEPS, 4), sem("dv_max", STEPS), sem("act_exp", STEPS, 2)
        dv_rd, dv_pn, pe_pT, act_pT = sem("dv_rd", STEPS), sem("dv_pn", STEPS, 2), sem("pe_pT", STEPS, 2), sem("act_pT", STEPS, 1)
        pe_o, act_aT = sem("pe_o", STEPS, 8), sem("act_aT", STEPS, 1)
        dv_kzero, pl_rope = sem("dv_kzero", 1, 1), sem("pl_rope", 6)
        dv_st, dv_mv, pl_var, pl_rstd, dv_xn = (sem("dv_st", NF), sem("dv_mv", NF), sem("pl_var", NF), sem("pl_rstd", NF),
                                                sem("dv_xn", NF, 2))
        pl_b2, pe_fT, act_fT, pe_out, dv_fy = (sem("pl_b2", NF), sem("pe_fT", NF, 2), sem("act_fT", NF, 1), sem("pe_out", NF, 2),
                                               sem("dv_fy", NF, 2))
        pe_h, act_gelu, dv_ag = sem("pe_h", 3 * NF, 6), sem("act_gelu", 3 * NF), sem("dv_ag", 3 * NF, 6)
        own = {e: sem(f"own_{e}") for e in ("pe", "dve", "pool", "sp")}

        def real(t, c, lag):
            return not isinstance(t, int) or 0 <= 4 * t + c - lag < STEPS

        def tiles(eng, body, L, last):
            for t in range(3):
                body(L, t, t % 2)
            with eng.Fori(0, (NT - 4) // 2) as i:
                for q in range(2):
                    body(L, 2 * i + (3 + q), (3 + q) % 2)
            for t in range(NT - 1, last):
                body(L, t, t % 2)

        def groups(eng, body, L):
            for m in range(2):
                body(L, m, m % 2)
            with eng.Fori(0, (NF - 4) // 2) as i:
                for q in range(2):
                    body(L, 2 * i + (2 + q), q)
            for m in range(NF - 2, NF + 2):
                body(L, m, m % 2)

        def row(t):
            return slice(t, t + 1) if isinstance(t, int) else bass.ds(t, 1)

        def rows(dram, first, n):
            return dram[bass.ds(first, n), :]

        KIND = [0, 1, 0, 1]
        HALF = [0, 0, 1, 1]

        block = ctx.enter_context(clearing(nc, sems))

        def load_xs(eng, L, t, p):
            eng.wait_ge(st_f, upto(st_f, L - 1, t >> 1, 16))
            eng.dma_start(xs[:, p, 0:64], rows(xf, t * P + 1, P)[:, 0:64]).then_inc(ld_x[p], 16)
            eng.dma_start(xs[:, p, 64:128], rows(xf, t * P, P)[:, 64:128]).then_inc(ld_x[p], 16)

        @block.sync
        def _(sp):
            for s in (st_a, st_f, ld_vw[0], ld_vw[1]):
                sp.sem_inc(s, ahead[s.num])
            sp.dma_start(ident[:], consts["ident"]).then_inc(ld_const, 16)
            sp.dma_start(rope0[:], consts["rope"].rearrange("p (k t d) -> p k t d", k=4, t=NT)).then_inc(ld_const, 16)
            sp.dma_start(mask[:], consts["mask"].rearrange("p (i c) -> p i c", i=2)).then_inc(ld_const, 16)

            def load_wqkv(layer):
                sp.dma_start(wqkv[:], w["Wqkv"][bass.ds(layer, 1), :, :].rearrange("l d n -> (l d) n")).then_inc(ld_wqkv, 16)
                for n, name in enumerate(("q_scale", "k_scale")):
                    sp.dma_start(qk_scales[:, n, :], w[name][bass.ds(layer, 1), :].broadcast_to([P, DH])).then_inc(ld_wqkv, 16)

            def load_wo(layer):
                sp.dma_start(wo[:], w["Wo"][bass.ds(layer, 1), :, :].rearrange("l (j p) n -> p (l j) n", p=P)).then_inc(ld_wo, 16)

            def load_wf(layer):
                sp.dma_start(w1[:], w["W1"][bass.ds(layer, 1), :, :].rearrange("l d n -> (l d) n")).then_inc(ld_wf, 16)
                col = lambda a: a.rearrange("l (n o) -> (l n) o", o=1)
                for c, (f0, m) in enumerate(HCH):
                    sp.dma_start(w2[0:m, c, :], w["W2"][bass.ds(layer, 1), f0:f0 + m, :].rearrange("l f n -> (l f) n")).then_inc(ld_wf, 16)
                    sp.dma_start(b1[0:m, c:c + 1], col(w["b1"][bass.ds(layer, 1), f0:f0 + m])).then_inc(ld_wf, 16)
                    sp.dma_start(b1[0:m, 3 + c:4 + c], col(w["b1"][bass.ds(layer, 1), HID + f0:HID + f0 + m])).then_inc(ld_wf, 16)
                sp.dma_start(ln_g[:], col(w["ln_g"][bass.ds(layer, 1), :])).then_inc(ld_wf, 16)
                sp.dma_start(ln_b[:], col(w["ln_b"][bass.ds(layer, 1), :])).then_inc(ld_wf, 16)
                sp.dma_start(b2[:], w["b2"][bass.ds(layer, 1), :].broadcast_to([P, D])).then_inc(ld_wf, 16)

            def tile(L, t, q):
                known = isinstance(t, int)
                if not known or 0 <= t - 3 < NT:
                    sp.wait_ge(dv_y, upto(dv_y, L, t - 3)).then_inc(own["sp"], 1)
                    sp.wait_ge(st_a, upto(st_a, L, t - 4, 16)).then_inc(own["sp"], 1)
                    sp.dma_start(rows(xa, (t - 3) * P + 1, P), xr[:, 1 - q, :]).then_inc(st_a, 16)
                if not known or t + 1 < NT:
                    sp.wait_ge(pe_xT, upto(pe_xT, L, t - 1)).then_inc(own["sp"], 1)
                    load_xs(sp, L, t + 1, 1 - q)
                if not known or 0 <= t - 1 < NT:
                    sp.wait_ge(act_v, upto(act_v, L, 2 * t - 1)).then_inc(own["sp"], 1)
                    sp.wait_ge(pe_o, upto(pe_o, L, 4 * t - 9))
                    p = 1 - q
                    sp.dma_start(vw[0:32, p, 0, :], vt[96:128, 1 - p, :]).then_inc(ld_vw[p], 16)
                    sp.dma_start(vw[32:96, p, 0, :], vt[0:64, p, :]).then_inc(ld_vw[p], 16)
                    sp.dma_start(vw[0:96, p, 1, :], vt[32:128, p, :]).then_inc(ld_vw[p], 16)
                if not known or 0 <= t - 2 < NT:
                    sp.wait_ge(st_a, upto(st_a, L, t - 4, 16)).then_inc(own["sp"], 1)
                    sp.dma_start(xr[:, q, :], rows(xf, (t - 2) * P + 1, P)).then_inc(ld_r[q], 16)

            def load_shifted(L, m, q):
                sp.wait_ge(st_a, upto(st_a, L, 2 * m + 1, 16)).then_inc(own["sp"], 1)
                sp.wait_ge(dv_xn, upto(dv_xn, L, m - 2))
                r = lambda first: rows(xa, first, FQ).rearrange("(s p) d -> p s d", p=P)
                sp.dma_start(fxs[:, q, :, 0:64], r(m * FQ + 1)[:, :, 0:64]).then_inc(ld_fs[q], 16)
                sp.dma_start(fxs[:, q, :, 64:128], r(m * FQ)[:, :, 64:128]).then_inc(ld_fs[q], 16)

            def group(L, m, q):
                known = isinstance(m, int)
                if not known or m + 1 < NF:
                    load_shifted(L, m + 1, 1 - q)
                if not known or m < NF:
                    sp.wait_ge(dv_fy, upto(dv_fy, L, m - 2)).then_inc(own["sp"], 1)
                    sp.dma_start(fx[:, q, :, :], rows(xa, m * FQ + 1, FQ).rearrange("(s p) d -> p s d", p=P)).then_inc(ld_f[q], 16)
                if not known or m >= 2:
                    sp.wait_ge(dv_fy, upto(dv_fy, L, m - 2)).then_inc(own["sp"], 1)
                    sp.wait_ge(st_f, upto(st_f, L, m - 3, 16))
                    sp.dma_start(rows(xf, (m - 2) * FQ + 1, FQ).rearrange("(s p) d -> p s d", p=P), fy[:, q, :, :]).then_inc(st_f, 16)

            load_wqkv(0)
            load_wo(0)
            load_wf(0)
            sp.wait_ge(zeroed, 6)
            with sp.Fori(0, DEPTH) as L:
                tiles(sp, tile, L, NT + 1)
                sp.wait_ge(pe_v, upto(pe_v, L, 2 * NT - 1))
                sp.wait_ge(pl_rope, upto(pl_rope, L, 5))
                load_wqkv((L + 1) % DEPTH)
                for t in range(NT + 1, NT + 3):
                    tile(L, t, t % 2)
                load_shifted(L, 0, 0)
                groups(sp, group, L)
                load_wo((L + 1) % DEPTH)
                sp.wait_ge(st_f, upto(st_f, L, NF - 1, 16)).then_inc(own["sp"], 1)
                load_wf((L + 1) % DEPTH)
            sp.wait_ge(ld_wqkv, 48 * (DEPTH + 1))
            sp.wait_ge(ld_wo, 16 * (DEPTH + 1))
            sp.wait_ge(ld_wf, 13 * 16 * (DEPTH + 1))

        @block.gpsimd
        def _(pool):
            for s in (pl_rn, pl_qr):
                pool.sem_inc(s, ahead[s.num])
            pool.memset(minus_half[:], -0.5).then_inc(zeroed, 1)
            for buf in (qbd, kT, vt, vw, pT):
                pool.memset(buf[:], 0.0).then_inc(zeroed, 1)

            def fold_rope(n):
                pool.wait_ge(ld_wqkv, upto(ld_wqkv, n, 0, 48))
                for kind in range(2):
                    whole = qk_scales[:, kind, :].unsqueeze(1).broadcast_to([P, NT, DH])
                    halves = qk_scales[:, kind, :].rearrange("p (a b) -> p a b", a=2)[:, ::-1, :]
                    pool.tensor_tensor(rope[:, 2 * kind, :, :], rope0[:, 2 * kind, :, :], whole, ALU.mult).then_inc(pl_rope, 1)
                    for a in range(2):
                        sl = slice(a * 32, a * 32 + 32)
                        pool.tensor_tensor(rope[:, 2 * kind + 1, :, sl], rope0[:, 2 * kind + 1, :, sl],
                                           halves[:, a, :].unsqueeze(1).broadcast_to([P, NT, 32]),
                                           ALU.mult).then_inc(pl_rope, 1)

            def tile(L, t, q):
                for c in range(4):
                    n, b = 4 * t + c, c % 2
                    if real(t, c, 1):
                        pool.wait_ge(dv_t2, upto(dv_t2, L, n - 1))
                        pool.wait_ge(pe_qkT, upto(pe_qkT, L, n - 3))
                        pool.tensor_tensor(qr[:, 1 - b, :], t1[:, 1 - b, :], t2[:, 1 - b, :], ALU.add).then_inc(pl_qr, 1)
                    if real(t, c, 0):
                        pool.wait_ge(dv_ssq, upto(dv_ssq, L, n)).then_inc(own["pool"], 1)
                        pool.tensor_scalar(sg[:, b, :], ss[:, b, :], 1e-24, None, ALU.max).then_inc(pl_sg, 1)
                        pool.wait_ge(pl_sg, upto(pl_sg, L, n))
                        pool.wait_ge(dv_qh, upto(dv_qh, L, n - 2))
                        pool.tensor_tensor(rn[:, b, :], sg[:, b, :], minus_half[:], ALU.pow).then_inc(pl_rn, 1)

            def group(L, m, q):
                known = isinstance(m, int)
                if not known or m < NF:
                    pool.wait_ge(dv_mv, upto(dv_mv, L, m)).then_inc(own["pool"], 1)
                    pool.tensor_scalar(var[:, q, :], mv[:, q, :, 1], 1e-5, None, ALU.add).then_inc(pl_var, 1)
                    pool.wait_ge(pl_var, upto(pl_var, L, m))
                    pool.tensor_tensor(rstd[:, q, :], var[:, q, :], minus_half[:, 0:FT], ALU.pow).then_inc(pl_rstd, 1)
                if not known or 0 <= m - 1 < NF:
                    pool.wait_ge(ld_f[1 - q], upto(ld_f[1 - q], L, (m - 1) >> 1, 16))
                    pool.tensor_tensor(fx[:, 1 - q, :, :], fx[:, 1 - q, :, :], b2[:].unsqueeze(1).broadcast_to([P, FT, D]),
                                       ALU.add).then_inc(pl_b2, 1)

            pool.wait_ge(zeroed, 6)
            pool.wait_ge(ld_const, 48)
            fold_rope(0)
            with pool.Fori(0, DEPTH) as L:
                tiles(pool, tile, L, NT + 1)
                pool.wait_ge(dv_t2, upto(dv_t2, L, STEPS - 1))
                fold_rope(L + 1)
                pool.wait_ge(ld_wf, upto(ld_wf, L, 0, 13 * 16)).then_inc(own["pool"], 1)
                groups(pool, group, L)

        @block.scalar
        def _(act):
            for s in (act_v, act_exp, act_qk, act_pT, act_aT, act_fT):
                act.sem_inc(s, ahead[s.num])

            def put_xT(L, t, p):
                act.wait_ge(pe_xT, upto(pe_xT, L, t))
                act.wait_ge(pe_v, upto(pe_v, L, 2 * t - 3))
                act.copy(xT[:, p, :], ps_x[:, 0:P]).then_inc(act_xT, 1)

            def tile(L, t, q):
                for c in range(4):
                    n, b = 4 * t + c, c % 2
                    if real(t, c, 0):
                        act.wait_ge(pe_qkv, upto(pe_qkv, L, n))
                        act.wait_ge(dv_ssq, upto(dv_ssq, L, n - 2))
                        act.activation(sq[:, b, :], ps_qk[b][:], ACT.Square).then_inc(act_sq, 1)
                    if real(t, c, 6):
                        act.wait_ge(pe_pT, upto(pe_pT, L, n - 6))
                        act.wait_ge(pe_o, upto(pe_o, L, n - 8))
                        act.copy(pT[0:KEYS, b, :, :], ps_pT[0:KEYS, :].rearrange("p (u q) -> p u q", u=4)).then_inc(act_pT, 1)
                    if real(t, c, 4):
                        act.wait_ge(dv_max, upto(dv_max, L, n - 4))
                        act.wait_ge(dv_pn, upto(dv_pn, L, n - 6))
                        for u in range(4):
                            last = act.activation(ex[:, b, u, :], ps_s[:, KEYS * u:KEYS * u + KEYS], ACT.Exp, bias=nmx[:, b, u:u + 1],
                                                  accum_out=sm[:, b, u:u + 1])
                        last.then_inc(act_exp, 1)
                    if real(t, c, 2):
                        tj, cj = t + (c - 2) // 4, (c - 2) % 4
                        pairs = slice(4 * HALF[cj], 4 * HALF[cj] + 4)
                        act.wait_ge(pe_qkT, upto(pe_qkT, L, n - 2))
                        act.wait_ge(pe_s, upto(pe_s, L, 4 * tj - 3 + 2 * HALF[cj]))
                        if KIND[cj] == 0:
                            for h in range(2):
                                r = slice(64 * h, 64 * h + 64)
                                last = act.copy(qbd[r, pairs, :, 64 * h:64 * h + 64],
                                                ps_qkT[r, :].rearrange("p (j b q) -> p j b q", j=4, b=2))
                            last.then_inc(act_qk, 1)
                        else:
                            act.copy(kT[:, pairs, 0:WINDOW], kT[:, pairs, P:P + WINDOW]).then_inc(act_kprev, 1)
                            act.wait_ge(act_kprev, upto(act_kprev, L, 2 * tj + HALF[cj]))
                            act.copy(kT[:, pairs, WINDOW:], ps_qkT[:].rearrange("p (j q) -> p j q", j=4)).then_inc(act_qk, 1)
                    if real(t, c, 7):
                        tj, g = t + (c - 7) // 4, (c - 7) % 4
                        p = (q + (c - 7) // 4) % 2
                        act.wait_ge(pe_o, upto(pe_o, L, n - 7))
                        act.wait_ge(pe_Wo, upto(pe_Wo, L, tj - 2))
                        for h in range(2):
                            r = slice(64 * h, 64 * h + 64)
                            last = act.copy(aT[r, p, 2 * g:2 * g + 2, :].rearrange("p j (b q) -> p (j b) q", b=2),
                                            ps_o[r, :].rearrange("p (u q) -> p u q", u=4)[:, :, 64 * h:64 * h + 64])
                        last.then_inc(act_aT, 1)
                    if c % 2 and real(t, c, 0):
                        half = c // 2
                        act.wait_ge(pe_v, upto(pe_v, L, 2 * t + half))
                        act.wait_ge(ld_vw[1 - q], upto(ld_vw[1 - q], L, (t - 1) >> 1, 48))
                        act.copy(vt[:, q, 512 * half:512 * half + 512], ps_v[:]).then_inc(act_v, 1)
                    if c == 2 and real(t + 1, 0, 0):
                        put_xT(L, t + 1, 1 - q)

            def group(L, m, q):
                known = isinstance(m, int)
                if not known or 0 <= m - 1 < NF:
                    for c, (_, f) in enumerate(HCH):
                        act.wait_ge(pe_h, upto(pe_h, L, 3 * m - 3 + c))
                        act.wait_ge(dv_ag, upto(dv_ag, L, 3 * m - 9 + c))
                        act.activation(gl[0:f, 1 - q, c, :], ps_h[1 - q][c][0:f, 0:FQ], ACT.Gelu,
                                       bias=b1[0:f, 3 + c:4 + c]).then_inc(act_gelu, 1)
                if not known or m < NF:
                    act.wait_ge(pe_fT, upto(pe_fT, L, m))
                    act.wait_ge(pe_h, upto(pe_h, L, 3 * m - 4))
                    act.activation(xnT[:, q, :], ps_fT[:, 0:FQ], ACT.Identity, bias=ln_b[:], scale=ln_g[:]).then_inc(act_fT, 1)

            act.wait_ge(ld_const, 48)
            act.copy(ident_bf[:], ident[:]).then_inc(act_const, 1)
            act.copy(mask_bf[:], mask[:]).then_inc(act_const, 1)
            act.wait_ge(zeroed, 6)
            with act.Fori(0, DEPTH) as L:
                load_xs(act, L, 0, 0)
                put_xT(L, 0, 0)
                act.wait_ge(dv_kzero, upto(dv_kzero, L, -1))
                tiles(act, tile, L, NT + 2)
                act.wait_ge(ld_wf, upto(ld_wf, L, 0, 13 * 16))
                groups(act, group, L)

        @block.vector
        def _(dve):
            for s in (dv_ssq, dv_qh, dv_y, dv_pn, dv_kzero, dv_xn, dv_fy, dv_ag):
                dve.sem_inc(s, ahead[s.num])
            heads = lambda a: a.rearrange("p (h d) -> p h d", h=8)
            split = lambda a: a.rearrange("p (h a b) -> p h a b", h=8, a=2)

            def tile(L, t, q):
                for c in range(4):
                    n, b = 4 * t + c, c % 2
                    if real(t, c, 5):
                        dve.wait_ge(act_exp, upto(act_exp, L, n - 5))
                        dve.reciprocal(rd[:, 1 - b, :], sm[:, 1 - b, :]).then_inc(dv_rd, 1)
                        dve.wait_ge(dv_rd, upto(dv_rd, L, n - 5))
                        dve.wait_ge(pe_pT, upto(pe_pT, L, n - 7))
                        dve.tensor_tensor(pn[:, 1 - b, :, :], ex[:, 1 - b, :, :],
                                          rd[:, 1 - b, :].unsqueeze(2).broadcast_to([P, 4, KEYS]), ALU.mult).then_inc(dv_pn, 1)
                    if real(t, c, 0):
                        dve.wait_ge(act_sq, upto(act_sq, L, n))
                        dve.wait_ge(pl_rn, upto(pl_rn, L, n - 2))
                        dve.tensor_reduce(ss[:, b, :], heads(sq[:, b, :]), AX.X, ALU.add).then_inc(dv_ssq, 1)
                    if real(t, c, 1):
                        dve.wait_ge(pl_rn, upto(pl_rn, L, n - 1))
                        dve.tensor_tensor(heads(qh[:, 1 - b, :]), heads(ps_qk[1 - b][:]),
                                          rn[:, 1 - b, :].unsqueeze(2).broadcast_to([P, 8, DH]), ALU.mult).then_inc(dv_qh, 1)
                    if real(t, c, 4):
                        dve.wait_ge(pe_s, upto(pe_s, L, n - 4))
                        dve.wait_ge(act_exp, upto(act_exp, L, n - 6))
                        dve.tensor_reduce(nmx[:, b, :], ps_s[:, 0:4 * KEYS].rearrange("p (u c) -> p u c", u=4), AX.X, ALU.max,
                                          negate=True).then_inc(dv_max, 1)
                    if real(t, c, 1):
                        tj, cj = t + (c - 1) // 4, (c - 1) % 4
                        dve.wait_ge(dv_qh, upto(dv_qh, L, n - 1))
                        dve.wait_ge(pl_qr, upto(pl_qr, L, n - 3))
                        dve.tensor_tensor(heads(t1[:, 1 - b, :]), heads(qh[:, 1 - b, :]),
                                          rope[:, 2 * KIND[cj], row(tj), :].broadcast_to([P, 8, DH]), ALU.mult)
                        dve.tensor_tensor(split(t2[:, 1 - b, :]), split(qh[:, 1 - b, :])[:, :, ::-1, :],
                                          rope[:, 2 * KIND[cj] + 1, row(tj), :].broadcast_to([P, 8, DH]).rearrange(
                                              "p h (a b) -> p h a b", a=2), ALU.mult).then_inc(dv_t2, 1)
                    if c == 3 and real(t - 2, 0, 0):
                        dve.wait_ge(pe_Wo, upto(pe_Wo, L, t - 2))
                        dve.wait_ge(ld_r[q], upto(ld_r[q], L, (t - 2) >> 1, 16))
                        dve.tensor_tensor(xr[:, q, :], ps_x[:, P:2 * P], xr[:, q, :], ALU.add).then_inc(dv_y, 1)

            def group(L, m, q):
                known = isinstance(m, int)
                if not known or m < NF:
                    dve.wait_ge(ld_fs[q], upto(ld_fs[q], L, m >> 1, 32))
                    for s in range(FT):
                        last = dve.bn_stats(st6[:, q, s, :], fxs[:, q, s, :])
                    last.then_inc(dv_st, 1)
                    dve.wait_ge(dv_st, upto(dv_st, L, m)).then_inc(own["dve"], 1)
                    for s in range(FT):
                        last = dve.bn_aggr(mv[:, q, s, :], st6[:, q, s, :])
                    last.then_inc(dv_mv, 1)
                if not known or 0 <= m - 1 < NF:
                    for c, (_, f) in enumerate(HCH):
                        dve.wait_ge(act_gelu, upto(act_gelu, L, 3 * m - 3 + c))
                        dve.wait_ge(pe_out, upto(pe_out, L, m - 3))
                        dve.scalar_tensor_tensor(out=ag[0:f, 1 - q, c, :], in0=ps_h[1 - q][c][0:f, FQ:2 * FQ], scalar=b1[0:f, c:c + 1],
                                                 in1=gl[0:f, 1 - q, c, :], op0=ALU.add, op1=ALU.mult).then_inc(dv_ag, 1)
                if not known or m < NF:
                    dve.wait_ge(pl_rstd, upto(pl_rstd, L, m))
                    dve.wait_ge(pe_fT, upto(pe_fT, L, m - 2))
                    for s in range(FT):
                        last = dve.tensor_scalar(xn[:, q, s, :], fxs[:, q, s, :], mv[:, q, s, 0:1], rstd[:, q, s:s + 1],
                                                 ALU.subtract, ALU.mult)
                    last.then_inc(dv_xn, 1)
                if not known or m >= 2:
                    dve.wait_ge(pe_out, upto(pe_out, L, m - 2))
                    dve.wait_ge(pl_b2, upto(pl_b2, L, m - 2))
                    dve.wait_ge(st_f, upto(st_f, L, m - 4, 16))
                    dve.tensor_tensor(fy[:, q, :, :], ps_f[:, 0:FQ].rearrange("p (s d) -> p s d", s=FT), fx[:, q, :, :],
                                      ALU.add).then_inc(dv_fy, 1)

            dve.wait_ge(ld_const, 48)
            with dve.Fori(0, DEPTH) as L:
                dve.wait_ge(pl_rope, upto(pl_rope, L, 5)).then_inc(own["dve"], 1)
                tiles(dve, tile, L, NT + 2)
                dve.wait_ge(pe_s, upto(pe_s, L, STEPS - 1))
                dve.memset(kT[:, :, P:P + WINDOW], 0.0).then_inc(dv_kzero, 1)
                dve.wait_ge(ld_wf, upto(ld_wf, L, 0, 13 * 16)).then_inc(own["dve"], 1)
                groups(dve, group, L)

        @block.tensor
        def _(pe):
            for s in (pe_xT, pe_Wo, pe_v, pe_qkT, pe_s, pe_pT, pe_o, pe_fT, pe_out, pe_h):
                pe.sem_inc(s, ahead[s.num])

            def transpose_x(L, t, p):
                pe.wait_ge(ld_x[p], upto(ld_x[p], L, t >> 1, 32))
                pe.wait_ge(dv_y, upto(dv_y, L, t - 4))
                pe.transpose(ps_x[:, 0:P], xs[:, p, :], ident[:]).then_inc(pe_xT, 1)

            def tile(L, t, q):
                known = isinstance(t, int)
                for c in range(4):
                    n, b = 4 * t + c, c % 2
                    if real(t, c, 0):
                        pe.wait_ge(act_xT, upto(act_xT, L, t))
                        pe.wait_ge(dv_qh, upto(dv_qh, L, n - 2))
                        at = INNER * KIND[c] + 512 * HALF[c]
                        pe.matmul(ps_qk[b][:], xT[:, q, :], wqkv[:, at:at + 512], start=True, stop=True).then_inc(pe_qkv, 1)
                    if real(t, c, 6):
                        pe.wait_ge(dv_pn, upto(dv_pn, L, n - 6))
                        pe.wait_ge(act_pT, upto(act_pT, L, n - 7))
                        for u in range(4):
                            last = pe.transpose(ps_pT[0:KEYS, P * u:P * u + P], pn[:, b, u, :], ident[:])
                        last.then_inc(pe_pT, 1)
                    if real(t, c, 4):
                        g = c
                        pe.wait_ge(act_qk, upto(act_qk, L, 4 * t - (3 if g < 2 else 1)))
                        pe.wait_ge(act_exp, upto(act_exp, L, n - 5))
                        first = known and t == 1
                        pe.matmul(ps_s[:, 0:4 * KEYS], ident_bf[:], mask_bf[:, 0 if first else 1, :], start=True, stop=False)
                        for u in range(4):
                            j, blk = 2 * g + u // 2, u % 2
                            last = pe.matmul(ps_s[:, KEYS * u:KEYS * u + KEYS], qbd[:, j, blk, :], kT[:, j, BLK * blk:BLK * blk + KEYS],
                                             start=False, stop=(u == 3))
                        last.then_inc(pe_s, 1)
                    if real(t, c, 2):
                        pe.wait_ge(pl_qr, upto(pl_qr, L, n - 2))
                        pe.wait_ge(act_qk, upto(act_qk, L, n - 3))
                        for j in range(4):
                            last = pe.transpose(ps_qkT[:, P * j:P * j + P], qr[:, b, P * j:P * j + P], ident[:])
                        last.then_inc(pe_qkT, 1)
                    if real(t, c, 7):
                        tj, g = t + (c - 7) // 4, (c - 7) % 4
                        p = (q + (c - 7) // 4) % 2
                        pe.wait_ge(act_pT, upto(act_pT, L, n - 7))
                        pe.wait_ge(act_aT, upto(act_aT, L, n - 8))
                        if known and n == 7:
                            pe.wait_ge(dv_fy, upto(dv_fy, L - 1, NF - 1))
                        if g == 0:
                            pe.wait_ge(ld_vw[p], upto(ld_vw[p], L, tj >> 1, 48))
                        for u in range(4):
                            j, blk = 2 * g + u // 2, u % 2
                            last = pe.matmul(ps_o[:, P * u:P * u + P], vw[:, p, blk, P * j:P * j + P], pT[:, 1 - b, u, :],
                                             start=True, stop=True)
                        last.then_inc(pe_o, 1)
                    if c % 2 and real(t, c, 0):
                        half = c // 2
                        pe.wait_ge(act_v, upto(act_v, L, 2 * t + half - 1))
                        at = 2 * INNER + 512 * half
                        pe.matmul(ps_v[:], xT[:, q, :], wqkv[:, at:at + 512], start=True, stop=True).then_inc(pe_v, 1)
                    if c == 2 and real(t + 1, 0, 0):
                        transpose_x(L, t + 1, 1 - q)
                    if c == 3 and real(t - 2, 0, 0):
                        pe.wait_ge(act_aT, upto(act_aT, L, 4 * t - 5))
                        pe.wait_ge(act_xT, upto(act_xT, L, min(t + 1, NT - 1) if known else t + 1))
                        pe.wait_ge(dv_y, upto(dv_y, L, t - 3))
                        for j in range(PAIRS):
                            last = pe.matmul(ps_x[:, P:2 * P], aT[:, q, j, :], wo[:, j, :], start=(j == 0), stop=(j == PAIRS - 1))
                        last.then_inc(pe_Wo, 1)

            def group(L, m, q):
                known = isinstance(m, int)
                if not known or 0 <= m - 1 < NF:
                    pe.wait_ge(act_fT, upto(act_fT, L, m - 1))
                    for c, (f0, f) in enumerate(HCH):
                        pe.wait_ge(dv_ag, upto(dv_ag, L, 3 * m - 9 + c))
                        pe.matmul(ps_h[1 - q][c][0:f, 0:FQ], w1[:, HID + f0:HID + f0 + f], xnT[:, 1 - q, :], start=True, stop=True)
                        pe.matmul(ps_h[1 - q][c][0:f, FQ:2 * FQ], w1[:, f0:f0 + f], xnT[:, 1 - q, :], start=True,
                                  stop=True).then_inc(pe_h, 1)
                if not known or m < NF:
                    pe.wait_ge(dv_xn, upto(dv_xn, L, m))
                    pe.wait_ge(act_fT, upto(act_fT, L, m - 1))
                    for s in range(FT):
                        last = pe.transpose(ps_fT[:, P * s:P * s + P], xn[:, q, s, :], ident[:])
                    last.then_inc(pe_fT, 1)
                if not known or m >= 2:
                    pe.wait_ge(dv_ag, upto(dv_ag, L, 3 * m - 4))
                    pe.wait_ge(dv_fy, upto(dv_fy, L, m - 3))
                    for s in range(FT):
                        for c, (_, f) in enumerate(HCH):
                            last = pe.matmul(ps_f[:, P * s:P * s + P], ag[0:f, q, c, P * s:P * s + P], w2[0:f, c, :],
                                             start=(c == 0), stop=(c == 2))
                    last.then_inc(pe_out, 1)

            pe.wait_ge(ld_const, 48)
            pe.wait_ge(act_const, 2)
            pe.wait_ge(zeroed, 6)
            with pe.Fori(0, DEPTH) as L:
                transpose_x(L, 0, 0)
                pe.wait_ge(ld_wqkv, upto(ld_wqkv, L, 0, 48))
                pe.wait_ge(ld_wo, upto(ld_wo, L, 0, 16)).then_inc(own["pe"], 1)
                tiles(pe, tile, L, NT + 2)
                pe.wait_ge(dv_y, upto(dv_y, L, NT - 1))
                pe.wait_ge(ld_wf, upto(ld_wf, L, 0, 13 * 16)).then_inc(own["pe"], 1)
                groups(pe, group, L)


def linear_attention(nc, tag, x_in, w, consts, x_out, xf):
    with ExitStack() as ctx:
        sems = []

        def sb(name, shape, dt=F32):
            return ctx.enter_context(nc.sbuf_tensor(f"{tag}_{name}", shape, dt))

        def sem(name):
            sems.append(ctx.enter_context(nc.semaphore(f"{tag}_{name}")))
            return sems[-1]

        banks = [ctx.enter_context(nc.psum_tensor(f"{tag}_bank{i}", [P, 512], F32)) for i in range(8)]
        ps_t = banks[4]
        ps_qk = banks[5:7]
        ps_kv = banks[7]

        GQ = GT * P
        HG = HEADS // HQ
        wqkv = sb("wqkv", [P, 3, D])
        wout = sb("wout", [P, D])
        bqkv = sb("bqkv", [P, 3, D])
        bout = sb("bout", [P, D])
        ident = sb("ident", [P, P])
        own_head = sb("own_head", [P, HQ * AD + HQ])
        proj_rows = sb("proj_rows", [P, HG, D])
        proj = sb("proj", [P, HEADS * FEATS])
        half = sb("half", [P, GT * 2 * HEADS])
        minus_half = sb("minus_half", [P, GT])
        xg = sb("xg", [P, GT, D])
        yg = sb("yg", [P, GT, D])
        x2 = sb("x2", [P, NT, D])
        st6 = sb("st6", [P, GT, 6])
        mv = sb("mv", [P, GT, 2])
        var = sb("var", [P, GT])
        rstd = sb("rstd", [P, GT])
        xn = sb("xn", [P, GT, D])
        xnT = sb("xnT", [P, GT, P])
        qk = sb("qk", [P, GT, 2, D])
        sq = sb("sq", [P, GT, 2, D])
        ss = sb("ss", [P, GT * 2 * HEADS])
        norm = sb("norm", [P, GT * 2 * HEADS])
        rn = sb("rn", [P, GT * 2 * HEADS])
        qkn = sb("qkn", [P, GT, 2, D])
        qkT = sb("qkT", [P, 2, GQ])
        v_one = sb("v_one", [P, GT, HG, HQ * AD + 1])
        kp = sb("kp", [P, GT, HEADS * FEATS])
        qp = sb("qp", [P, HG, N])
        kv = sb("kv", [P, HG, HQ * AD + 1])
        kvd = sb("kvd", [P, HG, HQ * AD + HQ])
        nrm = sb("nrm", [P, GT, HEADS])
        rec = sb("rec", [P, GT, HEADS])
        ao = sb("ao", [P, GT, D])
        aoT = sb("aoT", [P, GT, P])
        y = sb("y", [P, GT, D])

        ld_c, ld_p, ld_x, st_o, zeroed = sem("ld_c"), sem("ld_p"), sem("ld_x"), sem("st_o"), sem("zeroed")
        pe_proj, act_proj = sem("pe_proj"), sem("act_proj")
        dv_x2, dv_st, dv_mv, pl_var, pl_rstd, dv_xn, pl_xb = (sem("dv_x2"), sem("dv_st"), sem("dv_mv"), sem("pl_var"),
                                                              sem("pl_rstd"), sem("dv_xn"), sem("pl_xb"))
        pe_xT, act_xT, pe_qkv, dv_qk, dv_v = sem("pe_xT"), sem("act_xT"), sem("pe_qkv"), sem("dv_qk"), sem("dv_v")
        pl_sq, dv_ss, pl_root, pl_norm, dv_rn, dv_qkn = (sem("pl_sq"), sem("dv_ss"), sem("pl_root"), sem("pl_norm"),
                                                         sem("dv_rn"), sem("dv_qkn"))
        pe_qkT, act_qkT, pe_kp, dv_kp, pe_kv, dv_kv = (sem("pe_qkT"), sem("act_qkT"), sem("pe_kp"), sem("dv_kp"),
                                                       sem("pe_kv"), sem("dv_kv"))
        pe_qp, dv_qp, dv_kvd = sem("pe_qp"), sem("dv_qp"), sem("dv_kvd")
        pe_o, dv_nrm, dv_rec, dv_ao, pe_aT, act_aT, pe_y, dv_y = (sem("pe_o"), sem("dv_nrm"), sem("dv_rec"), sem("dv_ao"),
                                                                  sem("pe_aT"), sem("act_aT"), sem("pe_y"), sem("dv_y"))
        own_dve = sem("own_dve")
        own_pool = sem("own_pool")
        FINAL = NG
        LC = 16 * 10
        block = ctx.enter_context(clearing(nc, sems))

        def grouped(dram, first):
            return dram[bass.ds(first, GQ), :].rearrange("(s p) d -> p s d", p=P)

        @block.sync
        def _(sp):
            sp.dma_start(xg[:], grouped(x_in, 0)).then_inc(ld_x, 16)
            sp.dma_start(yg[:], grouped(xf, 1)).then_inc(ld_x, 16)
            sp.dma_start(ident[:], consts["ident"]).then_inc(ld_c, 16)
            for i, n in enumerate("qkv"):
                sp.dma_start(wqkv[:, i, :], w["W" + n]).then_inc(ld_c, 16)
                sp.dma_start(bqkv[:, i, :], w["b" + n].rearrange("(o d) -> o d", o=1).broadcast_to([P, D])).then_inc(ld_c, 16)
            sp.dma_start(own_head[:], consts["own_head"]).then_inc(ld_c, 16)
            sp.dma_start(wout[:], w["Wo"]).then_inc(ld_c, 16)
            sp.dma_start(bout[:], w["bo"].rearrange("(o d) -> o d", o=1).broadcast_to([P, D])).then_inc(ld_c, 16)
            with sp.Fori(1, NG) as g:
                sp.wait_ge(dv_xn, g)
                sp.wait_ge(pl_xb, g)
                sp.dma_start(xg[:], grouped(x_in, g * GQ)).then_inc(ld_x, 16)
                sp.dma_start(yg[:], grouped(xf, g * GQ + 1)).then_inc(ld_x, 16)
            for g in range(NG):
                sp.wait_ge(dv_y, g + 1)
                sp.dma_start(grouped(x_out, g * GQ), y[:]).then_inc(st_o, 16)
                sp.wait_ge(dv_xn, FINAL + g + 1)
                sp.dma_start(grouped(xf, g * GQ + 1), xn[:]).then_inc(st_o, 16)
            sp.wait_ge(st_o, 32 * NG)

        @block.gpsimd
        def _(pool):
            pool.memset(proj_rows[:], 0.0).then_inc(zeroed, 1)
            pool.memset(half[:], 0.5).then_inc(zeroed, 1)
            pool.memset(minus_half[:], -0.5).then_inc(zeroed, 1)
            pool.memset(v_one[:, :, :, HQ * AD:HQ * AD + 1], 1.0).then_inc(zeroed, 1)
            pool.wait_ge(zeroed, 4)

            def inverse_std(k):
                pool.wait_ge(dv_mv, k + 1).then_inc(own_pool, 1)
                pool.tensor_scalar(var[:], mv[:, :, 1], 1e-5, None, ALU.add).then_inc(pl_var, 1)
                pool.wait_ge(pl_var, k + 1)
                pool.tensor_tensor(rstd[:], var[:], minus_half[:], ALU.pow).then_inc(pl_rstd, 1)

            pool.wait_ge(ld_c, LC)
            with pool.Fori(0, NG) as g:
                inverse_std(g)
                pool.tensor_tensor(x2[:, bass.ds(g * GT, GT), :], xg[:], bout[:].unsqueeze(1).broadcast_to([P, GT, D]),
                                   ALU.add).then_inc(pl_xb, 1)
                pool.wait_ge(dv_qk, g + 1)
                pool.tensor_tensor(sq[:], qk[:], qk[:], ALU.mult).then_inc(pl_sq, 1)
                pool.wait_ge(dv_ss, g + 1)
                pool.tensor_tensor(norm[:], ss[:], half[:], ALU.pow).then_inc(pl_root, 1)
                pool.wait_ge(pl_root, g + 1).then_inc(own_pool, 1)
                pool.tensor_scalar(norm[:], norm[:], 1e-8, None, ALU.add).then_inc(pl_norm, 1)
            for g in range(NG):
                inverse_std(FINAL + g)

        @block.scalar
        def _(act):
            act.wait_ge(zeroed, 4)
            for h in range(HEADS):
                r = FEATS * (h % HQ)
                act.dma_start(proj_rows[r:r + FEATS, h // HQ, AD * h:AD * h + AD],
                              w["projection"][h:h + 1, :, :].rearrange("o f d -> (o f) d")).then_inc(ld_p, 16)
            act.wait_ge(pe_proj, 1)
            act.copy(proj[:], ps_t[:]).then_inc(act_proj, 1)
            with act.Fori(0, NG) as g:
                act.wait_ge(pe_xT, g + 1)
                act.copy(xnT[:], ps_t[:].rearrange("p (s q) -> p s q", s=GT)).then_inc(act_xT, 1)
                act.wait_ge(pe_qkT, g + 1)
                for i in (1, 0):
                    last = act.copy(qkT[:, i, :], ps_qk[i][:])
                last.then_inc(act_qkT, 1)
            for g in range(NG):
                act.wait_ge(pe_aT, g + 1)
                act.copy(aoT[:], ps_t[:].rearrange("p (s q) -> p s q", s=GT)).then_inc(act_aT, 1)

        @block.vector
        def _(dve):
            def norm_stats(k, src):
                for s in range(GT):
                    last = dve.bn_stats(st6[:, s, :], src[:, s, :])
                last.then_inc(dv_st, 1)
                dve.wait_ge(dv_st, k + 1).then_inc(own_dve, 1)
                for s in range(GT):
                    last = dve.bn_aggr(mv[:, s, :], st6[:, s, :])
                last.then_inc(dv_mv, 1)

            def normalise(k, src):
                dve.wait_ge(pl_rstd, k + 1)
                for s in range(GT):
                    last = dve.tensor_scalar(xn[:, s, :], src[:, s, :], mv[:, s, 0:1], rstd[:, s:s + 1], ALU.subtract, ALU.mult)
                last.then_inc(dv_xn, 1)

            dve.memset(kv[:], 0.0).then_inc(dv_kv, 1)
            with dve.Fori(0, NG) as g:
                dve.wait_ge(ld_x, 32 * g + 32)
                dve.tensor_tensor(xg[:], xg[:], yg[:], ALU.add).then_inc(dv_x2, 1)
                dve.wait_ge(dv_x2, g + 1)
                norm_stats(g, xg)
                normalise(g, xg)
                dve.wait_ge(ld_c, LC)
                dve.wait_ge(pe_qkv, g + 1)
                for s in range(GT):
                    last = dve.tensor_tensor(qk[:, s, :, :], banks[s][:, 0:2 * D].rearrange("p (k d) -> p k d", k=2),
                                             bqkv[:, 0:2, :], ALU.add)
                last.then_inc(dv_qk, 1)
                dve.wait_ge(zeroed, 4)
                for s in range(GT):
                    last = dve.tensor_tensor(v_one[:, s, :, 0:HQ * AD], banks[s][:, 2 * D:3 * D].rearrange("p (g d) -> p g d", g=HG),
                                             bqkv[:, 2, :].rearrange("p (g d) -> p g d", g=HG), ALU.add)
                last.then_inc(dv_v, 1)
                by_head = lambda a: a.rearrange("p s k (h d) -> p (s k h) d", d=AD)
                dve.wait_ge(pl_sq, g + 1)
                dve.tensor_reduce(ss[:], by_head(sq[:]), AX.X, ALU.add).then_inc(dv_ss, 1)
                dve.wait_ge(pl_norm, g + 1)
                dve.reciprocal(rn[:], norm[:]).then_inc(dv_rn, 1)
                dve.wait_ge(dv_rn, g + 1)
                dve.tensor_tensor(by_head(qkn[:]), by_head(qk[:]), rn[:].unsqueeze(2).broadcast_to([P, GT * 2 * HEADS, AD]),
                                  ALU.mult).then_inc(dv_qkn, 1)
                for s in range(GT):
                    dve.wait_ge(pe_kp, GT * g + s + 1)
                    dve.tensor_scalar(kp[:, s, :], banks[s][:], 0.0, FEAT_EPS, ALU.max, ALU.add).then_inc(dv_kp, 1)
                for i in range(HG):
                    dve.wait_ge(pe_qp, HG * g + i + 1)
                    dve.tensor_scalar(qp[:, i, bass.ds(g * GQ, GQ)], banks[i][:], 0.0, FEAT_EPS, ALU.max, ALU.add).then_inc(dv_qp, 1)
                dve.wait_ge(pe_kv, g + 1)
                dve.wait_ge(dv_kv, g + 1)
                dve.tensor_tensor(kv[:], kv[:], ps_kv[:, 0:HG * (HQ * AD + 1)].rearrange("p (g c) -> p g c", g=HG),
                                  ALU.add).then_inc(dv_kv, 1)
            C = HQ * AD
            dve.wait_ge(dv_kv, NG + 1)
            dve.tensor_tensor(kvd[:, :, 0:C], kv[:, :, 0:C], own_head[:, 0:C].unsqueeze(1).broadcast_to([P, HG, C]),
                              ALU.mult).then_inc(dv_kvd, 1)
            dve.tensor_tensor(kvd[:, :, C:C + HQ], kv[:, :, C:C + 1].broadcast_to([P, HG, HQ]),
                              own_head[:, C:C + HQ].unsqueeze(1).broadcast_to([P, HG, HQ]), ALU.mult).then_inc(dv_kvd, 1)
            for g in range(NG):
                for s in range(GT):
                    dve.wait_ge(pe_o, GT * g + s + 1)
                    o = banks[s][:, 0:HG * (C + HQ)].rearrange("p (g c) -> p g c", g=HG)
                    by_group = lambda a: a.rearrange("p (g h) -> p g h", g=HG)
                    dve.tensor_scalar(by_group(nrm[:, s, :]), o[:, :, C:C + HQ], 1e-6, None, ALU.max).then_inc(dv_nrm, 1)
                dve.wait_ge(dv_nrm, GT * g + GT)
                dve.reciprocal(rec[:], nrm[:]).then_inc(dv_rec, 1)
                dve.wait_ge(dv_rec, g + 1)
                if g:
                    dve.wait_ge(pe_aT, g)
                for s in range(GT):
                    o = banks[s][:, 0:HG * (C + HQ)].rearrange("p (g c) -> p g c", g=HG)
                    last = dve.tensor_tensor(ao[:, s, :].rearrange("p (g h d) -> p g h d", g=HG, h=HQ),
                                             o[:, :, 0:C].rearrange("p g (h d) -> p g h d", h=HQ),
                                             by_group(rec[:, s, :]).unsqueeze(3).broadcast_to([P, HG, HQ, AD]), ALU.mult)
                last.then_inc(dv_ao, 1)
                dve.wait_ge(pe_y, g + 1)
                dve.wait_ge(pl_xb, NG)
                if g:
                    dve.wait_ge(st_o, 32 * g)
                dve.tensor_tensor(y[:], ps_kv[:].rearrange("p (s d) -> p s d", s=GT), x2[:, g * GT:g * GT + GT, :],
                                  ALU.add).then_inc(dv_y, 1)
                dve.wait_ge(dv_y, g + 1)
                norm_stats(FINAL + g, y)
                normalise(FINAL + g, y)

        @block.tensor
        def _(pe):
            pe.wait_ge(ld_c, LC)
            pe.wait_ge(ld_p, 16 * HEADS)
            for i in range(HG):
                last = pe.transpose(ps_t[:, P * i:P * i + P], proj_rows[:, i, :], ident[:])
            last.then_inc(pe_proj, 1)
            pe.wait_ge(act_proj, 1)
            with pe.Fori(0, NG) as g:
                pe.wait_ge(dv_xn, g + 1)
                for s in range(GT):
                    last = pe.transpose(ps_t[:, P * s:P * s + P], xn[:, s, :], ident[:])
                last.then_inc(pe_xT, 1)
                pe.wait_ge(act_xT, g + 1)
                for s in range(GT):
                    last = pe.matmul(banks[s][:, 0:3 * D], xnT[:, s, :], wqkv[:].rearrange("p k d -> p (k d)"), start=True, stop=True)
                last.then_inc(pe_qkv, 1)
                pe.wait_ge(dv_qkn, g + 1)
                for i in (1, 0):
                    for s in range(GT):
                        last = pe.transpose(ps_qk[i][:, P * s:P * s + P], qkn[:, s, i, :], ident[:])
                last.then_inc(pe_qkT, 1)
                pe.wait_ge(act_qkT, g + 1)
                pe.wait_ge(dv_v, g + 1)
                for s in range(GT):
                    pe.matmul(banks[s][:], qkT[:, 1, P * s:P * s + P], proj[:], start=True, stop=True).then_inc(pe_kp, 1)
                for i in range(HG):
                    pe.wait_ge(dv_kp, GT * g + i + 1)
                    pe.matmul(banks[i][:], proj[:, P * i:P * i + P], qkT[:, 0, :], start=True, stop=True).then_inc(pe_qp, 1)
                pe.wait_ge(dv_kv, g + 1)
                for i in range(HG):
                    for s in range(GT):
                        last = pe.matmul(ps_kv[:, (HQ * AD + 1) * i:(HQ * AD + 1) * (i + 1)], kp[:, s, P * i:P * i + P],
                                         v_one[:, s, i, :], start=(s == 0), stop=(s == GT - 1))
                last.then_inc(pe_kv, 1)
                pe.wait_ge(dv_qp, HG * g + HG)
            pe.wait_ge(dv_kvd, 2)
            for g in range(NG):
                if g:
                    pe.wait_ge(dv_ao, g)
                for s in range(GT):
                    for i in range(HG):
                        c = HQ * AD + HQ
                        last = pe.matmul(banks[s][:, c * i:c * i + c], qp[:, i, P * (g * GT + s):P * (g * GT + s) + P], kvd[:, i, :],
                                         start=True, stop=True)
                    last.then_inc(pe_o, 1)
                pe.wait_ge(dv_ao, g + 1)
                for s in range(GT):
                    last = pe.transpose(ps_t[:, P * s:P * s + P], ao[:, s, :], ident[:])
                last.then_inc(pe_aT, 1)
                pe.wait_ge(act_aT, g + 1)
                if g:
                    pe.wait_ge(dv_y, g)
                for s in range(GT):
                    last = pe.matmul(ps_kv[:, P * s:P * s + P], aoT[:, s, :], wout[:], start=True, stop=True)
                last.then_inc(pe_y, 1)


def add_stack(nc, tag, x_in, xf, out):
    with ExitStack() as ctx:
        xg = ctx.enter_context(nc.sbuf_tensor(f"{tag}_xg", [P, NT, D], F32))
        yg = ctx.enter_context(nc.sbuf_tensor(f"{tag}_yg", [P, NT, D], F32))
        ld = [ctx.enter_context(nc.semaphore(f"{tag}_ld{g}")) for g in range(NG)]
        added = ctx.enter_context(nc.semaphore(f"{tag}_added"))
        stored = ctx.enter_context(nc.semaphore(f"{tag}_stored"))
        block = ctx.enter_context(nc.Block())

        def grouped(dram, first):
            return dram[first:first + GT * P, :].rearrange("(s p) d -> p s d", p=P)

        @block.sync
        def _(sp):
            for g in range(NG):
                sp.dma_start(xg[:, g * GT:g * GT + GT, :], grouped(x_in, g * GT * P)).then_inc(ld[g], 16)
                sp.dma_start(yg[:, g * GT:g * GT + GT, :], grouped(xf, g * GT * P + 1)).then_inc(ld[g], 16)
            for g in range(NG):
                sp.wait_ge(added, g + 1)
                sp.dma_start(grouped(out, g * GT * P), xg[:, g * GT:g * GT + GT, :]).then_inc(stored, 16)
            sp.wait_ge(stored, 16 * NG)

        @block.vector
        def _(dve):
            for g in range(NG):
                s = slice(g * GT, g * GT + GT)
                dve.wait_ge(ld[g], 32)
                dve.tensor_tensor(xg[:, s, :], xg[:, s, :], yg[:, s, :], ALU.add).then_inc(added, 1)


def block_program(nc, x, a, b, f, consts, out):
    x1 = nc.dram_tensor("x1", [N, D], F32, kind="Internal").ap()
    x3 = nc.dram_tensor("x3", [N, D], F32, kind="Internal").ap()
    xf = nc.dram_tensor("xf", [N + 1, D], F32, kind="Internal").ap()
    xa = nc.dram_tensor("xa", [N + 1, D], F32, kind="Internal").ap()
    softmax_attention(nc, "a", x, a["w_qkv"], a["w_out"], a["b_out"], consts, x1, xf, xa)
    local_stack(nc, "f", f, consts, xf, xa)
    linear_attention(nc, "b", x1, b, consts, x3, xf)
    local_stack(nc, "g", f, consts, xf, xa)
    add_stack(nc, "r", x3, xf, out)


A_NAMES = ["w_qkv", "w_out", "b_out"]
B_NAMES = ["Wq", "bq", "Wk", "bk", "Wv", "bv", "Wo", "bo", "projection"]
F_NAMES = ["Wqkv", "q_scale", "k_scale", "Wo", "ln_g", "ln_b", "W1", "b1", "W2", "b2"]


def kernel(**inputs):
    import concourse.bacc as bacc
    from concourse.bass_utils import run_bass_kernel_spmd

    nc = bacc.Bacc("TRN2", target_bir_lowering=False, num_devices=1)
    arrays = {}

    def load(name, a):
        arrays[name] = np.ascontiguousarray(a)
        return nc.dram_tensor(name, arrays[name].shape, F32, kind="ExternalInput").ap()

    x = load("in_x_dram", np.asarray(inputs["L0_attn_a_x"]).reshape(N, D))
    a = {n: load(f"in_a_{n}_dram", inputs[f"L0_attn_a_{n}"]) for n in A_NAMES}
    b = {n: load(f"in_b_{n}_dram", inputs[f"L0_attn_b_{n}"]) for n in B_NAMES}
    f = {n: load(f"in_f_{n}_dram", inputs[f"L0_ffn_{n}"]) for n in F_NAMES}
    consts = {n: load(f"const_{n}_dram", t) for n, t in host_tables().items()}
    out = nc.dram_tensor("out_0_dram", (N, D), F32, kind="ExternalOutput").ap()
    block_program(nc, x, a, b, f, consts, out)
    r = run_bass_kernel_spmd(nc, [arrays], core_ids=[0])
    return r.results[0]["out_0_dram"].reshape(1, N, D)
```

```python
from contextlib import ExitStack, contextmanager

import numpy as np

import concourse.bass as bass
from concourse import mybir

F32 = mybir.dt.float32
BF16 = mybir.dt.bfloat16
ALU = mybir.AluOpType
ACT = mybir.ActivationFunctionType
AX = mybir.AxisListType

P = 128
D = 128
N = 2048
NT = N // P
DEPTH = 6
HEADS = 16
DH = 64
INNER = HEADS * DH
WINDOW = 32
BLK = 64
KEYS = BLK + WINDOW
PAIRS = HEADS // 2
HID = int(D * 4 * 2 / 3)
HCH = [(0, 128), (128, 128), (256, HID - 256)]
FT = 2
FQ = FT * P
NF = NT // FT
GT = 4
NG = NT // GT
MASKED = -1e30
AD = D // HEADS
HQ = 4
FEATS = P // HQ
FEAT_EPS = 0.1
VW = 32


def host_tables():
    f = np.float32
    half = np.arange(0, DH, 2, dtype=f)
    inv_freq = (f(1.0) / np.power(f(10000.0), half / f(DH))).astype(f)
    t = np.arange(N, dtype=f)
    freqs = (t[:, None] * inv_freq[None, :]).astype(f)
    freqs = np.concatenate([freqs, freqs], -1)
    base = ((half + f(0.4 * DH)) / f(1.4 * DH)).astype(f)
    power = ((t - f(N // 2)) / f(WINDOW // 2)).astype(f)
    scale = np.power(base[None, :], power[:, None]).astype(f)
    scale = np.concatenate([scale, scale], -1)
    inv = (f(1.0) / scale).astype(f)
    cos, sin = np.cos(freqs), np.sin(freqs)
    sign = np.where(np.arange(DH) < DH // 2, f(-1), f(1))
    qk_scale = f(8.0)
    rope = np.stack([cos * scale * qk_scale, sign * sin * scale * qk_scale, cos * inv, sign * sin * inv])
    rope = rope.astype(f).reshape(4, NT, P, DH).transpose(2, 0, 1, 3)
    q = np.arange(P) % BLK
    c = np.arange(KEYS)
    seen = (c[None, :] >= q[:, None]) & (c[None, :] <= q[:, None] + WINDOW)
    rest = np.where(seen, f(0), f(MASKED))
    first = np.where(seen & (c[None, :] >= WINDOW), f(0), f(MASKED))
    mask = np.stack([np.stack([start, rest, start, rest], 1) for start in (first, rest)], 1)
    theta = (f(1.0) / np.power(f(10000.0), np.arange(0, AD, 2, dtype=f) / f(AD))).astype(f)
    angles = (t[:, None] * theta[None, :]).astype(f)
    angles = np.concatenate([angles, angles], -1)
    cos, sin = np.cos(angles), np.sin(angles)
    sign = np.where(np.arange(AD) < AD // 2, f(-1), f(1))
    down = f(1.0) / np.sqrt(f(AD))
    rope_a = np.stack([cos * down, sign * sin * down, cos, sign * sin]).astype(f).reshape(4, NT, P, AD).transpose(2, 0, 1, 3)
    fold = np.zeros((P, VW), f)
    for n in range(P):
        fold[n, n % VW] = 1
    own_head = np.zeros((P, HQ * AD + HQ), f)
    for n in range(P):
        h = n // FEATS
        own_head[n, h * AD:h * AD + AD] = 1
        own_head[n, HQ * AD + h] = 1
    return {
        "own_head": own_head,
        "rope_a": np.ascontiguousarray(rope_a.reshape(P, -1)),
        "fold": fold,
        "zero_row": np.zeros((1, D), f),
        "rope": np.ascontiguousarray(rope.reshape(P, -1)),
        "mask": np.ascontiguousarray(mask.astype(f).reshape(P, -1)),
        "ident": np.eye(P, dtype=f),
    }


@contextmanager
def clearing(nc, sems):
    with nc.Block() as block:
        yield block
    with nc.Block() as after:
        @after.sync
        def _(sp):
            for s in sems:
                sp.sem_clear(s)


def softmax_attention(nc, tag, x_in, w_qkv, w_out, b_out, consts, x_out, xf, xa):
    with ExitStack() as ctx:
        sems = []

        def sb(name, shape, dt=F32):
            return ctx.enter_context(nc.sbuf_tensor(f"{tag}_{name}", shape, dt))

        def sem(name):
            sems.append(ctx.enter_context(nc.semaphore(f"{tag}_{name}")))
            return sems[-1]

        banks = [ctx.enter_context(nc.psum_tensor(f"{tag}_bank{i}", [P, 512], F32)) for i in range(8)]
        ps_max = banks[0:2]
        ps_s = banks[2:6]
        ps_o = banks[6]
        ps_t = banks[7]

        GQ = GT * P
        wqkv = sb("wqkv", [P, 3 * D])
        wout = sb("wout", [P, D])
        bout = sb("bout", [P, D])
        ident = sb("ident", [P, P])
        ident_bf = sb("ident_bf", [P, P], BF16)
        rope = sb("rope", [P, 4, NT, AD])
        fold = sb("fold", [P, VW])
        minus_half = sb("minus_half", [P, NT])
        x = sb("x", [P, NT, D])
        st6 = sb("st6", [P, NT, 6])
        mv = sb("mv", [P, NT, 2])
        var = sb("var", [P, NT])
        rstd = sb("rstd", [P, NT])
        xn = sb("xn", [P, NT, D])
        xnT = sb("xnT", [P, 2, GT, P])
        qk = sb("qk", [P, 2, 2, GT, D])
        t1 = sb("t1", [P, 2, 2, GT, D])
        t2 = sb("t2", [P, 2, 2, GT, D])
        rest = sb("rest", [P, 2, 2, GT, D])
        parts = sb("parts", [P, 2, 3, NT, D], BF16)
        v_all = sb("v_all", [P, NT, D])
        stack = sb("stack", [P, 2, 2, NT, P], BF16)
        stackT = sb("stackT", [P, 4, 2, N], BF16)
        v_head = sb("v_head", [P, 2, NT, VW])
        maxima = sb("maxima", [P, NT, 4])
        neg = sb("neg", [P, 3, NT])
        pex = sb("pex", [P, 2, 2, GQ])
        osum = sb("osum", [P, NG, GQ])
        rec = sb("rec", [P, NT])
        ao = sb("ao", [P, NT, D])
        aoT = sb("aoT", [P, 2, GT, P])

        ld_c, st_o, st_0, zeroed, act_ident = sem("ld_c"), sem("st_o"), sem("st_0"), sem("zeroed"), sem("act_ident")
        ld_x = [sem(f"ld_x{g}") for g in range(NG)]
        dv_st, dv_mv, pl_var, pl_rstd, dv_xn = sem("dv_st"), sem("dv_mv"), sem("pl_var"), sem("pl_rstd"), sem("dv_xn")
        pe_xT, act_xT, pe_qkv, act_qk, act_v = sem("pe_xT"), sem("act_xT"), sem("pe_qkv"), sem("act_qk"), sem("act_v")
        dv_t2, pl_t1, pl_qr = sem("dv_t2"), sem("pl_t1"), sem("pl_qr")
        dv_part, dv_rest = sem("dv_part"), sem("dv_rest")
        pl_stack, pl_vh = sem("pl_stack"), sem("pl_vh")
        pe_first, act_first, pe_second, act_second = sem("pe_first"), sem("act_first"), sem("pe_second"), sem("act_second")
        pe_max, dv_max, dv_neg, dv_negp = sem("pe_max"), sem("dv_max"), sem("dv_neg"), sem("dv_negp")
        pe_s, act_ex, pe_pv, dv_os, pe_f, dv_rec, dv_ao = (sem("pe_s"), sem("act_ex"), sem("pe_pv"), sem("dv_os"),
                                                           sem("pe_f"), sem("dv_rec"), sem("dv_ao"))
        pe_aT, act_aT, pe_y, pl_xb, dv_y = sem("pe_aT"), sem("act_aT"), sem("pe_y"), sem("pl_xb"), sem("dv_y")
        own = {e: sem(f"own_{e}") for e in ("pool",)}

        PASS, STEPS = 4 * NT, NT // 2 * NG
        EARLY = 12
        LATE = (PASS - EARLY) // 2

        def carried(n):
            ahead, m = (1, EARLY + 2 * n) if n < LATE else (2, 2 * (n - LATE))
            return ahead, (m, m + 1)

        FIRST = {(2, 1): 0, (2, 3): 1, (2, 5): 2, (2, 7): 3}
        SECOND = {(3, 5): 0, (3, 6): 1}
        FOLD, OUTPUT = (0, 3), (0, 4)
        block = ctx.enter_context(clearing(nc, sems))

        def grouped(dram, first):
            return dram[first:first + GQ, :].rearrange("(s p) d -> p s d", p=P)

        def of(g):
            return slice(g * GT, g * GT + GT)

        def all_heads(eng, head):
            head(0, 0)
            with eng.Fori(0, (HEADS - 4) // 4) as i:
                for u in range(1, 5):
                    head(4 * i + u, u)
            for h in range(HEADS - 3, HEADS):
                head(h, h)

        def exists(h, ahead):
            return not isinstance(h, int) or 0 <= h + ahead < HEADS

        @block.sync
        def _(sp):
            for g in range(NG):
                sp.dma_start(x[:, of(g), :], grouped(x_in, g * GQ)).then_inc(ld_x[g], 16)
            sp.dma_start(ident[:], consts["ident"]).then_inc(ld_c, 16)
            sp.dma_start(wqkv[:], w_qkv).then_inc(ld_c, 16)
            sp.dma_start(rope[:], consts["rope_a"].rearrange("p (k t d) -> p k t d", k=4, t=NT)).then_inc(ld_c, 16)
            sp.dma_start(fold[:], consts["fold"]).then_inc(ld_c, 16)
            sp.dma_start(wout[:], w_out).then_inc(ld_c, 16)
            sp.dma_start(bout[:], b_out.rearrange("(o d) -> o d", o=1).broadcast_to([P, D])).then_inc(ld_c, 16)
            sp.dma_start(xf[0:1, :], consts["zero_row"]).then_inc(st_0, 16)
            sp.dma_start(xa[0:1, :], consts["zero_row"]).then_inc(st_0, 16)
            for g in range(NG):
                sp.wait_ge(dv_y, g + 1)
                sp.dma_start(grouped(x_out, g * GQ), x[:, of(g), :]).then_inc(st_o, 16)
                sp.wait_ge(dv_xn, NG + g + 1)
                sp.dma_start(grouped(xf, g * GQ + 1), xn[:, of(g), :]).then_inc(st_o, 16)
            sp.wait_ge(st_0, 32)
            sp.wait_ge(st_o, 32 * NG)

        @block.gpsimd
        def _(pool):
            pool.memset(minus_half[:], -0.5).then_inc(zeroed, 1)
            pool.memset(stack[:], 0.0).then_inc(zeroed, 1)
            pool.memset(v_head[:], 0.0).then_inc(zeroed, 1)
            pool.wait_ge(zeroed, 3)
            pool.memset(stack[:, :, 1, :, 72:75], 1.0).then_inc(zeroed, 1)
            pool.memset(v_head[:, :, :, AD:AD + 1], 1.0).then_inc(zeroed, 1)
            pool.wait_ge(zeroed, 5)

            def inverse_std(k, s):
                pool.wait_ge(dv_mv, k + 1)
                pool.tensor_scalar(var[:, s], mv[:, s, 1], 1e-5, None, ALU.add).then_inc(pl_var, 1)
                pool.wait_ge(pl_var, k + 1)
                pool.tensor_tensor(rstd[:, s], var[:, s], minus_half[:, s], ALU.pow).then_inc(pl_rstd, 1)

            for g in range(NG):
                inverse_std(g, of(g))
            pool.wait_ge(ld_c, 96)
            heads = lambda a: a.rearrange("p s (h d) -> p s h d", d=AD)

            def cosines(g):
                pool.wait_ge(act_qk, g + 1)
                if g >= 2:
                    pool.wait_ge(dv_part, 3 * g - 3)
                for kind in range(2):
                    tab = rope[:, 2 * kind, of(g), :].unsqueeze(2).broadcast_to([P, GT, HEADS, AD])
                    pool.tensor_tensor(heads(t1[:, g % 2, kind, :, :]), heads(qk[:, g % 2, kind, :, :]), tab, ALU.mult).then_inc(pl_t1, 1)

            for g in range(NG):
                cosines(g)
                for kind in range(2):
                    pool.wait_ge(pl_t1, 2 * g + kind + 1)
                    pool.wait_ge(dv_t2, 4 * g + 2 * kind + 2)
                    pool.tensor_tensor(t1[:, g % 2, kind, :, :], t1[:, g % 2, kind, :, :], t2[:, g % 2, kind, :, :],
                                       ALU.add).then_inc(pl_qr, 1)

            def one(a, h):
                return a[:, :, h * AD:h * AD + AD] if isinstance(h, int) else a[:, :, bass.ds(h * AD, AD)]

            def put_stack(h, p):
                for i in range(3):
                    last = pool.tensor_copy(stack[:, p, 0, :, 24 * i:24 * i + 24].rearrange("p t (j d) -> p t j d", j=3),
                                            one(parts[:, 0, i, :, :], h).unsqueeze(2).broadcast_to([P, NT, 3, AD]))
                    pool.tensor_copy(stack[:, p, 1, :, 0:72].rearrange("p t (i j d) -> p t i j d", i=3, j=3)[:, :, :, i, :],
                                     one(parts[:, 1, i, :, :], h).unsqueeze(2).broadcast_to([P, NT, 3, AD]))
                pool.memset(stack[:, p, 0, :, 72:75], 0.0).then_inc(pl_stack, 1)

            def put_v(h, p):
                pool.tensor_copy(v_head[:, p, :, 0:AD], one(v_all, h)).then_inc(pl_vh, 1)

            def head(h, u):
                if exists(h, 1) and u != 0:
                    pool.wait_ge(pe_pv, STEPS * h + 2).then_inc(own["pool"], 1)
                    put_v(h + 1, (u + 1) % 2)
                if exists(h, 2):
                    pool.wait_ge(pe_second, 2 * h + 2).then_inc(own["pool"], 1)
                    put_stack(h + 2, u % 2)

            pool.wait_ge(dv_part, 3 * NG)
            put_stack(0, 0)
            put_stack(1, 1)
            pool.wait_ge(act_v, NG)
            put_v(0, 0)
            put_v(1, 1)
            all_heads(pool, head)
            pool.wait_ge(dv_xn, NG)
            for g in range(NG):
                pool.tensor_tensor(x[:, of(g), :], x[:, of(g), :], bout[:].unsqueeze(1).broadcast_to([P, GT, D]),
                                   ALU.add).then_inc(pl_xb, 1)
            for g in range(NG):
                inverse_std(NG + g, of(g))

        @block.scalar
        def _(act):
            act.sem_inc(act_ex, 2)

            def put_xT(g):
                act.wait_ge(pe_xT, g + 1)
                if g >= 2:
                    act.wait_ge(pe_qkv, g - 1)
                act.copy(xnT[:, g % 2, :, :], ps_t[:].rearrange("p (s q) -> p s q", s=GT)).then_inc(act_xT, 1)

            put_xT(0)
            for g in range(NG):
                if g + 1 < NG:
                    put_xT(g + 1)
                act.wait_ge(pe_qkv, g + 1)
                if g >= 2:
                    act.wait_ge(pl_t1, 2 * g - 2)
                    act.wait_ge(dv_t2, 4 * g - 4)
                for s in range(GT):
                    last = act.copy(qk[:, g % 2, :, s, :], banks[s][:, 0:2 * D].rearrange("p (k d) -> p k d", k=2))
                last.then_inc(act_qk, 1)
                for s in range(GT):
                    last = act.copy(v_all[:, g * GT + s, :], banks[s][:, 2 * D:3 * D])
                last.then_inc(act_v, 1)

            act.wait_ge(ld_c, 96)
            act.copy(ident_bf[:], ident[:]).then_inc(act_ident, 1)

            def first(h, slot, n):
                act.wait_ge(pe_first, 4 * h + n + 1)
                act.copy(stackT[:, slot, 1 - n // 2, 1024 * (n % 2):1024 * (n % 2) + 1024], ps_t[:].bitcast(BF16)).then_inc(act_first, 1)

            def second(h, slot, n):
                act.wait_ge(pe_second, 2 * h + n + 1)
                act.copy(stackT[:, slot, 0, 1024 * n:1024 * n + 1024], ps_t[:].bitcast(BF16)).then_inc(act_second, 1)

            def head(h, u):
                for g in range(NG):
                    for r in range(8):
                        n = STEPS * h + (g * 8 + r)
                        b = r % 2
                        act.wait_ge(pe_s, n + 1)
                        act.wait_ge(pe_pv, n + 1)
                        for e in range(2):
                            last = act.activation(pex[:, b, e, :], ps_s[2 * b + e][:], ACT.Exp)
                        last.then_inc(act_ex, 1)
                        if (g, r) in FIRST and exists(h, 2):
                            first(h + 2, (u + 2) % 4, FIRST[g, r])
                        if (g, r) in SECOND and exists(h, 1):
                            second(h + 1, (u + 1) % 4, SECOND[g, r])

            for h in range(2):
                for n in range(4):
                    first(h, h, n)
            for n in range(2):
                second(0, 0, n)
            all_heads(act, head)
            for g in range(NG):
                act.wait_ge(pe_aT, g + 1)
                if g >= 2:
                    act.wait_ge(pe_y, g - 1)
                act.copy(aoT[:, g % 2, :, :], ps_t[:].rearrange("p (s q) -> p s q", s=GT)).then_inc(act_aT, 1)

        @block.vector
        def _(dve):
            dve.sem_inc(dv_max, 2)
            dve.sem_inc(dv_os, 1)

            def norm_stats(k, g):
                for s in range(GT):
                    last = dve.bn_stats(st6[:, g * GT + s, :], x[:, g * GT + s, :])
                last.then_inc(dv_st, 1)
                dve.wait_ge(dv_st, k + 1)
                for s in range(GT):
                    last = dve.bn_aggr(mv[:, g * GT + s, :], st6[:, g * GT + s, :])
                last.then_inc(dv_mv, 1)

            def normalise(k, g):
                dve.wait_ge(pl_rstd, k + 1)
                for s in range(g * GT, g * GT + GT):
                    last = dve.tensor_scalar(xn[:, s, :], x[:, s, :], mv[:, s, 0:1], rstd[:, s:s + 1], ALU.subtract, ALU.mult)
                last.then_inc(dv_xn, 1)

            for g in range(NG + 1):
                if g < NG:
                    dve.wait_ge(ld_x[g], 16)
                    norm_stats(g, g)
                if g >= 1:
                    normalise(g - 1, g - 1)
            dve.wait_ge(ld_c, 96)
            heads = lambda a: a.rearrange("p s (h d) -> p s h d", d=AD)

            def sines(g):
                dve.wait_ge(act_qk, g + 1)
                if g >= 2:
                    dve.wait_ge(pl_qr, 2 * g - 2)
                for kind in range(2):
                    for a in range(2):
                        tab = rope[:, 2 * kind + 1, of(g), AD // 2 * a:AD // 2 * a + AD // 2]
                        dve.tensor_tensor(heads(t2[:, g % 2, kind, :, :])[:, :, :, AD // 2 * a:AD // 2 * a + AD // 2],
                                          heads(qk[:, g % 2, kind, :, :])[:, :, :, AD // 2 * (1 - a):AD // 2 * (1 - a) + AD // 2],
                                          tab.unsqueeze(2).broadcast_to([P, GT, HEADS, AD // 2]), ALU.mult).then_inc(dv_t2, 1)

            sines(0)
            for g in range(NG):
                if g + 1 < NG:
                    sines(g + 1)
                dve.wait_ge(pl_qr, 2 * g + 2)
                for i in range(3):
                    src = t1[:, g % 2, :, :, :] if i == 0 else rest[:, i - 1, :, :, :]
                    dve.tensor_copy(parts[:, :, i, of(g), :], src).then_inc(dv_part, 1)
                    if i < 2:
                        dve.wait_ge(dv_part, 3 * g + i + 1)
                        dve.tensor_tensor(rest[:, i, :, :, :], src, parts[:, :, i, of(g), :], ALU.subtract).then_inc(dv_rest, 1)
                        dve.wait_ge(dv_rest, 2 * g + i + 1)

            def maximum(h, m):
                dve.wait_ge(pe_max, PASS * h + (m + 1))
                dve.tensor_reduce(maxima[:, m // 4, m % 4:m % 4 + 1], ps_max[m % 2][:], AX.X, ALU.max).then_inc(dv_max, 1)

            def negate(h, p):
                dve.wait_ge(dv_max, PASS * h + (PASS + 2))
                dve.tensor_reduce(neg[:, 0, :], maxima[:], AX.X, ALU.max, negate=True).then_inc(dv_neg, 1)
                dve.wait_ge(pe_first, 4 * h + 4)
                for i in range(3):
                    dve.wait_ge(dv_neg, 3 * h + (i + 1))
                    at = stack[:, p, 0, :, 72 + i]
                    dve.tensor_copy(at, neg[:, i, :]).then_inc(dv_negp, 1)
                    if i < 2:
                        dve.wait_ge(dv_negp, 3 * h + (i + 1))
                        dve.tensor_tensor(neg[:, i + 1, :], neg[:, i, :], at, ALU.subtract).then_inc(dv_neg, 1)

            def sums(h, g):
                dve.wait_ge(pe_pv, STEPS * h + (8 * g + 10))
                dve.tensor_copy(osum[:, g, :], ps_o[:]).then_inc(dv_os, 1)

            def outputs(h):
                dve.wait_ge(pe_f, h + 1)
                both = ps_t[:, 0:NT * VW].rearrange("p (t c) -> p t c", t=NT)
                dve.reciprocal(rec[:], both[:, :, AD]).then_inc(dv_rec, 1)
                dve.wait_ge(dv_rec, h + 1)
                at = ao[:, :, h * AD:h * AD + AD] if isinstance(h, int) else ao[:, :, bass.ds(h * AD, AD)]
                dve.tensor_tensor(at, both[:, :, 0:AD], rec[:].unsqueeze(2).broadcast_to([P, NT, AD]), ALU.mult).then_inc(dv_ao, 1)

            def head(h, u):
                for g in range(NG):
                    for r in range(8):
                        if r == 1 and (g or exists(h, -1)):
                            if g:
                                sums(h, g - 1)
                            else:
                                sums(h - 1, NG - 1)
                        if g * 8 + r == LATE and exists(h, 1):
                            negate(h + 1, (u + 1) % 2)
                        ahead, which = carried(g * 8 + r)
                        if exists(h, ahead):
                            for m in which:
                                maximum(h + ahead, m)
                        if (g, r) == OUTPUT and exists(h, -1):
                            outputs(h - 1)

            for m in range(PASS):
                maximum(0, m)
            negate(0, 0)
            for m in range(EARLY):
                maximum(1, m)
            all_heads(dve, head)
            sums(HEADS - 1, NG - 1)
            outputs(HEADS - 1)
            for g in range(NG + 1):
                if g < NG:
                    dve.wait_ge(pe_y, g + 1)
                    dve.wait_ge(pl_xb, NG)
                    dve.tensor_tensor(x[:, of(g), :], banks[g][:].rearrange("p (s d) -> p s d", s=GT), x[:, of(g), :],
                                      ALU.add).then_inc(dv_y, 1)
                    dve.wait_ge(dv_y, g + 1)
                    norm_stats(NG + g, g)
                if g >= 1:
                    normalise(NG + g - 1, g - 1)

        @block.tensor
        def _(pe):
            pe.sem_inc(pe_pv, 2)

            def transpose_x(g):
                pe.wait_ge(dv_xn, g + 1)
                if g:
                    pe.wait_ge(act_xT, g)
                for s in range(GT):
                    last = pe.transpose(ps_t[:, P * s:P * s + P], xn[:, g * GT + s, :], ident[:])
                last.then_inc(pe_xT, 1)

            pe.wait_ge(ld_c, 96)
            transpose_x(0)
            for g in range(NG):
                if g + 1 < NG:
                    transpose_x(g + 1)
                pe.wait_ge(act_xT, g + 1)
                if g:
                    pe.wait_ge(act_v, g)
                for s in range(GT):
                    last = pe.matmul(banks[s][:, 0:3 * D], xnT[:, g % 2, s, :], wqkv[:], start=True, stop=True)
                last.then_inc(pe_qkv, 1)

            def transposes(p, kind, half):
                for t in range(8):
                    last = pe.transpose(ps_t[:].bitcast(BF16)[:, P * t:P * t + P], stack[:, p, kind, 8 * half + t, :], ident_bf[:])
                return last

            def first(h, p, n):
                if n == 0:
                    pe.wait_ge(pl_stack, h + 1)
                    if exists(h, -3):
                        pe.wait_ge(dv_ao, h - 2)
                    if exists(h, -2):
                        pe.wait_ge(act_second, 2 * h - 2)
                if not (isinstance(h, int) and 4 * h + n == 0):
                    pe.wait_ge(act_first, 4 * h + n)
                transposes(p, 1 - n // 2, n % 2).then_inc(pe_first, 1)

            def second(h, p, n):
                pe.wait_ge(dv_negp, 3 * h + 3)
                if n:
                    pe.wait_ge(act_second, 2 * h + 1)
                elif exists(h, 1):
                    pe.wait_ge(act_first, 4 * h + 8)
                transposes(p, 0, n).then_inc(pe_second, 1)

            def scores_for_max(h, slot, m):
                pe.wait_ge(dv_max, PASS * h + (m + 1))
                pe.matmul(ps_max[m % 2][:], stackT[:, slot, 0, P * (m // 4):P * (m // 4) + P],
                          stackT[:, slot, 1, GQ * (m % 4):GQ * (m % 4) + GQ], start=True, stop=True).then_inc(pe_max, 1)

            def scores(h, slot, g, r):
                pe.wait_ge(act_ex, STEPS * h + (g * 8 + r + 1))
                for e in range(2):
                    kt = 2 * r + e
                    last = pe.matmul(ps_s[2 * (r % 2) + e][:], stackT[:, slot, 1, P * kt:P * kt + P],
                                     stackT[:, slot, 0, GQ * g:GQ * g + GQ], start=True, stop=True)
                last.then_inc(pe_s, 1)

            def values(h, p, g, r):
                pe.wait_ge(act_ex, STEPS * h + (g * 8 + r + 3))
                if r == 0:
                    pe.wait_ge(dv_os, NG * h + (g + 1))
                for e in range(2):
                    kt = 2 * r + e
                    c = 32 * (kt % 4)
                    last = pe.matmul(ps_o[c:c + VW, :], v_head[:, p, kt, :], pex[:, r % 2, e, :], start=(kt < 4), stop=(kt >= 12),
                                     tile_position=(0, c))
                last.then_inc(pe_pv, 1)

            def fold_sums(h):
                pe.wait_ge(dv_os, NG * h + (NG + 1))
                if exists(h, 1):
                    pe.wait_ge(act_second, 2 * h + 4)
                for t in range(NT):
                    last = pe.matmul(ps_t[:, VW * t:VW * t + VW], osum[:, t // GT, P * (t % GT):P * (t % GT) + P], fold[:],
                                     start=True, stop=True)
                last.then_inc(pe_f, 1)

            def head(h, u):
                pe.wait_ge(act_second, 2 * h + 2)
                pe.wait_ge(pl_vh, h + 1)
                for g in range(NG):
                    for r in range(8):
                        ahead, which = carried(g * 8 + r)
                        if exists(h, ahead):
                            if which[0] == 0:
                                pe.wait_ge(act_first, 4 * h + 12)
                            scores_for_max(h + ahead, (u + ahead) % 4, which[0])
                        scores(h, u % 4, g, r)
                        if exists(h, ahead):
                            scores_for_max(h + ahead, (u + ahead) % 4, which[1])
                        if r:
                            values(h, u % 2, g, r - 1)
                        elif g:
                            values(h, u % 2, g - 1, 7)
                        elif exists(h, -1):
                            values(h - 1, (u + 1) % 2, NG - 1, 7)
                        if (g, r) == FOLD and exists(h, -1):
                            fold_sums(h - 1)
                        if (g, r) in FIRST and exists(h, 2):
                            first(h + 2, u % 2, FIRST[g, r])
                        if (g, r) in SECOND and exists(h, 1):
                            second(h + 1, (u + 1) % 2, SECOND[g, r])

            pe.wait_ge(act_ident, 1)
            pe.wait_ge(zeroed, 5)
            pe.wait_ge(act_v, NG)
            for h in range(2):
                for n in range(4):
                    first(h, h, n)
            pe.wait_ge(act_first, 4)
            for m in range(PASS):
                scores_for_max(0, 0, m)
            for n in range(2):
                second(0, 0, n)
            pe.wait_ge(act_first, 8)
            for m in range(EARLY):
                scores_for_max(1, 1, m)
            all_heads(pe, head)
            values(HEADS - 1, 1, NG - 1, 7)
            fold_sums(HEADS - 1)
            pe.wait_ge(dv_ao, HEADS)
            for g in range(NG + 1):
                if g < NG:
                    if g:
                        pe.wait_ge(act_aT, g)
                    for s in range(GT):
                        last = pe.transpose(ps_t[:, P * s:P * s + P], ao[:, g * GT + s, :], ident[:])
                    last.then_inc(pe_aT, 1)
                if g >= 1:
                    pe.wait_ge(act_aT, g)
                    for s in range(GT):
                        last = pe.matmul(banks[g - 1][:, P * s:P * s + P], aoT[:, (g - 1) % 2, s, :], wout[:], start=True, stop=True)
                    last.then_inc(pe_y, 1)


def local_stack(nc, tag, w, consts, xf, xa):
    with ExitStack() as ctx:
        sems, per_layer, ahead = [], {}, {}

        def sb(name, shape, dt=F32):
            return ctx.enter_context(nc.sbuf_tensor(f"{tag}_{name}", shape, dt))

        def sem(name, each=0, start=0):
            s = ctx.enter_context(nc.semaphore(f"{tag}_{name}"))
            sems.append(s)
            per_layer[s.num], ahead[s.num] = each, start
            return s

        def upto(s, L, n, by=1):
            return L * per_layer[s.num] + (n * by + (by + ahead[s.num]))

        banks = [ctx.enter_context(nc.psum_tensor(f"{tag}_bank{i}", [P, 512], F32)) for i in range(8)]
        ps_qk = banks[0:2]
        ps_v = banks[2]
        ps_qkT = banks[3]
        ps_pT = banks[4]
        ps_s = banks[5]
        ps_o = banks[6]
        ps_y = banks[7]
        ps_h = [[banks[0], banks[1], banks[3]], [banks[4], banks[5], banks[7]]]
        ps_fT = banks[2]
        ps_f = banks[6]

        wqkv = sb("wqkv", [P, 3 * INNER])
        wo = sb("wo", [P, PAIRS, D])
        w1 = sb("w1", [P, 2 * HID])
        w2 = sb("w2", [P, 3, D])
        ln_g = sb("ln_g", [P, 1])
        ln_b = sb("ln_b", [P, 1])
        b1 = sb("b1", [P, 6])
        b2 = sb("b2", [P, D])
        qk_scales = sb("qk_scales", [P, 2, DH])
        rope0 = sb("rope0", [P, 4, NT, DH])
        rope = sb("rope", [P, 4, NT, DH])
        mask = sb("mask", [P, 2, 4 * KEYS])
        mask_bf = sb("mask_bf", [P, 2, 4 * KEYS], BF16)
        ident = sb("ident", [P, P])
        ident_bf = sb("ident_bf", [P, P], BF16)
        minus_half = sb("minus_half", [P, 8])

        xs = sb("xs", [P, 2, D])
        xT = sb("xT", [P, 2, P])
        sq = sb("sq", [P, 2, 512])
        ss = sb("ss", [P, 2, 8])
        sg = sb("sg", [P, 2, 8])
        rn = sb("rn", [P, 2, 8])
        qh = sb("qh", [P, 2, 512])
        t1 = sb("t1", [P, 2, 512])
        t2 = sb("t2", [P, 2, 512])
        qr = sb("qr", [P, 2, 512])
        qbd = sb("qbd", [P, PAIRS, 2, 2 * BLK])
        kT = sb("kT", [P, PAIRS, WINDOW + P])
        vt = sb("vt", [P, 2, INNER])
        vw = sb("vw", [P, 2, 2, INNER])
        nmx = sb("nmx", [P, 2, 4])
        ex = sb("ex", [P, 2, 4, KEYS])
        sm = sb("sm", [P, 2, 4])
        rd = sb("rd", [P, 2, 4])
        pn = sb("pn", [P, 2, 4, KEYS])
        pT = sb("pT", [P, 2, 4, P])
        aT = sb("aT", [P, 2, PAIRS, P])
        xr = sb("xr", [P, 2, D])
        fx = sb("fx", [P, 2, FT, D])
        fxs = sb("fxs", [P, 2, FT, D])
        fy = sb("fy", [P, 2, FT, D])
        st6 = sb("st6", [P, 2, FT, 6])
        mv = sb("mv", [P, 2, FT, 2])
        var = sb("var", [P, 2, FT])
        rstd = sb("rstd", [P, 2, FT])
        xn = sb("xn", [P, 2, FT, D])
        xnT = sb("xnT", [P, 2, FQ])
        gl = sb("gl", [P, 2, 3, FQ])
        ag = sb("ag", [P, 2, 3, FQ])

        STEPS = 4 * NT
        ld_ident, ld_rope, ld_mask, zeroed, act_const = (sem("ld_ident"), sem("ld_rope"), sem("ld_mask"), sem("zeroed"),
                                                          sem("act_const"))
        ld_wqkv, ld_scales, ld_wo, ld_wf = sem("ld_wqkv", 16), sem("ld_scales", 32), sem("ld_wo", 16), sem("ld_wf", 13 * 16)
        ld_x = [sem(f"ld_x{p}", 32 * NT // 2) for p in range(2)]
        ld_r = [sem(f"ld_r{p}", 16 * NT // 2) for p in range(2)]
        ld_vw = [sem(f"ld_vw{p}", 48 * NT // 2, 48) for p in range(2)]
        ld_f = [sem(f"ld_f{p}", 16 * NF // 2) for p in range(2)]
        ld_fs = [sem(f"ld_fs{p}", 32 * NF // 2) for p in range(2)]
        st_a, st_f = sem("st_a", 16 * NT, 32), sem("st_f", 16 * NF, 16 * NF)
        pe_xT, act_xT, pe_Wo, dv_y = sem("pe_xT", NT, 2), sem("act_xT", NT), sem("pe_Wo", NT, 2), sem("dv_y", NT, 4)
        pe_v, act_v = sem("pe_v", 2 * NT, 3), sem("act_v", 2 * NT, 1)
        pe_qkv, act_sq, dv_ssq = sem("pe_qkv", STEPS), sem("act_sq", STEPS), sem("dv_ssq", STEPS, 2)
        pl_sg, pl_rn, dv_qh, dv_t2, pl_qr = (sem("pl_sg", STEPS), sem("pl_rn", STEPS, 2), sem("dv_qh", STEPS, 2),
                                             sem("dv_t2", STEPS), sem("pl_qr", STEPS, 2))
        pe_qkT, act_kprev, act_qk = sem("pe_qkT", STEPS, 2), sem("act_kprev", STEPS // 2), sem("act_qk", STEPS, 1)
        pe_s, dv_max, act_exp = sem("pe_s", STEPS, 4), sem("dv_max", STEPS), sem("act_exp", STEPS, 2)
        dv_rd, dv_pn, pe_pT, act_pT = sem("dv_rd", STEPS), sem("dv_pn", STEPS, 2), sem("pe_pT", STEPS, 2), sem("act_pT", STEPS, 1)
        pe_o, act_aT = sem("pe_o", STEPS, 8), sem("act_aT", STEPS, 1)
        dv_kzero, pl_rope = sem("dv_kzero", 1, 1), sem("pl_rope", 6)
        dv_st, dv_mv, pl_var, pl_rstd, dv_xn = (sem("dv_st", NF), sem("dv_mv", NF), sem("pl_var", NF), sem("pl_rstd", NF),
                                                sem("dv_xn", NF, 2))
        pl_b2, pe_fT, act_fT, pe_out, dv_fy = (sem("pl_b2", NF), sem("pe_fT", NF, 2), sem("act_fT", NF, 1), sem("pe_out", NF, 2),
                                               sem("dv_fy", NF, 2))
        pe_h, act_gelu, dv_ag = sem("pe_h", 3 * NF, 6), sem("act_gelu", 3 * NF), sem("dv_ag", 3 * NF, 6)
        own = {e: sem(f"own_{e}") for e in ("pe", "dve", "pool", "sp")}

        def real(t, c, lag):
            return not isinstance(t, int) or 0 <= 4 * t + c - lag < STEPS

        def layer(eng, body, group, L, last):
            for t in range(3):
                body(L, t, t % 2)
            with eng.Fori(0, (NT - 6) // 2) as i:
                for q in range(2):
                    body(L, 2 * i + (3 + q), (3 + q) % 2)
            for t in range(NT - 3, NT):
                body(L, t, t % 2)
            for t in range(NT, NT + 3):
                if t < last:
                    body(L, t, t % 2)
                if t < NT + 2:
                    group(L, t - NT, t % 2)
            groups(eng, group, L)

        def groups(eng, body, L):
            for m in range(2, NF + 3):
                body(L, m, m % 2)

        def row(t):
            return slice(t, t + 1) if isinstance(t, int) else bass.ds(t, 1)

        def rows(dram, first, n):
            return dram[bass.ds(first, n), :]

        KIND = [0, 1, 0, 1]
        HALF = [0, 0, 1, 1]

        block = ctx.enter_context(clearing(nc, sems))

        def load_xs(eng, L, t, p):
            eng.wait_ge(st_f, upto(st_f, L - 1, t >> 1, 16))
            eng.dma_start(xs[:, p, 0:64], rows(xf, t * P + 1, P)[:, 0:64]).then_inc(ld_x[p], 16)
            eng.dma_start(xs[:, p, 64:128], rows(xf, t * P, P)[:, 64:128]).then_inc(ld_x[p], 16)

        @block.sync
        def _(sp):
            for s in (st_a, st_f, ld_vw[0], ld_vw[1]):
                sp.sem_inc(s, ahead[s.num])
            def load_wqkv(layer):
                sp.dma_start(wqkv[:], w["Wqkv"][bass.ds(layer, 1), :, :].rearrange("l d n -> (l d) n")).then_inc(ld_wqkv, 16)

            def load_scales(layer):
                for n, name in enumerate(("q_scale", "k_scale")):
                    sp.dma_start(qk_scales[:, n, :], w[name][bass.ds(layer, 1), :].broadcast_to([P, DH])).then_inc(ld_scales, 16)

            def load_wo(layer):
                sp.dma_start(wo[:], w["Wo"][bass.ds(layer, 1), :, :].rearrange("l (j p) n -> p (l j) n", p=P)).then_inc(ld_wo, 16)

            def load_wf(layer):
                sp.dma_start(w1[:], w["W1"][bass.ds(layer, 1), :, :].rearrange("l d n -> (l d) n")).then_inc(ld_wf, 16)
                col = lambda a: a.rearrange("l (n o) -> (l n) o", o=1)
                for c, (f0, m) in enumerate(HCH):
                    sp.dma_start(w2[0:m, c, :], w["W2"][bass.ds(layer, 1), f0:f0 + m, :].rearrange("l f n -> (l f) n")).then_inc(ld_wf, 16)
                    sp.dma_start(b1[0:m, c:c + 1], col(w["b1"][bass.ds(layer, 1), f0:f0 + m])).then_inc(ld_wf, 16)
                    sp.dma_start(b1[0:m, 3 + c:4 + c], col(w["b1"][bass.ds(layer, 1), HID + f0:HID + f0 + m])).then_inc(ld_wf, 16)
                sp.dma_start(ln_g[:], col(w["ln_g"][bass.ds(layer, 1), :])).then_inc(ld_wf, 16)
                sp.dma_start(ln_b[:], col(w["ln_b"][bass.ds(layer, 1), :])).then_inc(ld_wf, 16)
                sp.dma_start(b2[:], w["b2"][bass.ds(layer, 1), :].broadcast_to([P, D])).then_inc(ld_wf, 16)

            def tile(L, t, q):
                known = isinstance(t, int)
                if not known or 0 <= t - 1 < NT:
                    sp.wait_ge(act_v, upto(act_v, L, 2 * t - 1)).then_inc(own["sp"], 1)
                    sp.wait_ge(pe_o, upto(pe_o, L, 4 * t - 9))
                    p = 1 - q
                    sp.dma_start(vw[0:32, p, 0, :], vt[96:128, 1 - p, :]).then_inc(ld_vw[p], 16)
                    sp.dma_start(vw[32:96, p, 0, :], vt[0:64, p, :]).then_inc(ld_vw[p], 16)
                    sp.dma_start(vw[0:96, p, 1, :], vt[32:128, p, :]).then_inc(ld_vw[p], 16)
                if not known or t + 2 < NT:
                    sp.wait_ge(pe_xT, upto(pe_xT, L, t)).then_inc(own["sp"], 1)
                    load_xs(sp, L, t + 2, q)
                if known and t == NT:
                    sp.wait_ge(pe_qkv, upto(pe_qkv, L, STEPS - 1)).then_inc(own["sp"], 1)
                    sp.wait_ge(pl_rope, upto(pl_rope, L, 5)).then_inc(own["sp"], 1)
                    load_scales((L + 1) % DEPTH)
                    load_wqkv((L + 1) % DEPTH)
                    load_shifted(L, 0, 0)
                    load_shifted(L, 1, 1)
                if not known or 0 <= t - 3 < NT:
                    sp.wait_ge(dv_y, upto(dv_y, L, t - 3)).then_inc(own["sp"], 1)
                    sp.wait_ge(st_a, upto(st_a, L, t - 4, 16)).then_inc(own["sp"], 1)
                    sp.dma_start(rows(xa, (t - 3) * P + 1, P), xr[:, 1 - q, :]).then_inc(st_a, 16)
                if not known or 0 <= t - 2 < NT:
                    sp.wait_ge(st_a, upto(st_a, L, t - 4, 16)).then_inc(own["sp"], 1)
                    sp.dma_start(xr[:, q, :], rows(xf, (t - 2) * P + 1, P)).then_inc(ld_r[q], 16)

            def load_shifted(L, m, q):
                sp.wait_ge(dv_xn, upto(dv_xn, L, m - 2)).then_inc(own["sp"], 1)
                sp.wait_ge(st_a, upto(st_a, L, 2 * m + 1, 16)).then_inc(own["sp"], 1)
                r = lambda first: rows(xa, first, FQ).rearrange("(s p) d -> p s d", p=P)
                sp.dma_start(fxs[:, q, :, 0:64], r(m * FQ + 1)[:, :, 0:64]).then_inc(ld_fs[q], 16)
                sp.dma_start(fxs[:, q, :, 64:128], r(m * FQ)[:, :, 64:128]).then_inc(ld_fs[q], 16)

            def group(L, m, q):
                known = isinstance(m, int)
                if not known or m + 2 < NF:
                    load_shifted(L, m + 2, q)
                if not known or 0 <= m - 1 < NF:
                    sp.wait_ge(dv_fy, upto(dv_fy, L, m - 3)).then_inc(own["sp"], 1)
                    sp.dma_start(fx[:, 1 - q, :, :],
                                 rows(xa, (m - 1) * FQ + 1, FQ).rearrange("(s p) d -> p s d", p=P)).then_inc(ld_f[1 - q], 16)
                if not known or m >= 3:
                    sp.wait_ge(dv_fy, upto(dv_fy, L, m - 3)).then_inc(own["sp"], 1)
                    sp.wait_ge(st_f, upto(st_f, L, m - 4, 16))
                    sp.dma_start(rows(xf, (m - 3) * FQ + 1, FQ).rearrange("(s p) d -> p s d", p=P),
                                 fy[:, 1 - q, :, :]).then_inc(st_f, 16)
                if known and m == 2:
                    sp.wait_ge(pe_Wo, upto(pe_Wo, L, NT - 1)).then_inc(own["sp"], 1)
                    load_wo((L + 1) % DEPTH)
                if known and m == NF - 2:
                    for p in range(2):
                        sp.wait_ge(pe_xT, upto(pe_xT, L, NT - 2 + p)).then_inc(own["sp"], 1)
                        load_xs(sp, L + 1, p, p)
                if known and m == NF + 1:
                    sp.wait_ge(pe_out, upto(pe_out, L, NF - 1)).then_inc(own["sp"], 1)
                    sp.wait_ge(pl_b2, upto(pl_b2, L, NF - 1)).then_inc(own["sp"], 1)
                    load_wf((L + 1) % DEPTH)

            sp.dma_start(ident[:], consts["ident"]).then_inc(ld_ident, 16)
            load_xs(sp, 0, 0, 0)
            load_scales(0)
            sp.dma_start(rope0[:], consts["rope"].rearrange("p (k t d) -> p k t d", k=4, t=NT)).then_inc(ld_rope, 16)
            load_wqkv(0)
            load_xs(sp, 0, 1, 1)
            sp.dma_start(mask[:], consts["mask"].rearrange("p (i c) -> p i c", i=2)).then_inc(ld_mask, 16)
            load_wo(0)
            load_wf(0)
            sp.wait_ge(zeroed, 6)
            with sp.Fori(0, DEPTH) as L:
                layer(sp, tile, group, L, NT + 3)
            for p in range(2):
                sp.wait_ge(ld_x[p], upto(ld_x[p], DEPTH, 0, 32))
            sp.wait_ge(ld_wqkv, 16 * (DEPTH + 1))
            sp.wait_ge(ld_scales, 32 * (DEPTH + 1))
            sp.wait_ge(ld_wo, 16 * (DEPTH + 1))
            sp.wait_ge(st_f, upto(st_f, DEPTH - 1, NF - 1, 16))
            sp.wait_ge(ld_wf, 13 * 16 * (DEPTH + 1))

        @block.gpsimd
        def _(pool):
            for s in (pl_rn, pl_qr):
                pool.sem_inc(s, ahead[s.num])
            pool.memset(minus_half[:], -0.5).then_inc(zeroed, 1)
            for buf in (qbd, kT):
                pool.memset(buf[:], 0.0).then_inc(zeroed, 1)

            def fold_rope(n, kind):
                pool.wait_ge(ld_scales, upto(ld_scales, n, 0, 32))
                whole = qk_scales[:, kind, :].unsqueeze(1).broadcast_to([P, NT, DH])
                halves = qk_scales[:, kind, :].rearrange("p (a b) -> p a b", a=2)[:, ::-1, :]
                pool.tensor_tensor(rope[:, 2 * kind, :, :], rope0[:, 2 * kind, :, :], whole, ALU.mult).then_inc(pl_rope, 1)
                for a in range(2):
                    sl = slice(a * 32, a * 32 + 32)
                    pool.tensor_tensor(rope[:, 2 * kind + 1, :, sl], rope0[:, 2 * kind + 1, :, sl],
                                       halves[:, a, :].unsqueeze(1).broadcast_to([P, NT, 32]),
                                       ALU.mult).then_inc(pl_rope, 1)

            def tile(L, t, q):
                for c in range(4):
                    n, b = 4 * t + c, c % 2
                    if real(t, c, 0):
                        pool.wait_ge(dv_ssq, upto(dv_ssq, L, n)).then_inc(own["pool"], 1)
                        pool.tensor_scalar(sg[:, b, :], ss[:, b, :], 1e-24, None, ALU.max).then_inc(pl_sg, 1)
                        pool.wait_ge(pl_sg, upto(pl_sg, L, n))
                        pool.wait_ge(dv_qh, upto(dv_qh, L, n - 2))
                        pool.tensor_tensor(rn[:, b, :], sg[:, b, :], minus_half[:], ALU.pow).then_inc(pl_rn, 1)
                    if real(t, c, 1):
                        pool.wait_ge(dv_t2, upto(dv_t2, L, n - 1))
                        pool.wait_ge(pe_qkT, upto(pe_qkT, L, n - 3))
                        pool.tensor_tensor(qr[:, 1 - b, :], t1[:, 1 - b, :], t2[:, 1 - b, :], ALU.add).then_inc(pl_qr, 1)

            def inverse_std(L, m, q):
                pool.wait_ge(dv_mv, upto(dv_mv, L, m)).then_inc(own["pool"], 1)
                pool.tensor_scalar(var[:, q, :], mv[:, q, :, 1], 1e-5, None, ALU.add).then_inc(pl_var, 1)
                pool.wait_ge(pl_var, upto(pl_var, L, m))
                pool.tensor_tensor(rstd[:, q, :], var[:, q, :], minus_half[:, 0:FT], ALU.pow).then_inc(pl_rstd, 1)

            def group(L, m, q):
                known = isinstance(m, int)
                if known and m == 0:
                    inverse_std(L, 0, 0)
                if not known or m + 1 < NF:
                    inverse_std(L, m + 1, 1 - q)
                if not known or 0 <= m - 2 < NF:
                    pool.wait_ge(ld_wf, upto(ld_wf, L, 0, 13 * 16))
                    pool.wait_ge(ld_f[q], upto(ld_f[q], L, (m - 2) >> 1, 16))
                    pool.tensor_tensor(fx[:, q, :, :], fx[:, q, :, :], b2[:].unsqueeze(1).broadcast_to([P, FT, D]),
                                       ALU.add).then_inc(pl_b2, 1)
                if known and m < 2:
                    pool.wait_ge(dv_t2, upto(dv_t2, L, STEPS - 1))
                    fold_rope(L + 1, m)

            pool.wait_ge(zeroed, 6)
            pool.wait_ge(ld_rope, 16)
            fold_rope(0, 0)
            fold_rope(0, 1)
            with pool.Fori(0, DEPTH) as L:
                layer(pool, tile, group, L, NT + 1)

        @block.scalar
        def _(act):
            for s in (act_v, act_exp, act_qk, act_pT, act_aT, act_fT):
                act.sem_inc(s, ahead[s.num])

            def put_mask():
                act.wait_ge(ld_mask, 16)
                act.copy(mask_bf[:], mask[:]).then_inc(act_const, 1)

            def put_xT(L, t, p):
                act.wait_ge(pe_xT, upto(pe_xT, L, t))
                act.wait_ge(pe_v, upto(pe_v, L, 2 * t - 3))
                act.copy(xT[:, p, :], ps_v[:, 0:P]).then_inc(act_xT, 1)

            def tile(L, t, q):
                for c in range(4):
                    n, b = 4 * t + c, c % 2
                    if real(t, c, 0):
                        act.wait_ge(pe_qkv, upto(pe_qkv, L, n))
                        act.wait_ge(dv_ssq, upto(dv_ssq, L, n - 2))
                        act.activation(sq[:, b, :], ps_qk[b][:], ACT.Square).then_inc(act_sq, 1)
                    if real(t, c, 6):
                        act.wait_ge(pe_pT, upto(pe_pT, L, n - 6))
                        act.wait_ge(pe_o, upto(pe_o, L, n - 8))
                        act.copy(pT[0:KEYS, b, :, :], ps_pT[0:KEYS, :].rearrange("p (u q) -> p u q", u=4)).then_inc(act_pT, 1)
                    if real(t, c, 4):
                        act.wait_ge(dv_max, upto(dv_max, L, n - 4))
                        act.wait_ge(dv_pn, upto(dv_pn, L, n - 6))
                        for u in range(4):
                            last = act.activation(ex[:, b, u, :], ps_s[:, KEYS * u:KEYS * u + KEYS], ACT.Exp, bias=nmx[:, b, u:u + 1],
                                                  accum_out=sm[:, b, u:u + 1])
                        last.then_inc(act_exp, 1)
                    if real(t, c, 2):
                        tj, cj = t + (c - 2) // 4, (c - 2) % 4
                        pairs = slice(4 * HALF[cj], 4 * HALF[cj] + 4)
                        act.wait_ge(pe_qkT, upto(pe_qkT, L, n - 2))
                        act.wait_ge(pe_s, upto(pe_s, L, 4 * tj - 3 + 2 * HALF[cj]))
                        if KIND[cj] == 0:
                            for h in range(2):
                                r = slice(64 * h, 64 * h + 64)
                                last = act.copy(qbd[r, pairs, :, 64 * h:64 * h + 64],
                                                ps_qkT[r, :].rearrange("p (j b q) -> p j b q", j=4, b=2))
                            last.then_inc(act_qk, 1)
                        else:
                            act.copy(kT[:, pairs, 0:WINDOW], kT[:, pairs, P:P + WINDOW]).then_inc(act_kprev, 1)
                            act.wait_ge(act_kprev, upto(act_kprev, L, 2 * tj + HALF[cj]))
                            act.copy(kT[:, pairs, WINDOW:], ps_qkT[:].rearrange("p (j q) -> p j q", j=4)).then_inc(act_qk, 1)
                    if real(t, c, 7):
                        tj, g = t + (c - 7) // 4, (c - 7) % 4
                        p = (q + (c - 7) // 4) % 2
                        act.wait_ge(pe_o, upto(pe_o, L, n - 7))
                        act.wait_ge(pe_Wo, upto(pe_Wo, L, tj - 2))
                        act.copy(aT[:, p, 2 * g:2 * g + 2, :], ps_o[:, 0:2 * P].rearrange("p (j q) -> p j q", j=2)).then_inc(act_aT, 1)
                    if c % 2 == 0 and real(t, c, 0):
                        half = c // 2
                        act.wait_ge(pe_v, upto(pe_v, L, 2 * t + half))
                        act.wait_ge(ld_vw[1 - q], upto(ld_vw[1 - q], L, (t - 1) >> 1, 48))
                        act.copy(vt[:, q, 512 * half:512 * half + 512], ps_v[:]).then_inc(act_v, 1)
                    if c == 1 and real(t + 1, 0, 0):
                        put_xT(L, t + 1, 1 - q)

            def group(L, m, q):
                known = isinstance(m, int)
                if known and m == 0:
                    act.wait_ge(ld_wf, upto(ld_wf, L, 0, 13 * 16))
                if not known or m < NF:
                    act.wait_ge(pe_fT, upto(pe_fT, L, m))
                    act.wait_ge(pe_h, upto(pe_h, L, 3 * m - 4))
                    act.activation(xnT[:, q, :], ps_fT[:, 0:FQ], ACT.Identity, bias=ln_b[:], scale=ln_g[:]).then_inc(act_fT, 1)
                if not known or 0 <= m - 1 < NF:
                    for c, (_, f) in enumerate(HCH):
                        act.wait_ge(pe_h, upto(pe_h, L, 3 * m - 3 + c))
                        act.wait_ge(dv_ag, upto(dv_ag, L, 3 * m - 9 + c))
                        act.activation(gl[0:f, 1 - q, c, :], ps_h[1 - q][c][0:f, 0:FQ], ACT.Gelu,
                                       bias=b1[0:f, 3 + c:4 + c]).then_inc(act_gelu, 1)

            act.wait_ge(ld_ident, 16)
            act.copy(ident_bf[:], ident[:]).then_inc(act_const, 1)
            act.wait_ge(zeroed, 6)
            put_mask()
            with act.Fori(0, DEPTH) as L:
                put_xT(L, 0, 0)
                act.wait_ge(dv_kzero, upto(dv_kzero, L, -1))
                layer(act, tile, group, L, NT + 2)

        @block.vector
        def _(dve):
            for s in (dv_ssq, dv_qh, dv_y, dv_pn, dv_kzero, dv_xn, dv_fy, dv_ag):
                dve.sem_inc(s, ahead[s.num])
            heads = lambda a: a.rearrange("p (h d) -> p h d", h=8)
            split = lambda a: a.rearrange("p (h a b) -> p h a b", h=8, a=2)

            def tile(L, t, q):
                for c in range(4):
                    n, b = 4 * t + c, c % 2
                    if real(t, c, 5):
                        dve.wait_ge(act_exp, upto(act_exp, L, n - 5))
                        dve.reciprocal(rd[:, 1 - b, :], sm[:, 1 - b, :]).then_inc(dv_rd, 1)
                        dve.wait_ge(dv_rd, upto(dv_rd, L, n - 5))
                        dve.wait_ge(pe_pT, upto(pe_pT, L, n - 7))
                        dve.tensor_tensor(pn[:, 1 - b, :, :], ex[:, 1 - b, :, :],
                                          rd[:, 1 - b, :].unsqueeze(2).broadcast_to([P, 4, KEYS]), ALU.mult).then_inc(dv_pn, 1)
                    if real(t, c, 4):
                        dve.wait_ge(pe_s, upto(pe_s, L, n - 4))
                        dve.wait_ge(act_exp, upto(act_exp, L, n - 6))
                        dve.tensor_reduce(nmx[:, b, :], ps_s[:, 0:4 * KEYS].rearrange("p (u c) -> p u c", u=4), AX.X, ALU.max,
                                          negate=True).then_inc(dv_max, 1)
                    if real(t, c, 0):
                        dve.wait_ge(act_sq, upto(act_sq, L, n))
                        dve.wait_ge(pl_rn, upto(pl_rn, L, n - 2))
                        dve.tensor_reduce(ss[:, b, :], heads(sq[:, b, :]), AX.X, ALU.add).then_inc(dv_ssq, 1)
                    if real(t, c, 1):
                        dve.wait_ge(pl_rn, upto(pl_rn, L, n - 1))
                        dve.tensor_tensor(heads(qh[:, 1 - b, :]), heads(ps_qk[1 - b][:]),
                                          rn[:, 1 - b, :].unsqueeze(2).broadcast_to([P, 8, DH]), ALU.mult).then_inc(dv_qh, 1)
                    if real(t, c, 1):
                        tj, cj = t + (c - 1) // 4, (c - 1) % 4
                        dve.wait_ge(dv_qh, upto(dv_qh, L, n - 1))
                        dve.wait_ge(pl_qr, upto(pl_qr, L, n - 3))
                        dve.tensor_tensor(heads(t1[:, 1 - b, :]), heads(qh[:, 1 - b, :]),
                                          rope[:, 2 * KIND[cj], row(tj), :].broadcast_to([P, 8, DH]), ALU.mult)
                        dve.tensor_tensor(split(t2[:, 1 - b, :]), split(qh[:, 1 - b, :])[:, :, ::-1, :],
                                          rope[:, 2 * KIND[cj] + 1, row(tj), :].broadcast_to([P, 8, DH]).rearrange(
                                              "p h (a b) -> p h a b", a=2), ALU.mult).then_inc(dv_t2, 1)
                    if c == 0 and real(t - 3, 0, 0):
                        dve.wait_ge(pe_Wo, upto(pe_Wo, L, t - 3))
                        dve.wait_ge(ld_r[1 - q], upto(ld_r[1 - q], L, (t - 3) >> 1, 16))
                        dve.tensor_tensor(xr[:, 1 - q, :], ps_y[:, 0:P], xr[:, 1 - q, :], ALU.add).then_inc(dv_y, 1)

            def row_stats(L, m, q):
                dve.wait_ge(ld_fs[q], upto(ld_fs[q], L, m >> 1, 32))
                for s in range(FT):
                    last = dve.bn_stats(st6[:, q, s, :], fxs[:, q, s, :])
                last.then_inc(dv_st, 1)
                dve.wait_ge(dv_st, upto(dv_st, L, m)).then_inc(own["dve"], 1)
                for s in range(FT):
                    last = dve.bn_aggr(mv[:, q, s, :], st6[:, q, s, :])
                last.then_inc(dv_mv, 1)

            def group(L, m, q):
                known = isinstance(m, int)
                if known and m == 0:
                    row_stats(L, 0, 0)
                if not known or m < NF:
                    dve.wait_ge(pl_rstd, upto(pl_rstd, L, m))
                    dve.wait_ge(pe_fT, upto(pe_fT, L, m - 2))
                    for s in range(FT):
                        last = dve.tensor_scalar(xn[:, q, s, :], fxs[:, q, s, :], mv[:, q, s, 0:1], rstd[:, q, s:s + 1],
                                                 ALU.subtract, ALU.mult)
                    last.then_inc(dv_xn, 1)
                if not known or m >= 3:
                    dve.wait_ge(pe_out, upto(pe_out, L, m - 3))
                    dve.wait_ge(pl_b2, upto(pl_b2, L, m - 3))
                    dve.wait_ge(st_f, upto(st_f, L, m - 5, 16))
                    dve.tensor_tensor(fy[:, 1 - q, :, :], ps_f[:, 0:FQ].rearrange("p (s d) -> p s d", s=FT), fx[:, 1 - q, :, :],
                                      ALU.add).then_inc(dv_fy, 1)
                if not known or m + 1 < NF:
                    row_stats(L, m + 1, 1 - q)
                if not known or 0 <= m - 1 < NF:
                    dve.wait_ge(ld_wf, upto(ld_wf, L, 0, 13 * 16))
                    for c, (_, f) in enumerate(HCH):
                        dve.wait_ge(act_gelu, upto(act_gelu, L, 3 * m - 3 + c))
                        dve.wait_ge(pe_out, upto(pe_out, L, m - 3))
                        dve.scalar_tensor_tensor(out=ag[0:f, 1 - q, c, :], in0=ps_h[1 - q][c][0:f, FQ:2 * FQ], scalar=b1[0:f, c:c + 1],
                                                 in1=gl[0:f, 1 - q, c, :], op0=ALU.add, op1=ALU.mult).then_inc(dv_ag, 1)

            for buf in (vt, vw, pT):
                dve.memset(buf[:], 0.0).then_inc(zeroed, 1)
            with dve.Fori(0, DEPTH) as L:
                dve.wait_ge(pl_rope, upto(pl_rope, L, 5)).then_inc(own["dve"], 1)
                layer(dve, tile, group, L, NT + 3)
                dve.wait_ge(pe_s, upto(pe_s, L, STEPS - 1))
                dve.memset(kT[:, :, P:P + WINDOW], 0.0).then_inc(dv_kzero, 1)

        @block.tensor
        def _(pe):
            for s in (pe_xT, pe_Wo, pe_v, pe_qkT, pe_s, pe_pT, pe_o, pe_fT, pe_out, pe_h):
                pe.sem_inc(s, ahead[s.num])

            def transpose_x(L, t, p):
                pe.wait_ge(ld_x[p], upto(ld_x[p], L, t >> 1, 32))
                pe.wait_ge(act_v, upto(act_v, L, 2 * t - 2))
                pe.transpose(ps_v[:, 0:P], xs[:, p, :], ident[:]).then_inc(pe_xT, 1)

            def tile(L, t, q):
                known = isinstance(t, int)
                for c in range(4):
                    n, b = 4 * t + c, c % 2
                    if real(t, c, 0):
                        pe.wait_ge(act_xT, upto(act_xT, L, t))
                        pe.wait_ge(dv_qh, upto(dv_qh, L, n - 2))
                        at = INNER * KIND[c] + 512 * HALF[c]
                        pe.matmul(ps_qk[b][:], xT[:, q, :], wqkv[:, at:at + 512], start=True, stop=True).then_inc(pe_qkv, 1)
                    if real(t, c, 6):
                        pe.wait_ge(dv_pn, upto(dv_pn, L, n - 6))
                        pe.wait_ge(act_pT, upto(act_pT, L, n - 7))
                        for u in range(4):
                            last = pe.transpose(ps_pT[0:KEYS, P * u:P * u + P], pn[:, b, u, :], ident[:])
                        last.then_inc(pe_pT, 1)
                    if real(t, c, 4):
                        g = c
                        pe.wait_ge(act_qk, upto(act_qk, L, 4 * t - (3 if g < 2 else 1)))
                        pe.wait_ge(act_exp, upto(act_exp, L, n - 5))
                        first = known and t == 1
                        if first and c == 0:
                            pe.wait_ge(act_const, 2)
                        pe.matmul(ps_s[:, 0:4 * KEYS], ident_bf[:], mask_bf[:, 0 if first else 1, :], start=True, stop=False)
                        for u in range(4):
                            j, blk = 2 * g + u // 2, u % 2
                            last = pe.matmul(ps_s[:, KEYS * u:KEYS * u + KEYS], qbd[:, j, blk, :], kT[:, j, BLK * blk:BLK * blk + KEYS],
                                             start=False, stop=(u == 3))
                        last.then_inc(pe_s, 1)
                    if real(t, c, 2):
                        pe.wait_ge(pl_qr, upto(pl_qr, L, n - 2))
                        pe.wait_ge(act_qk, upto(act_qk, L, n - 3))
                        for j in range(4):
                            last = pe.transpose(ps_qkT[:, P * j:P * j + P], qr[:, b, P * j:P * j + P], ident[:])
                        last.then_inc(pe_qkT, 1)
                    if real(t, c, 7):
                        tj, g = t + (c - 7) // 4, (c - 7) % 4
                        p = (q + (c - 7) // 4) % 2
                        pe.wait_ge(act_pT, upto(act_pT, L, n - 7))
                        pe.wait_ge(act_aT, upto(act_aT, L, n - 8))
                        if known and n == 7:
                            pe.wait_ge(dv_fy, upto(dv_fy, L - 1, NF - 1))
                        if g == 0:
                            pe.wait_ge(ld_vw[p], upto(ld_vw[p], L, tj >> 1, 48))
                        for u in range(4):
                            j, blk = 2 * g + u // 2, u % 2
                            for h in range(2):
                                r = slice(DH * h, DH * h + DH)
                                last = pe.matmul(ps_o[r, BLK * u:BLK * u + BLK], vw[:, p, blk, P * j + DH * h:P * j + DH * h + DH],
                                                 pT[:, 1 - b, u, BLK * h:BLK * h + BLK], start=True, stop=True, tile_position=(0, DH * h))
                        last.then_inc(pe_o, 1)
                    if c % 2 == 0 and real(t, c, 0):
                        half = c // 2
                        pe.wait_ge(act_v, upto(act_v, L, 2 * t + half - 1))
                        if half and real(t + 1, 0, 0):
                            pe.wait_ge(act_xT, upto(act_xT, L, t + 1))
                        at = 2 * INNER + 512 * half
                        pe.matmul(ps_v[:], xT[:, q, :], wqkv[:, at:at + 512], start=True, stop=True).then_inc(pe_v, 1)
                    if c == 1 and real(t + 1, 0, 0):
                        transpose_x(L, t + 1, 1 - q)
                    if c == 3 and real(t - 2, 0, 0):
                        pe.wait_ge(act_aT, upto(act_aT, L, 4 * t - 5))
                        pe.wait_ge(dv_y, upto(dv_y, L, t - 3))
                        for j in range(PAIRS):
                            last = pe.matmul(ps_y[:, 0:P], aT[:, q, j, :], wo[:, j, :], start=(j == 0), stop=(j == PAIRS - 1))
                        last.then_inc(pe_Wo, 1)

            def group(L, m, q):
                known = isinstance(m, int)
                if known and m == 0:
                    pe.wait_ge(act_v, upto(act_v, L, 2 * NT - 1))
                    pe.wait_ge(ld_wf, upto(ld_wf, L, 0, 13 * 16))
                if known and m == 1:
                    pe.wait_ge(dv_qh, upto(dv_qh, L, STEPS - 1))
                    pe.wait_ge(act_qk, upto(act_qk, L, STEPS - 1))
                if not known or m < NF:
                    pe.wait_ge(dv_xn, upto(dv_xn, L, m))
                    pe.wait_ge(act_fT, upto(act_fT, L, m - 1))
                    for s in range(FT):
                        last = pe.transpose(ps_fT[:, P * s:P * s + P], xn[:, q, s, :], ident[:])
                    last.then_inc(pe_fT, 1)
                if not known or 0 <= m - 1 < NF:
                    pe.wait_ge(act_fT, upto(act_fT, L, m - 1))
                    for c, (f0, f) in enumerate(HCH):
                        pe.wait_ge(dv_ag, upto(dv_ag, L, 3 * m - 9 + c))
                        pe.matmul(ps_h[1 - q][c][0:f, 0:FQ], w1[:, HID + f0:HID + f0 + f], xnT[:, 1 - q, :], start=True, stop=True)
                        pe.matmul(ps_h[1 - q][c][0:f, FQ:2 * FQ], w1[:, f0:f0 + f], xnT[:, 1 - q, :], start=True,
                                  stop=True).then_inc(pe_h, 1)
                if not known or 0 <= m - 2 < NF:
                    pe.wait_ge(dv_ag, upto(dv_ag, L, 3 * m - 4))
                    pe.wait_ge(dv_fy, upto(dv_fy, L, m - 3))
                    for s in range(FT):
                        for c, (_, f) in enumerate(HCH):
                            last = pe.matmul(ps_f[:, P * s:P * s + P], ag[0:f, q, c, P * s:P * s + P], w2[0:f, c, :],
                                             start=(c == 0), stop=(c == 2))
                    last.then_inc(pe_out, 1)
                if known and m == 1:
                    pe.wait_ge(dv_y, upto(dv_y, L, NT - 1)).then_inc(own["pe"], 1)

            pe.wait_ge(ld_ident, 16)
            with pe.Fori(0, DEPTH) as L:
                transpose_x(L, 0, 0)
                pe.wait_ge(ld_wqkv, upto(ld_wqkv, L, 0, 16))
                pe.wait_ge(ld_wo, upto(ld_wo, L, 0, 16)).then_inc(own["pe"], 1)
                layer(pe, tile, group, L, NT + 2)


def linear_attention(nc, tag, x_in, w, consts, x_out, xf):
    with ExitStack() as ctx:
        sems = []

        def sb(name, shape, dt=F32):
            return ctx.enter_context(nc.sbuf_tensor(f"{tag}_{name}", shape, dt))

        def sem(name):
            sems.append(ctx.enter_context(nc.semaphore(f"{tag}_{name}")))
            return sems[-1]

        banks = [ctx.enter_context(nc.psum_tensor(f"{tag}_bank{i}", [P, 512], F32)) for i in range(8)]
        ps_t = banks[4]
        ps_qk = banks[5:7]
        ps_kv = banks[7]

        GQ = GT * P
        HG = HEADS // HQ
        C = HQ * AD
        ps_y = banks[5:7]
        wqkv = sb("wqkv", [P, 3, D])
        wout = sb("wout", [P, D])
        bqkv = sb("bqkv", [P, 3, D])
        bout = sb("bout", [P, D])
        ident = sb("ident", [P, P])
        own_head = sb("own_head", [P, C + HQ])
        proj_rows = sb("proj_rows", [P, HG, D])
        proj = sb("proj", [P, HEADS * FEATS])
        minus_half = sb("minus_half", [P, GT])
        x2 = sb("x2", [P, NT, D])
        y = sb("y", [P, NT, D])
        st6 = sb("st6", [P, NT, 6])
        mv = sb("mv", [P, NT, 2])
        var = sb("var", [P, NT])
        rstd = sb("rstd", [P, NT])
        xn = sb("xn", [P, NT, D])
        xnT = sb("xnT", [P, GT, P])
        qk = sb("qk", [P, GT, 2, D])
        sq = sb("sq", [P, GT, 2, D])
        ss = sb("ss", [P, GT * 2 * HEADS])
        root = sb("root", [P, GT * 2 * HEADS])
        inv = sb("inv", [P, GT * 2 * HEADS])
        root2 = sb("root2", [P, GT * 2 * HEADS])
        norm = sb("norm", [P, GT * 2 * HEADS])
        rn = sb("rn", [P, GT * 2 * HEADS])
        qkn = sb("qkn", [P, GT, 2, D])
        qkT = sb("qkT", [P, 2, GQ])
        v_one = sb("v_one", [P, 2, GT, HG, C + 1])
        kp = sb("kp", [P, GT, HEADS * FEATS])
        qp = sb("qp", [P, HG, N])
        kv = sb("kv", [P, HG, C + 1])
        kvd = sb("kvd", [P, HG, C + HQ])
        nrm = sb("nrm", [P, GT, HEADS])
        rec = sb("rec", [P, GT, HEADS])
        ao = sb("ao", [P, 2, GT, D])
        aoT = sb("aoT", [P, 2, GT, P])

        ld_c, ld_p, st_o, zeroed = sem("ld_c"), sem("ld_p"), sem("st_o"), sem("zeroed")
        ld_x = [sem(f"ld_x{g}") for g in range(NG)]
        pe_proj, act_proj = sem("pe_proj"), sem("act_proj")
        dv_x2, dv_st, dv_mv, pl_var, pl_rstd, dv_xn, pl_xb = (sem("dv_x2"), sem("dv_st"), sem("dv_mv"), sem("pl_var"),
                                                              sem("pl_rstd"), sem("dv_xn"), sem("pl_xb"))
        pe_xT, act_xT, pe_qkv, dv_qk, dv_v = sem("pe_xT"), sem("act_xT"), sem("pe_qkv"), sem("dv_qk"), sem("dv_v")
        act_sq, dv_ss, act_root, dv_newton, dv_rn, dv_qkn = (sem("act_sq"), sem("dv_ss"), sem("act_root"), sem("dv_newton"),
                                                             sem("dv_rn"), sem("dv_qkn"))
        pe_qkT, act_qkT, pe_kp, dv_kp, pe_kv, dv_kv = (sem("pe_qkT"), sem("act_qkT"), sem("pe_kp"), sem("dv_kp"),
                                                       sem("pe_kv"), sem("dv_kv"))
        pe_qp, dv_qp, dv_kvd = sem("pe_qp"), sem("dv_qp"), sem("dv_kvd")
        pe_o, dv_nrm, dv_rec, dv_ao, pe_aT, act_aT, pe_y, dv_y = (sem("pe_o"), sem("dv_nrm"), sem("dv_rec"), sem("dv_ao"),
                                                                  sem("pe_aT"), sem("act_aT"), sem("pe_y"), sem("dv_y"))
        LC = 16 * 10
        block = ctx.enter_context(clearing(nc, sems))

        def grouped(dram, first):
            return dram[first:first + GQ, :].rearrange("(s p) d -> p s d", p=P)

        def of(g):
            return slice(g * GT, g * GT + GT)

        @block.sync
        def _(sp):
            for g in range(NG):
                sp.dma_start(x2[:, of(g), :], grouped(x_in, g * GQ)).then_inc(ld_x[g], 16)
                sp.dma_start(y[:, of(g), :], grouped(xf, g * GQ + 1)).then_inc(ld_x[g], 16)
                if g == 0:
                    sp.dma_start(ident[:], consts["ident"]).then_inc(ld_c, 16)
                    for i, n in enumerate("qkv"):
                        sp.dma_start(wqkv[:, i, :], w["W" + n]).then_inc(ld_c, 16)
                        sp.dma_start(bqkv[:, i, :], w["b" + n].rearrange("(o d) -> o d", o=1).broadcast_to([P, D])).then_inc(ld_c, 16)
            sp.dma_start(own_head[:], consts["own_head"]).then_inc(ld_c, 16)
            sp.dma_start(wout[:], w["Wo"]).then_inc(ld_c, 16)
            sp.dma_start(bout[:], w["bo"].rearrange("(o d) -> o d", o=1).broadcast_to([P, D])).then_inc(ld_c, 16)
            for g in range(NG):
                sp.wait_ge(dv_y, g + 1)
                sp.dma_start(grouped(x_out, g * GQ), x2[:, of(g), :]).then_inc(st_o, 16)
                sp.wait_ge(dv_xn, NG + g + 1)
                sp.dma_start(grouped(xf, g * GQ + 1), xn[:, of(g), :]).then_inc(st_o, 16)
            sp.wait_ge(st_o, 32 * NG)

        @block.gpsimd
        def _(pool):
            pool.memset(proj_rows[:], 0.0).then_inc(zeroed, 1)
            pool.memset(minus_half[:], -0.5).then_inc(zeroed, 1)
            pool.memset(v_one[:, :, :, :, C:C + 1], 1.0).then_inc(zeroed, 1)
            pool.wait_ge(zeroed, 3)

            def inverse_std(k, g):
                pool.wait_ge(dv_mv, k + 1)
                pool.tensor_scalar(var[:, of(g)], mv[:, of(g), 1], 1e-5, None, ALU.add).then_inc(pl_var, 1)
                pool.wait_ge(pl_var, k + 1)
                pool.tensor_tensor(rstd[:, of(g)], var[:, of(g)], minus_half[:], ALU.pow).then_inc(pl_rstd, 1)

            for g in range(NG):
                inverse_std(g, g)
            pool.wait_ge(ld_c, LC)
            pool.wait_ge(dv_xn, NG)
            for g in range(NG):
                pool.tensor_tensor(x2[:, of(g), :], x2[:, of(g), :], bout[:].unsqueeze(1).broadcast_to([P, GT, D]),
                                   ALU.add).then_inc(pl_xb, 1)
            for g in range(NG):
                inverse_std(NG + g, g)

        @block.scalar
        def _(act):
            act.wait_ge(zeroed, 3)
            for h in range(HEADS):
                r = FEATS * (h % HQ)
                act.dma_start(proj_rows[r:r + FEATS, h // HQ, AD * h:AD * h + AD],
                              w["projection"][h:h + 1, :, :].rearrange("o f d -> (o f) d")).then_inc(ld_p, 16)
            act.wait_ge(pe_proj, 1)
            act.copy(proj[:], ps_t[:]).then_inc(act_proj, 1)
            for g in range(NG + 1):
                if g >= 1:
                    act.wait_ge(dv_ss, g)
                    act.activation(root[:], ss[:], ACT.Sqrt).then_inc(act_root, 1)
                if g < NG:
                    act.wait_ge(pe_xT, g + 1)
                    act.copy(xnT[:], ps_t[:].rearrange("p (s q) -> p s q", s=GT)).then_inc(act_xT, 1)
                if g >= 1:
                    act.wait_ge(pe_qkT, g)
                    for i in (1, 0):
                        last = act.copy(qkT[:, i, :], ps_qk[i][:])
                    last.then_inc(act_qkT, 1)
                if g < NG:
                    act.wait_ge(dv_qk, g + 1)
                    act.activation(sq[:], qk[:], ACT.Square).then_inc(act_sq, 1)
            for g in range(NG):
                act.wait_ge(pe_aT, g + 1)
                if g >= 2:
                    act.wait_ge(pe_y, g - 1)
                act.copy(aoT[:, g % 2, :, :], ps_t[:].rearrange("p (s q) -> p s q", s=GT)).then_inc(act_aT, 1)

        @block.vector
        def _(dve):
            def norm_stats(k, g):
                for s in range(g * GT, g * GT + GT):
                    last = dve.bn_stats(st6[:, s, :], x2[:, s, :])
                last.then_inc(dv_st, 1)
                dve.wait_ge(dv_st, k + 1)
                for s in range(g * GT, g * GT + GT):
                    last = dve.bn_aggr(mv[:, s, :], st6[:, s, :])
                last.then_inc(dv_mv, 1)

            def normalise(k, g):
                dve.wait_ge(pl_rstd, k + 1)
                for s in range(g * GT, g * GT + GT):
                    last = dve.tensor_scalar(xn[:, s, :], x2[:, s, :], mv[:, s, 0:1], rstd[:, s:s + 1], ALU.subtract, ALU.mult)
                last.then_inc(dv_xn, 1)

            by_head = lambda a: a.rearrange("p s k (h d) -> p (s k h) d", d=AD)

            def unit_length(g):
                dve.wait_ge(act_sq, g + 1)
                dve.tensor_reduce(ss[:], by_head(sq[:]), AX.X, ALU.add).then_inc(dv_ss, 1)
                dve.wait_ge(act_root, g + 1)
                dve.tensor_scalar(root2[:], root[:], 1e-18, None, ALU.max).then_inc(dv_newton, 1)
                dve.wait_ge(dv_newton, 4 * g + 1)
                dve.reciprocal(inv[:], root2[:]).then_inc(dv_newton, 1)
                dve.wait_ge(dv_newton, 4 * g + 2)
                dve.tensor_tensor(root2[:], ss[:], inv[:], ALU.mult).then_inc(dv_newton, 1)
                dve.wait_ge(dv_newton, 4 * g + 3)
                dve.tensor_tensor(norm[:], root[:], root2[:], ALU.add).then_inc(dv_newton, 1)
                dve.wait_ge(dv_newton, 4 * g + 4)
                dve.tensor_scalar(norm[:], norm[:], 0.5, 1e-8, ALU.mult, ALU.add).then_inc(dv_rn, 1)
                dve.wait_ge(dv_rn, 2 * g + 1)
                dve.reciprocal(rn[:], norm[:]).then_inc(dv_rn, 1)
                dve.wait_ge(dv_rn, 2 * g + 2)
                dve.tensor_tensor(by_head(qkn[:]), by_head(qk[:]), rn[:].unsqueeze(2).broadcast_to([P, GT * 2 * HEADS, AD]),
                                  ALU.mult).then_inc(dv_qkn, 1)

            def features(g):
                for s in range(GT):
                    dve.wait_ge(pe_kp, GT * g + s + 1)
                    dve.tensor_scalar(kp[:, s, :], banks[s][:], 0.0, FEAT_EPS, ALU.max, ALU.add).then_inc(dv_kp, 1)
                for i in range(HG):
                    dve.wait_ge(pe_qp, HG * g + i + 1)
                    dve.tensor_scalar(qp[:, i, g * GQ:g * GQ + GQ], banks[i][:], 0.0, FEAT_EPS, ALU.max, ALU.add).then_inc(dv_qp, 1)
                dve.wait_ge(pe_kv, g + 1)
                dve.wait_ge(dv_kv, g + 1)
                dve.tensor_tensor(kv[:], kv[:], ps_kv[:, 0:HG * (C + 1)].rearrange("p (g c) -> p g c", g=HG),
                                  ALU.add).then_inc(dv_kv, 1)

            dve.memset(kv[:], 0.0).then_inc(dv_kv, 1)
            for g in range(NG + 1):
                if g < NG:
                    dve.wait_ge(ld_x[g], 32)
                    dve.tensor_tensor(x2[:, of(g), :], x2[:, of(g), :], y[:, of(g), :], ALU.add).then_inc(dv_x2, 1)
                    dve.wait_ge(dv_x2, g + 1)
                    norm_stats(g, g)
                if g >= 1:
                    unit_length(g - 1)
                if g < NG:
                    normalise(g, g)
                    dve.wait_ge(ld_c, LC)
                    dve.wait_ge(pe_qkv, g + 1)
                    for s in range(GT):
                        last = dve.tensor_tensor(qk[:, s, :, :], banks[s][:, 0:2 * D].rearrange("p (k d) -> p k d", k=2),
                                                 bqkv[:, 0:2, :], ALU.add)
                    last.then_inc(dv_qk, 1)
                    dve.wait_ge(zeroed, 3)
                    for s in range(GT):
                        last = dve.tensor_tensor(v_one[:, g % 2, s, :, 0:C], banks[s][:, 2 * D:3 * D].rearrange("p (g d) -> p g d", g=HG),
                                                 bqkv[:, 2, :].rearrange("p (g d) -> p g d", g=HG), ALU.add)
                    last.then_inc(dv_v, 1)
                if g >= 1:
                    features(g - 1)
            dve.wait_ge(dv_kv, NG + 1)
            dve.tensor_tensor(kvd[:, :, 0:C], kv[:, :, 0:C], own_head[:, 0:C].unsqueeze(1).broadcast_to([P, HG, C]),
                              ALU.mult).then_inc(dv_kvd, 1)
            dve.tensor_tensor(kvd[:, :, C:C + HQ], kv[:, :, C:C + 1].broadcast_to([P, HG, HQ]),
                              own_head[:, C:C + HQ].unsqueeze(1).broadcast_to([P, HG, HQ]), ALU.mult).then_inc(dv_kvd, 1)

            by_group = lambda a: a.rearrange("p (g h) -> p g h", g=HG)

            def quotients(g):
                def sums(s):
                    at = (s % 2) * HG * (C + HQ)
                    return banks[2 * (g % 2) + s // 2][:, at:at + HG * (C + HQ)].rearrange("p (g c) -> p g c", g=HG)

                dve.wait_ge(pe_o, g + 1)
                for s in range(GT):
                    last = dve.tensor_scalar(by_group(nrm[:, s, :]), sums(s)[:, :, C:C + HQ], 1e-6, None, ALU.max)
                last.then_inc(dv_nrm, 1)
                dve.wait_ge(dv_nrm, g + 1)
                dve.reciprocal(rec[:], nrm[:]).then_inc(dv_rec, 1)
                dve.wait_ge(dv_rec, g + 1)
                if g >= 2:
                    dve.wait_ge(pe_aT, g - 1)
                for s in range(GT):
                    last = dve.tensor_tensor(ao[:, g % 2, s, :].rearrange("p (g h d) -> p g h d", g=HG, h=HQ),
                                             sums(s)[:, :, 0:C].rearrange("p g (h d) -> p g h d", h=HQ),
                                             by_group(rec[:, s, :]).unsqueeze(3).broadcast_to([P, HG, HQ, AD]), ALU.mult)
                last.then_inc(dv_ao, 1)

            quotients(0)
            for g in range(NG + 1):
                if g + 1 < NG:
                    quotients(g + 1)
                if g < NG:
                    dve.wait_ge(pe_y, g + 1)
                    dve.wait_ge(pl_xb, NG)
                    dve.tensor_tensor(x2[:, of(g), :], ps_y[g % 2][:].rearrange("p (s d) -> p s d", s=GT), x2[:, of(g), :],
                                      ALU.add).then_inc(dv_y, 1)
                    dve.wait_ge(dv_y, g + 1)
                    norm_stats(NG + g, g)
                if g >= 1:
                    normalise(NG + g - 1, g - 1)

        @block.tensor
        def _(pe):
            pe.wait_ge(ld_c, LC)
            pe.wait_ge(ld_p, 16 * HEADS)
            for i in range(HG):
                last = pe.transpose(ps_t[:, P * i:P * i + P], proj_rows[:, i, :], ident[:])
            last.then_inc(pe_proj, 1)
            pe.wait_ge(act_proj, 1)
            for g in range(NG + 1):
                if g < NG:
                    pe.wait_ge(dv_xn, g + 1)
                    for s in range(GT):
                        last = pe.transpose(ps_t[:, P * s:P * s + P], xn[:, g * GT + s, :], ident[:])
                    last.then_inc(pe_xT, 1)
                if g >= 1:
                    pe.wait_ge(dv_qkn, g)
                    for i in (1, 0):
                        for s in range(GT):
                            last = pe.transpose(ps_qk[i][:, P * s:P * s + P], qkn[:, s, i, :], ident[:])
                    last.then_inc(pe_qkT, 1)
                if g < NG:
                    pe.wait_ge(act_xT, g + 1)
                    if g >= 2:
                        pe.wait_ge(dv_qp, HG * (g - 1))
                    for s in range(GT):
                        last = pe.matmul(banks[s][:, 0:3 * D], xnT[:, s, :], wqkv[:].rearrange("p k d -> p (k d)"), start=True, stop=True)
                    last.then_inc(pe_qkv, 1)
                if g >= 1:
                    pe.wait_ge(act_qkT, g)
                    pe.wait_ge(dv_v, min(g + 1, NG))
                    for s in range(GT):
                        pe.matmul(banks[s][:], qkT[:, 1, P * s:P * s + P], proj[:], start=True, stop=True).then_inc(pe_kp, 1)
                    for i in range(HG):
                        pe.wait_ge(dv_kp, GT * (g - 1) + i + 1)
                        pe.matmul(banks[i][:], proj[:, P * i:P * i + P], qkT[:, 0, :], start=True, stop=True).then_inc(pe_qp, 1)
                    pe.wait_ge(dv_kv, g)
                    for i in range(HG):
                        for s in range(GT):
                            last = pe.matmul(ps_kv[:, (C + 1) * i:(C + 1) * (i + 1)], kp[:, s, P * i:P * i + P],
                                             v_one[:, (g - 1) % 2, s, i, :], start=(s == 0), stop=(s == GT - 1))
                    last.then_inc(pe_kv, 1)
            pe.wait_ge(dv_kvd, 2)

            def weighted(g):
                if g >= 2:
                    pe.wait_ge(dv_ao, g - 1)
                for s in range(GT):
                    for i in range(HG):
                        at = ((s % 2) * HG + i) * (C + HQ)
                        last = pe.matmul(banks[2 * (g % 2) + s // 2][:, at:at + C + HQ],
                                         qp[:, i, P * (g * GT + s):P * (g * GT + s) + P], kvd[:, i, :], start=True, stop=True)
                last.then_inc(pe_o, 1)

            weighted(0)
            for g in range(NG):
                if g + 1 < NG:
                    weighted(g + 1)
                pe.wait_ge(dv_ao, g + 1)
                if g:
                    pe.wait_ge(act_aT, g)
                for s in range(GT):
                    last = pe.transpose(ps_t[:, P * s:P * s + P], ao[:, g % 2, s, :], ident[:])
                last.then_inc(pe_aT, 1)
                pe.wait_ge(act_aT, g + 1)
                if g >= 2:
                    pe.wait_ge(dv_y, g - 1)
                for s in range(GT):
                    last = pe.matmul(ps_y[g % 2][:, P * s:P * s + P], aoT[:, g % 2, s, :], wout[:], start=True, stop=True)
                last.then_inc(pe_y, 1)


def add_stack(nc, tag, x_in, xf, out):
    with ExitStack() as ctx:
        xg = ctx.enter_context(nc.sbuf_tensor(f"{tag}_xg", [P, NT, D], F32))
        yg = ctx.enter_context(nc.sbuf_tensor(f"{tag}_yg", [P, NT, D], F32))
        ld = [ctx.enter_context(nc.semaphore(f"{tag}_ld{g}")) for g in range(NG)]
        added = ctx.enter_context(nc.semaphore(f"{tag}_added"))
        stored = ctx.enter_context(nc.semaphore(f"{tag}_stored"))
        block = ctx.enter_context(nc.Block())

        def grouped(dram, first):
            return dram[first:first + GT * P, :].rearrange("(s p) d -> p s d", p=P)

        @block.sync
        def _(sp):
            for g in range(NG):
                sp.dma_start(xg[:, g * GT:g * GT + GT, :], grouped(x_in, g * GT * P)).then_inc(ld[g], 16)
                sp.dma_start(yg[:, g * GT:g * GT + GT, :], grouped(xf, g * GT * P + 1)).then_inc(ld[g], 16)
            for g in range(NG):
                sp.wait_ge(added, g + 1)
                sp.dma_start(grouped(out, g * GT * P), xg[:, g * GT:g * GT + GT, :]).then_inc(stored, 16)
            sp.wait_ge(stored, 16 * NG)

        @block.vector
        def _(dve):
            for g in range(NG):
                s = slice(g * GT, g * GT + GT)
                dve.wait_ge(ld[g], 32)
                dve.tensor_tensor(xg[:, s, :], xg[:, s, :], yg[:, s, :], ALU.add).then_inc(added, 1)


def block_program(nc, x, a, b, f, consts, out):
    x1 = nc.dram_tensor("x1", [N, D], F32, kind="Internal").ap()
    x3 = nc.dram_tensor("x3", [N, D], F32, kind="Internal").ap()
    xf = nc.dram_tensor("xf", [N + 1, D], F32, kind="Internal").ap()
    xa = nc.dram_tensor("xa", [N + 1, D], F32, kind="Internal").ap()
    softmax_attention(nc, "a", x, a["w_qkv"], a["w_out"], a["b_out"], consts, x1, xf, xa)
    local_stack(nc, "f", f, consts, xf, xa)
    linear_attention(nc, "b", x1, b, consts, x3, xf)
    local_stack(nc, "g", f, consts, xf, xa)
    add_stack(nc, "r", x3, xf, out)


A_NAMES = ["w_qkv", "w_out", "b_out"]
B_NAMES = ["Wq", "bq", "Wk", "bk", "Wv", "bv", "Wo", "bo", "projection"]
F_NAMES = ["Wqkv", "q_scale", "k_scale", "Wo", "ln_g", "ln_b", "W1", "b1", "W2", "b2"]


def kernel(**inputs):
    import concourse.bacc as bacc
    from concourse.bass_utils import run_bass_kernel_spmd

    nc = bacc.Bacc("TRN2", target_bir_lowering=False, num_devices=1)
    arrays = {}

    def load(name, a):
        arrays[name] = np.ascontiguousarray(a)
        return nc.dram_tensor(name, arrays[name].shape, F32, kind="ExternalInput").ap()

    x = load("in_x_dram", np.asarray(inputs["L0_attn_a_x"]).reshape(N, D))
    a = {n: load(f"in_a_{n}_dram", inputs[f"L0_attn_a_{n}"]) for n in A_NAMES}
    b = {n: load(f"in_b_{n}_dram", inputs[f"L0_attn_b_{n}"]) for n in B_NAMES}
    f = {n: load(f"in_f_{n}_dram", inputs[f"L0_ffn_{n}"]) for n in F_NAMES}
    consts = {n: load(f"const_{n}_dram", t) for n, t in host_tables().items()}
    out = nc.dram_tensor("out_0_dram", (N, D), F32, kind="ExternalOutput").ap()
    block_program(nc, x, a, b, f, consts, out)
    r = run_bass_kernel_spmd(nc, [arrays], core_ids=[0])
    return r.results[0]["out_0_dram"].reshape(1, N, D)
```
